# Optimizing a Trainium2 kernel written in Bass

```python
import numpy as np
import jax
import jax.numpy as jnp

def _softmax(x, axis=-1):
    return jax.nn.softmax(x, axis=axis)

def _gelu(x):
    return jax.nn.gelu(x, approximate=True)

def _silu(x):
    return jax.nn.silu(x)

def _sigmoid(x):
    return jax.nn.sigmoid(x)

def _layernorm(x, axis=-1, eps=1e-05):
    m = jnp.mean(x, axis=axis, keepdims=True)
    v = jnp.var(x, axis=axis, keepdims=True)
    return (x - m) / jnp.sqrt(v + eps)

def _scatter_add(tgt, idx, src, axis=0):
    return tgt.at[idx].add(src)

def _segment_sum(src, seg, n):
    return jax.ops.segment_sum(src, seg, n)
kernel_name = 'mk_flamingo_gated_d2_seqx_r8_dd4cde'

def setup_inputs(seed: int=0):
    np.random.seed(seed)
    _w = jnp.asarray

    def _rec_inputs():
        import jax
        import jax.numpy as jnp
        _rk = jax.random.key(seed)
        x = -0.0002928 + 1 * jax.random.normal(jax.random.fold_in(_rk, 1), (4, 256, 128), jnp.float32)
        _lenS = 256 - jax.random.randint(jax.random.fold_in(_rk, 7), (4,), 0, max(1, 256 // 4) + 1, jnp.int32)
        _lenS2 = 512 - jax.random.randint(jax.random.fold_in(_rk, 8), (4,), 0, max(1, 512 // 4) + 1, jnp.int32)
        _ctx_512P = jax.random.normal(jax.random.fold_in(_rk, 11), (4, 16, 64), jnp.float32)
        _ctx_512c = jax.random.dirichlet(jax.random.fold_in(_rk, 511), 0.3 * jnp.ones((16,), jnp.float32), (4, 512))
        _ctx_512t = jnp.einsum('bsk,bkd->bsd', _ctx_512c, _ctx_512P)
        _ctx_512t = _ctx_512t * jax.lax.rsqrt(jnp.mean(jnp.square(_ctx_512t)) + 1e-12) * 0.953939
        ctx_512 = 0.00222621 + 0.99962 * (_ctx_512t + 0.3 * jax.random.normal(jax.random.fold_in(_rk, 611), (4, 512, 64), jnp.float32))
        _g = jax.random.normal(jax.random.fold_in(_rk, 9001), (2, 2), jnp.float32)
        _g = jnp.sign(_g) * jnp.maximum(jnp.abs(_g), 1.0) + (_g == 0) * 1.0
        g_xattn = _g[0]
        g_ffn = _g[1]
        return (x, ctx_512, g_xattn, g_ffn)
    x, ctx_512, g_xattn, g_ffn = _rec_inputs()

    def _L0_xattn_setup():
        import jax, jax.numpy as jnp
        import numpy as np
        B, T, TC, C, CC, H = (2, 256, 64, 128, 64, 16)
        D = C // H

        def _heads(t):
            b, l, _ = t.shape
            return t.reshape(b, l, H, D).transpose(0, 2, 1, 3)
        key = jax.random.key(seed)
        ks = jax.random.split(key, 18)
        w = lambda k, i, o: jax.random.normal(k, (i, o), jnp.float32) / np.sqrt(i).astype(np.float32)
        return {'x': jax.random.normal(ks[0], (B, T, C), jnp.float32), 'cross_input': jax.random.normal(ks[1], (B, TC, CC), jnp.float32), 'Wk': w(ks[2], C, C), 'bk': jnp.zeros((C,), jnp.float32), 'Wq': w(ks[3], C, C), 'bq': jnp.zeros((C,), jnp.float32), 'Wv': w(ks[4], C, C), 'bv': jnp.zeros((C,), jnp.float32), 'Wck': w(ks[5], CC, C), 'bck': jnp.zeros((C,), jnp.float32), 'Wcq': w(ks[6], C, C), 'bcq': jnp.zeros((C,), jnp.float32), 'Wcv': w(ks[7], CC, C), 'bcv': jnp.zeros((C,), jnp.float32), 'Wp': w(ks[8], C, C), 'bp': jnp.zeros((C,), jnp.float32)}
    _L0_xattn_all = _L0_xattn_setup()
    _L0_xattn_in = {k: v for k, v in _L0_xattn_all.items() if k in ('Wk', 'bk', 'Wq', 'bq', 'Wv', 'bv', 'Wck', 'bck', 'Wcq', 'bcq', 'Wcv', 'bcv', 'Wp', 'bp')}
    del _L0_xattn_all

    def _L0_ffn_setup():
        import jax, jax.numpy as jnp
        import numpy as np
        B, S, H, F, G = (8, 256, 128, 512, 128)
        EPS = 1e-05

        def _dequant(q, scales, g):
            K, N = q.shape
            w = (q.astype(jnp.float32) - 128.0).reshape(K // g, g, N) * scales[:, None, :]
            return w.reshape(K, N)
        key = jax.random.key(seed)
        ks = jax.random.split(key, 8)
        x = jax.random.normal(ks[0], (B, S, H), dtype=jnp.float32)
        ln_gamma = jnp.ones((H,), jnp.float32)
        ln_beta = jnp.zeros((H,), jnp.float32)
        fc1_q = jax.random.randint(ks[1], (H, F), 0, 32, dtype=jnp.int32)
        fc2_q = jax.random.randint(ks[2], (F, H), 0, 32, dtype=jnp.int32)
        fc1_scales = jax.random.uniform(ks[3], (H // G, F), jnp.float32) * 0.02 + 0.001
        fc2_scales = jax.random.uniform(ks[4], (F // G, H), jnp.float32) * 0.02 + 0.001
        fc1_bias = jax.random.normal(ks[5], (F,), jnp.float32) * 0.02
        fc2_bias = jax.random.normal(ks[6], (H,), jnp.float32) * 0.02
        return {'x': x, 'ln_gamma': ln_gamma, 'ln_beta': ln_beta, 'fc1_q': fc1_q, 'fc1_scales': fc1_scales, 'fc1_bias': fc1_bias, 'fc2_q': fc2_q, 'fc2_scales': fc2_scales, 'fc2_bias': fc2_bias}
    _L0_ffn_all = _L0_ffn_setup()
    _L0_ffn_in = {k: v for k, v in _L0_ffn_all.items() if k in ('ln_gamma', 'ln_beta', 'fc1_q', 'fc1_scales', 'fc1_bias', 'fc2_q', 'fc2_scales', 'fc2_bias')}
    del _L0_ffn_all

    def _L1_xattn_setup():
        import jax, jax.numpy as jnp
        import numpy as np
        NUM_HEADS = 16
        HEAD_DIM = 64
        Q_DIM = 128
        KV_DIM = 64
        INNER = NUM_HEADS * HEAD_DIM
        key = jax.random.key(seed)
        ks = jax.random.split(key, 7)
        B, N, M = (32, 128, 256)
        q = jax.random.normal(ks[0], (B, N, Q_DIM), dtype=jnp.float32)
        kv = jax.random.normal(ks[1], (B, M, KV_DIM), dtype=jnp.float32)
        Wq = jax.random.normal(ks[2], (Q_DIM, INNER), dtype=jnp.float32) / np.sqrt(Q_DIM)
        Wk = jax.random.normal(ks[3], (KV_DIM, INNER), dtype=jnp.float32) / np.sqrt(KV_DIM)
        Wv = jax.random.normal(ks[4], (KV_DIM, INNER), dtype=jnp.float32) / np.sqrt(KV_DIM)
        Wo = jax.random.normal(ks[5], (INNER, Q_DIM), dtype=jnp.float32) / np.sqrt(INNER)
        bo = jax.random.normal(ks[6], (Q_DIM,), dtype=jnp.float32) * 0.01
        return {'q': q, 'kv': kv, 'Wq': Wq, 'Wk': Wk, 'Wv': Wv, 'Wo': Wo, 'bo': bo}
    _L1_xattn_all = _L1_xattn_setup()
    _L1_xattn_in = {k: v for k, v in _L1_xattn_all.items() if k in ('Wq', 'Wk', 'Wv', 'Wo', 'bo')}
    del _L1_xattn_all

    def _L1_ffn_setup():
        import jax, jax.numpy as jnp
        import numpy as np
        import math
        D_MODEL = 128
        N_EXPERTS = 16
        D_FF = 512
        CAP_FACTOR = 1.25
        MIN_CAPACITY = 4

        def _capacity(num_tokens, num_experts):
            cap = math.floor(CAP_FACTOR * num_tokens / num_experts)
            cap += cap % 2
            return max(cap, MIN_CAPACITY)

        def _top1_router(gate_logits, capacity):
            s, e = gate_logits.shape
            probs = jax.nn.softmax(gate_logits, axis=-1)
            top1 = jnp.argmax(gate_logits, axis=-1)
            mask = jax.nn.one_hot(top1, e, dtype=jnp.int32)
            ranks = jnp.cumsum(mask, axis=0) - 1
            mask = mask * (ranks < capacity).astype(jnp.int32)
            rank1 = jnp.sum(mask * ranks, axis=-1)
            ranks_oh = jax.nn.one_hot(rank1, capacity, dtype=probs.dtype)
            weight = mask.astype(probs.dtype) * probs
            combine_weights = weight[:, :, None] * ranks_oh[:, None, :]
            sec_mask = combine_weights > 0
            return (combine_weights, sec_mask)
        key = jax.random.key(seed)
        k1, k2, k3, k4 = jax.random.split(key, 4)
        x = jax.random.normal(k1, (4, 256, D_MODEL), dtype=jnp.float32)
        gate_w = jax.random.normal(k2, (N_EXPERTS, D_MODEL), dtype=jnp.float32) * math.sqrt(0.1 / D_MODEL)
        w1 = jax.random.normal(k3, (N_EXPERTS, D_MODEL, D_FF), dtype=jnp.float32) * (1.0 / math.sqrt(D_MODEL))
        w2 = jax.random.normal(k4, (N_EXPERTS, D_FF, D_MODEL), dtype=jnp.float32) * (1.0 / math.sqrt(D_FF))
        return {'x': x, 'gate_w': gate_w, 'w1': w1, 'w2': w2}
    _L1_ffn_all = _L1_ffn_setup()
    _L1_ffn_in = {k: v for k, v in _L1_ffn_all.items() if k in ('gate_w', 'w1', 'w2')}
    del _L1_ffn_all
    return {'x': x, 'ctx_512': ctx_512, 'g_xattn': g_xattn, 'g_ffn': g_ffn, 'L0_xattn_Wk': _L0_xattn_in['Wk'], 'L0_xattn_bk': _L0_xattn_in['bk'], 'L0_xattn_Wq': _L0_xattn_in['Wq'], 'L0_xattn_bq': _L0_xattn_in['bq'], 'L0_xattn_Wv': _L0_xattn_in['Wv'], 'L0_xattn_bv': _L0_xattn_in['bv'], 'L0_xattn_Wck': _L0_xattn_in['Wck'], 'L0_xattn_bck': _L0_xattn_in['bck'], 'L0_xattn_Wcq': _L0_xattn_in['Wcq'], 'L0_xattn_bcq': _L0_xattn_in['bcq'], 'L0_xattn_Wcv': _L0_xattn_in['Wcv'], 'L0_xattn_bcv': _L0_xattn_in['bcv'], 'L0_xattn_Wp': _L0_xattn_in['Wp'], 'L0_xattn_bp': _L0_xattn_in['bp'], 'L0_ffn_ln_gamma': _L0_ffn_in['ln_gamma'], 'L0_ffn_ln_beta': _L0_ffn_in['ln_beta'], 'L0_ffn_fc1_q': _L0_ffn_in['fc1_q'], 'L0_ffn_fc1_scales': _L0_ffn_in['fc1_scales'], 'L0_ffn_fc1_bias': _L0_ffn_in['fc1_bias'], 'L0_ffn_fc2_q': _L0_ffn_in['fc2_q'], 'L0_ffn_fc2_scales': _L0_ffn_in['fc2_scales'], 'L0_ffn_fc2_bias': _L0_ffn_in['fc2_bias'], 'L1_xattn_Wq': _L1_xattn_in['Wq'], 'L1_xattn_Wk': _L1_xattn_in['Wk'], 'L1_xattn_Wv': _L1_xattn_in['Wv'], 'L1_xattn_Wo': _L1_xattn_in['Wo'], 'L1_xattn_bo': _L1_xattn_in['bo'], 'L1_ffn_gate_w': _L1_ffn_in['gate_w'], 'L1_ffn_w1': _L1_ffn_in['w1'], 'L1_ffn_w2': _L1_ffn_in['w2']}

def reference(x, ctx_512, g_xattn, g_ffn, L0_xattn_Wk, L0_xattn_bk, L0_xattn_Wq, L0_xattn_bq, L0_xattn_Wv, L0_xattn_bv, L0_xattn_Wck, L0_xattn_bck, L0_xattn_Wcq, L0_xattn_bcq, L0_xattn_Wcv, L0_xattn_bcv, L0_xattn_Wp, L0_xattn_bp, L0_ffn_ln_gamma, L0_ffn_ln_beta, L0_ffn_fc1_q, L0_ffn_fc1_scales, L0_ffn_fc1_bias, L0_ffn_fc2_q, L0_ffn_fc2_scales, L0_ffn_fc2_bias, L1_xattn_Wq, L1_xattn_Wk, L1_xattn_Wv, L1_xattn_Wo, L1_xattn_bo, L1_ffn_gate_w, L1_ffn_w1, L1_ffn_w2):
    import jax
    import jax.numpy as jnp

    def _L0_xattn_ref(x, cross_input, Wk, bk, Wq, bq, Wv, bv, Wck, bck, Wcq, bcq, Wcv, bcv, Wp, bp):
        import jax, jax.numpy as jnp
        import numpy as np
        B, T, TC, C, CC, H = (2, 256, 64, 128, 64, 16)
        D = C // H

        def _heads(t):
            b, l, _ = t.shape
            return t.reshape(b, l, H, D).transpose(0, 2, 1, 3)
        scale = np.float32(1.0 / np.sqrt(D))
        q = _heads(x @ Wq + bq)
        k = _heads(x @ Wk + bk)
        v = _heads(x @ Wv + bv)
        att = jnp.einsum('bhqd,bhkd->bhqk', q, k) * scale
        causal = jnp.tril(jnp.ones((T, T), bool))
        att = jnp.where(causal[None, None], att, -jnp.inf)
        y = jnp.einsum('bhqk,bhkd->bhqd', jax.nn.softmax(att, axis=-1), v)
        qc = _heads(x @ Wcq + bcq)
        kc = _heads(cross_input @ Wck + bck)
        vc = _heads(cross_input @ Wcv + bcv)
        attc = jnp.einsum('bhqd,bhkd->bhqk', qc, kc) * scale
        y = y + jnp.einsum('bhqk,bhkd->bhqd', jax.nn.softmax(attc, axis=-1), vc)
        y = y.transpose(0, 2, 1, 3).reshape(x.shape[0], T, C)
        return y @ Wp + bp

    def _L0_ffn_ref(x, ln_gamma, ln_beta, fc1_q, fc1_scales, fc1_bias, fc2_q, fc2_scales, fc2_bias):
        import jax, jax.numpy as jnp
        import numpy as np
        B, S, H, F, G = (8, 256, 128, 512, 128)
        EPS = 1e-05

        def _dequant(q, scales, g):
            K, N = q.shape
            w = (q.astype(jnp.float32) - 128.0).reshape(K // g, g, N) * scales[:, None, :]
            return w.reshape(K, N)
        residual = x
        mu = jnp.mean(x, axis=-1, keepdims=True)
        var = jnp.mean(jnp.square(x - mu), axis=-1, keepdims=True)
        h = (x - mu) * jax.lax.rsqrt(var + EPS) * ln_gamma + ln_beta
        hf = h.reshape(-1, H)
        w1 = _dequant(fc1_q, fc1_scales, G)
        y = hf @ w1 + fc1_bias
        y = jax.nn.silu(y)
        w2 = _dequant(fc2_q, fc2_scales, G)
        z = y @ w2 + fc2_bias
        return residual + 0.5 * z.reshape(residual.shape)

    def _L1_xattn_ref(q, kv, Wq, Wk, Wv, Wo, bo):
        import jax, jax.numpy as jnp
        import numpy as np
        NUM_HEADS = 16
        HEAD_DIM = 64
        Q_DIM = 128
        KV_DIM = 64
        INNER = NUM_HEADS * HEAD_DIM
        B, N, _ = q.shape
        M = kv.shape[1]
        scale = HEAD_DIM ** (-0.5)
        qh = (q @ Wq).reshape(B, N, NUM_HEADS, HEAD_DIM).transpose(0, 2, 1, 3)
        kh = (kv @ Wk).reshape(B, M, NUM_HEADS, HEAD_DIM).transpose(0, 2, 1, 3)
        vh = (kv @ Wv).reshape(B, M, NUM_HEADS, HEAD_DIM).transpose(0, 2, 1, 3)
        scores = jnp.einsum('bhnd,bhmd->bhnm', qh, kh) * scale
        attn = jax.nn.softmax(scores, axis=-1)
        out = jnp.einsum('bhnm,bhmd->bhnd', attn, vh)
        out = out.transpose(0, 2, 1, 3).reshape(B, N, INNER)
        return out @ Wo + bo

    def _L1_ffn_ref(x, gate_w, w1, w2):
        import jax, jax.numpy as jnp
        import numpy as np
        import math
        D_MODEL = 128
        N_EXPERTS = 16
        D_FF = 512
        CAP_FACTOR = 1.25
        MIN_CAPACITY = 4

        def _capacity(num_tokens, num_experts):
            cap = math.floor(CAP_FACTOR * num_tokens / num_experts)
            cap += cap % 2
            return max(cap, MIN_CAPACITY)

        def _top1_router(gate_logits, capacity):
            s, e = gate_logits.shape
            probs = jax.nn.softmax(gate_logits, axis=-1)
            top1 = jnp.argmax(gate_logits, axis=-1)
            mask = jax.nn.one_hot(top1, e, dtype=jnp.int32)
            ranks = jnp.cumsum(mask, axis=0) - 1
            mask = mask * (ranks < capacity).astype(jnp.int32)
            rank1 = jnp.sum(mask * ranks, axis=-1)
            ranks_oh = jax.nn.one_hot(rank1, capacity, dtype=probs.dtype)
            weight = mask.astype(probs.dtype) * probs
            combine_weights = weight[:, :, None] * ranks_oh[:, None, :]
            sec_mask = combine_weights > 0
            return (combine_weights, sec_mask)
        tokens = x.reshape(-1, D_MODEL)
        s = tokens.shape[0]
        capacity = _capacity(s, N_EXPERTS)
        gate_logits = tokens.astype(jnp.float32) @ gate_w.T
        combine_weights, sec_mask = _top1_router(gate_logits, capacity)
        dispatch = jnp.einsum('sec,sd->ecd', sec_mask.astype(tokens.dtype), tokens)
        h = jax.nn.gelu(jnp.einsum('ecd,edf->ecf', dispatch, w1))
        expert_out = jnp.einsum('ecf,efd->ecd', h, w2)
        out = jnp.einsum('sec,ecd->sd', combine_weights.astype(tokens.dtype), expert_out)
        return out.reshape(x.shape)
    x = x + jnp.tanh(g_xattn[0]) * _L0_xattn_ref(_layernorm(x, axis=-1), ctx_512, L0_xattn_Wk, L0_xattn_bk, L0_xattn_Wq, L0_xattn_bq, L0_xattn_Wv, L0_xattn_bv, L0_xattn_Wck, L0_xattn_bck, L0_xattn_Wcq, L0_xattn_bcq, L0_xattn_Wcv, L0_xattn_bcv, L0_xattn_Wp, L0_xattn_bp)
    x = x + jnp.tanh(g_ffn[0]) * _L0_ffn_ref(_layernorm(x, axis=-1), L0_ffn_ln_gamma, L0_ffn_ln_beta, L0_ffn_fc1_q, L0_ffn_fc1_scales, L0_ffn_fc1_bias, L0_ffn_fc2_q, L0_ffn_fc2_scales, L0_ffn_fc2_bias)
    x = x + jnp.tanh(g_xattn[1]) * _L1_xattn_ref(_layernorm(x, axis=-1), ctx_512, L1_xattn_Wq, L1_xattn_Wk, L1_xattn_Wv, L1_xattn_Wo, L1_xattn_bo)
    x = x + jnp.tanh(g_ffn[1]) * _L1_ffn_ref(_layernorm(x, axis=-1), L1_ffn_gate_w, L1_ffn_w1, L1_ffn_w2)
    return x

_drawn_inputs = setup_inputs


def setup_inputs(seed=0):
    import zlib

    import numpy as np

    out = dict(_drawn_inputs(seed))
    spreads = {'g_ffn': (-1.0, 0.6),
     'L0_xattn_bk': (0.0, 2.0),
     'L0_xattn_bq': (0.0, 0.602),
     'L0_xattn_bv': (0.0, 0.1),
     'L0_xattn_bck': (0.0, 2.0),
     'L0_xattn_bcq': (0.0, 0.51),
     'L0_xattn_bcv': (0.0, 0.751),
     'L0_xattn_bp': (0.0, 0.1),
     'L0_ffn_ln_gamma': (1.0, 0.2),
     'L0_ffn_ln_beta': (0.0, 0.1)}
    factors = {'L0_ffn_fc1_scales': 3.558,
     'L0_ffn_fc1_bias': 57.68,
     'L0_ffn_fc2_bias': 55.853,
     'L1_xattn_Wq': 8.0,
     'L1_xattn_Wk': 8.0,
     'L1_xattn_Wv': 8.0,
     'L1_xattn_Wo': 8.0,
     'L1_xattn_bo': 64.0,
     'L1_ffn_gate_w': 27.388,
     'L1_ffn_w1': 32.276,
     'L1_ffn_w2': 27.449}
    for name, (base, spread) in spreads.items():
        noise = np.random.default_rng([zlib.crc32(name.encode()), seed]).standard_normal(out[name].shape)
        drawn = base * np.exp(spread * noise) if base else spread * noise
        out[name] = jnp.asarray(drawn.astype(out[name].dtype))
    for name, factor in factors.items():
        out[name] = (out[name] * factor).astype(out[name].dtype)
    return out
```

```python
from contextlib import ExitStack

import concourse.bass as bass
from concourse import mybir

F32 = mybir.dt.float32
F32R = mybir.dt.float32r
BF16 = mybir.dt.bfloat16
I32 = mybir.dt.int32
U32 = mybir.dt.uint32
ALU = mybir.AluOpType
ACT = mybir.ActivationFunctionType
X = mybir.AxisListType.X

P = 128
B, T, C = 4, 256, 128
TC, CC = 512, 64
QT, KT = T // P, TC // P
H, D0, D1 = 16, 8, 64
G = 4
NG = H // G
FF = 512
FT = FF // P
E = 16
TILES = B * QT
CAP = int(1.25 * B * T / E)
CAP += CAP % 2
SLOTS = E * CAP
ST = SLOTS // P
EPS = 1e-5
NEG = -1e30
FAR = 1e6
SCALE0 = D0 ** -0.5
SCALE1 = D1 ** -0.5
ROWS = 96
ONE0 = ROWS
END0 = ONE0 + 2 * G
ONE1 = 64
DV = D0 + 1


class Chain:

    def __init__(self, eng, sem):
        self.eng, self.sem, self.n = eng, sem, 0

    def __call__(self, ins):
        self.n += 1
        ins.then_inc(self.sem, 1)
        self.eng.wait_ge(self.sem, self.n)


def build(nc, x, ctx, ctxT, g_xattn, g_ffn, w0, b0, bv0, bp0, gamma, beta, fc1_q, fc1_s, fc1_b,
          fc2_q, fc2_s, fc2_b, wqT, wkT, wvT, wo, bo, gate_wT, w1, w2, out):
    place = [(nc.sbuf_base + 31) // 32 * 32]

    def sb(name, shape, dt=F32, at=None):
        size = 2 if dt == BF16 else 4
        for n in shape[1:]:
            size *= n
        offset = place[0] if at is None else at
        if at is None:
            place[0] += (size + 31) // 32 * 32
        return nc.alloc_sbuf_tensor_at(name, shape, dt, offset=offset)

    with ExitStack() as stack:
        def sem(name):
            return stack.enter_context(nc.semaphore(name))

        w1_all = sb("w1_all", [P, E, FF])
        Aall = sb("Aall", [P, H, P])
        Ball = sb("Ball", [P, H // 2, P])
        w0_sb = sb("w0_sb", [P, 7, C])
        b0_sb = sb("b0_sb", [P, 4])
        bv_sb = sb("bv_sb", [P, 2])
        bvsum = sb("bvsum", [P, 1])
        bp_sb = sb("bp_sb", [P, C])
        gb_sb = sb("gb_sb", [P, 2])
        fc1 = sb("fc1", [P, FF])
        fc2 = sb("fc2", [P, FT, C])
        fc1b = sb("fc1b", [P, FT])
        fc1bh = sb("fc1bh", [P, FT])
        fc2bh = sb("fc2bh", [P, C])
        bo_sb = sb("bo_sb", [P, 1])
        gates = sb("gates", [P, 4])
        tg = sb("tg", [P, 4])
        gwT = sb("gwT", [P, E])
        ident = sb("ident", [P, P])
        identb = sb("identb", [P, P], BF16)
        causal = sb("causal", [P, P], BF16)
        tri = sb("tri", [P, P], BF16)
        onesb = sb("onesb", [P, P], BF16)
        ones32 = sb("ones32", [P, 32])
        ones8 = sb("ones8", [2 * G, TC])
        nd = sb("nd", [P, 2 * G])
        mhalf = sb("mhalf", [P, TILES])
        iota_i = sb("iota_i", [P, E], I32)
        iota_e = sb("iota_e", [P, E])
        x_all = sb("x_all", [P, TILES, C])

        KC_at = place[0]
        KC = sb("KC", [P, H, TC], F32R)
        KS_at = place[0]
        KS = sb("KS", [P, H, T], F32R)
        QS_at = place[0]
        assert QS_at - KC_at == 4 * H * (TC + T)
        QS = sb("QS", [P, H, T], F32R)
        QC = sb("QC", [P, H, T], F32R)
        QH = KC[:, :, 0:T]
        QL = KS
        w2_all = sb("w2_all", [P, E, FT, C], at=QS_at)

        Pc_at = place[0]
        Pc = sb("Pc", [P, 2 * G, KT * T])
        Ps_at = place[0]
        Ps = sb("Ps", [P, G, 3 * P])
        raw = sb("raw", [P, 3 * T + TC], at=Pc_at)
        hi = sb("hi", [P, 3 * T + TC], F32R, at=Pc_at + 4 * (3 * T + TC))
        lo = sb("lo", [P, 3 * T + TC], F32R, at=Pc_at + 8 * (3 * T + TC))
        wqT_sb = sb("wqT_sb", [D1, H, C], at=Pc_at)
        wkT_sb = sb("wkT_sb", [D1, H, CC], at=Pc_at + 4 * H * C)
        wvT_sb = sb("wvT_sb", [D1, H, CC], at=Pc_at + 4 * H * (C + CC))
        wo_sb = sb("wo_sb", [D1, H, C], at=Pc_at + 4 * H * (C + 2 * CC))
        U = sb("U", [P, H // 2, T], at=Ps_at)
        place[0] = max(place[0], Ps_at + 4 * H // 2 * T)
        sT = sb("sT", [P, FT, T], at=Ps_at)
        th = sb("th", [P, FT, T], at=Pc_at)
        fcq = sb("fcq", [P, 2, FF], I32, at=KC_at)
        fcs = sb("fcs", [P, 2, FF], at=KC_at + 8 * FF)

        ctx_sb = sb("ctx_sb", [P, KT, CC])
        cT = sb("cT", [P, TC])
        K1 = sb("K1", [P, TC], F32R)
        K2 = sb("K2", [ROWS, TC], F32R)
        Vs = sb("Vs", [P, QT, H, DV])
        Vc = sb("Vc", [P, KT, H, DV])
        xn = sb("xn", [P, QT, C])
        xnT = sb("xnT", [P, T])
        y = sb("y", [P, QT, C])
        x1 = sb("x1", [P, QT, C])
        xn1 = sb("xn1", [P, QT, C])
        rmax = sb("rmax", [P, 2, QT, 2 * G])
        OT_at = place[0]
        OT = sb("OT", [P, 2 * T])
        rc0 = sb("rc0", [P, 2 * QT, G])
        yn = sb("yn", [P, 2 * QT, G, D0])
        yT = sb("yT", [P, T])
        tmp = sb("tmp", [P, QT, C])
        rsum = sb("rsum", [P, T])
        R = sb("R", [P, 2, 2, T], at=OT_at)
        assert place[0] >= OT_at + 16 * T
        oT = sb("oT", [P, T])
        stats = sb("stats", [P, TILES, 6])
        mv = sb("mv", [P, TILES, 2])
        ve = sb("ve", [P, TILES])
        rstd = sb("rstd", [P, TILES])

        at = [KC_at]

        def late(name, shape, dt=F32):
            t = sb(name, shape, dt, at=at[0])
            n = 4 if dt != BF16 else 2
            for k in shape[1:]:
                n *= k
            at[0] += (n + 31) // 32 * 32
            assert at[0] <= QS_at, at[0] - QS_at
            return t
        xm = late("xm", [P, TILES, C])
        xmT = late("xmT", [P, TILES * P])
        XD = late("XD", [P, ST, C])
        XT = late("XT", [P, SLOTS])
        hT = late("hT", [P, 2, FT, CAP])
        YB = late("YB", [CAP, E, C])
        Yg = late("Yg", [P, TILES, C])
        lmax = late("lmax", [P, TILES])
        eq = late("eq", [P, TILES, E])
        arg = late("arg", [P, TILES])
        pick = late("pick", [P, TILES, E])
        oh = late("oh", [P, TILES, E], BF16)
        ex = late("ex", [P, TILES, E])
        exs = late("exs", [P, TILES])
        wgt = late("wgt", [P, TILES])
        rk = late("rk", [P, TILES])
        drop = late("drop", [P, TILES])
        slot = late("slot", [P, TILES])
        slot_i = late("slot_i", [P, TILES], U32)
        assert place[0] <= nc.sbuf_usable_end, (place[0], nc.sbuf_usable_end)

        zrow = y
        PS = stack.enter_context(nc.psum_tensor("PS", [P, 8, 512], F32))
        MX, STB, AV, MISC = 0, 2, 6, 7
        x_slots = nc.dram_tensor("x_slots", (SLOTS, C), F32)
        parts_dram = nc.dram_tensor("parts_dram", (2, P, 3 * T + TC), F32)
        r_dram = nc.dram_tensor("r_dram", (2, G, T), F32)
        y_slots = nc.dram_tensor("y_slots", (SLOTS, C), F32)

        s_load = sem("s_load")
        s_loadw = sem("s_loadw")
        s_w1 = sem("s_w1")
        s_pool0 = sem("s_pool0")
        s_dve0 = sem("s_dve0")
        s_zero = sem("s_zero")
        s_zslots = sem("s_zslots")
        s_ab = sem("s_ab")
        s_abc = sem("s_abc")
        s_tanh = sem("s_tanh")
        s_setup = sem("s_setup")
        s_const = sem("s_const")
        arrived = sem("arrived")
        released = {k: sem(f"released_{k}") for k in ("pe", "act", "dve", "sp")}
        names = ("ctx_in ones_in ctx_ps kv_sb var rstd_ok xn_ok xT_ps xT_sb proj_ps split_hi split_lo parts_out rinv_out "
                 "v_sb q_in k_in c_in mx_ps mx_ok mt_ps mt_sb st_ps exp_ok self_ok av_ps av_sb "
                 "ot_ps ot_sb yn_ok y_ok o_ps o_sb f_ps tanh_ok t1_ok s_ok z_ps z_sb kk_hi kk_lo "
                 "q1_ps qh_ok ql_ok sum_sb rinv_in0 rinv_in1 un_ok o1_ps o1_sb o1T_ps x_ok dchain achain masked").split()
        S = {n: sem(n) for n in names}
        t_names = ("t_var t_rstd t_xm t_xT t_xTsb t_lg t_d t_lm t_ex t_oh t_rk t_slot t_sc t_xd t_dT t_dTsb t_h t_g "
                   "t_y t_ysb t_yw t_w2 t_out t_yzero t_chain").split()
        TS = {n: sem(n) for n in t_names}
        s_back = [sem(f"s_back{t}") for t in range(TILES)]

        block = stack.enter_context(nc.Block())

        def end_of_batch(eng, key):
            eng.drain().then_inc(arrived, 1)
            eng.wait_ge(released[key], 1)
            eng.sem_clear(released[key])

        def r_rows(sp, g):
            sp.wait_ge(S["sum_sb"], g + 1)
            if g >= 2:
                sp.wait_ge(S[f"rinv_in{g % 2}"], 32 * (g // 2))
            sp.dma_start(r_dram[g % 2], rsum[0:P:32, :]).then_inc(S["rinv_out"], 16)
            sp.wait_ge(S["rinv_out"], 16 * (g + 1))
            if g >= 2:
                sp.wait_ge(S["un_ok"], g - 1)
            for i in range(2):
                sp.dma_start(R[D1 * i:D1 * i + D1, g % 2, :, :], r_dram[g % 2, i:G:2, :].partition_broadcast(D1)
                             ).then_inc(S[f"rinv_in{g % 2}"], 16)

        def rows_ok(n):
            return 2 * G * min(n, NG) + G * max(n - NG, 0)

        @block.sync
        def _(sp):
            for b in range(B):
                sp.dma_start(x_all[:, QT * b:QT * b + QT, :],
                             x[b].rearrange("(t p) c -> p t c", p=P)).then_inc(s_load, 16)
            for j in range(7):
                rows = CC if j in (4, 5) else C
                sp.dma_start(w0_sb[0:rows, j, :], w0[j]).then_inc(s_load, 16)
            for j in range(4):
                sp.dma_start(b0_sb[:, j:j + 1], b0[j].rearrange("(c o) -> c o", o=1)).then_inc(s_load, 16)
            for j in range(2):
                sp.dma_start(bv_sb[:, j:j + 1], bv0[j].rearrange("(c o) -> c o", o=1)).then_inc(s_load, 16)
            sp.dma_start(bp_sb[:, :], bp0.partition_broadcast(P)).then_inc(s_load, 16)
            sp.dma_start(gb_sb[:, 0:1], gamma.rearrange("(c o) -> c o", o=1)).then_inc(s_load, 16)
            sp.dma_start(gb_sb[:, 1:2], beta.rearrange("(c o) -> c o", o=1)).then_inc(s_load, 16)
            sp.dma_start(fc1b[:, :], fc1_b).then_inc(s_load, 16)
            sp.dma_start(fc2bh[:, :], fc2_b.partition_broadcast(P)).then_inc(s_load, 16)
            sp.dma_start(bo_sb[:, :], bo.rearrange("(c o) -> c o", o=1)).then_inc(s_load, 16)
            sp.dma_start(gates[:, 0:2], g_xattn.partition_broadcast(P)).then_inc(s_load, 16)
            sp.dma_start(gates[:, 2:4], g_ffn.partition_broadcast(P)).then_inc(s_load, 16)
            sp.dma_start(gwT[:, :], gate_wT).then_inc(s_load, 16)
            sp.dma_start(fcq[:, 0, :], fc1_q).then_inc(s_load, 16)
            sp.dma_start(fcq[:, 1, :].rearrange("p (f c) -> p f c", f=FT),
                         fc2_q.rearrange("(f p) c -> p f c", p=P)).then_inc(s_load, 16)
            sp.dma_start(fcs[:, 0, :], fc1_s.rearrange("o f -> (o f)").partition_broadcast(P)).then_inc(s_load, 16)
            sp.dma_start(fcs[:, 1, :], fc2_s.rearrange("f c -> (f c)").partition_broadcast(P)).then_inc(s_load, 16)
            sp.dma_start(wqT_sb[:, :, :], wqT).then_inc(s_loadw, 16)
            sp.dma_start(wkT_sb[:, :, :], wkT).then_inc(s_loadw, 16)
            sp.dma_start(wvT_sb[:, :, :], wvT).then_inc(s_loadw, 16)
            sp.dma_start(wo_sb[:, :, :], wo).then_inc(s_loadw, 16)
            for e in range(E):
                sp.dma_start(w1_all[:, e, :], w1[e]).then_inc(s_w1, 16)
            sp.wait_ge(s_zero, 1)
            for j in range(ST):
                sp.dma_start(x_slots[j * P:(j + 1) * P, :], zrow[:, 0, :]).then_inc(s_zslots, 16)
            sp.wait_ge(s_zslots, 16 * ST)
            sp.wait_ge(s_const, 1)
            sp.wait_ge(s_abc, 1)
            sp.wait_ge(s_zero, 2)
            with sp.Fori(0, B) as b:
                sp.dma_start(cT[0:CC, :], ctxT[bass.ds(b, 1)].rearrange("o c k -> (o c) k")).then_inc(S["ctx_in"], 16)
                sp.dma_start(cT[CC:P, :], ctxT[bass.ds(b, 1)].rearrange("o c k -> (o c) k")).then_inc(S["ctx_in"], 16)
                sp.dma_start(ctx_sb[:, :, :],
                             ctx[bass.ds(b, 1)].rearrange("o (t p) c -> p (o t) c", p=P)).then_inc(S["ctx_in"], 16)
                sp.dma_start(KC[ONE0:END0, :, 0:T].bitcast(F32), ones8[:, 0:T].unsqueeze(1).broadcast_to([2 * G, H, T])
                             ).then_inc(S["ones_in"], 16)
                for n, (dst, off, w, parts, s) in enumerate((
                        (KC, 3 * T, TC, (0, 1, 0), "c_in"), (QS, 0, T, (0, 0, 1), "q_in"),
                        (KS, T, T, (0, 1, 0), "k_in"), (QC, 2 * T, T, (0, 0, 1), "c_in"))):
                    sp.wait_ge(S["split_hi"], n + 1)
                    sp.dma_start(parts_dram[0, :, off:off + w], hi[:, off:off + w].bitcast(F32)).then_inc(S["parts_out"], 16)
                    sp.wait_ge(S["split_lo"], n + 1)
                    sp.dma_start(parts_dram[1, :, off:off + w], lo[:, off:off + w].bitcast(F32)).then_inc(S["parts_out"], 16)
                    sp.wait_ge(S["parts_out"], 32 * (n + 1))
                    for j, part in enumerate(parts):
                        sp.dma_start(dst[D0 * j:D0 * j + D0, :, :].bitcast(F32),
                                     parts_dram[part, :, off:off + w].rearrange("(h d) k -> d h k", d=D0)
                                     ).then_inc(S[s], 16)
                for g in range(NG - 1):
                    r_rows(sp, g)
                r_rows(sp, NG - 1)
                end_of_batch(sp, "sp")
            for e in range(E):
                sp.dma_start(w2_all[:, e, :, :], w2[e].rearrange("(f p) c -> p f c", p=P)).then_inc(TS["t_w2"], 16)
            sp.wait_ge(TS["t_sc"], 16 * TILES)
            sp.dma_start(XD[:, :, :], x_slots[:, :].rearrange("(t p) c -> p t c", p=P)).then_inc(TS["t_xd"], 16)
            for q in range(E // 4):
                sp.wait_ge(TS["t_ysb"], q + 1)
                sp.dma_start(y_slots[q * 4 * CAP:(q + 1) * 4 * CAP, :].rearrange("(e s) c -> s e c", s=CAP),
                             YB[:, 4 * q:4 * q + 4, :]).then_inc(TS["t_yw"], 16)
            for t in range(TILES):
                sp.wait_ge(TS["t_out"], t + 1)
                sp.dma_start(out[t // QT, (t % QT) * P:(t % QT + 1) * P, :], xm[:, t, :]).then_inc(TS["t_d"], 16)
            sp.wait_ge(TS["t_d"], 16 * TILES)

        @block.gpsimd
        def _(pool):
            link = Chain(pool, s_pool0)

            def diagonal(t, op, fill, base=0, step=-1, mult=1):
                return pool.affine_select(out=t[:, :], in_=t[:, :], compare_op=op, fill=fill, base=base,
                                          pattern=[[step, P]], channel_multiplier=mult)
            pool.memset(ident[:, :], 0.0)
            pool.memset(identb[:, :], 0.0)
            pool.memset(causal[:, :], 0.0)
            pool.memset(nd[:, :], 0.0)
            link(pool.memset(tri[:, :], 1.0))
            diagonal(ident, ALU.not_equal, 1.0)
            diagonal(identb, ALU.not_equal, 1.0)
            diagonal(causal, ALU.is_ge, NEG)
            diagonal(tri, ALU.is_ge, 0.0, step=1, mult=-1)
            pool.memset(ones8[:, :], 1.0)
            pool.affine_select(out=nd[:, :], in_=nd[:, :], compare_op=ALU.not_equal, fill=-1.0, base=0,
                               pattern=[[-1, 2 * G]], channel_multiplier=1)
            pool.memset(mhalf[:, :], -0.5)
            link(pool.iota(iota_i[:, :], pattern=[[1, E]], base=-E, channel_multiplier=0))
            pool.tensor_copy(iota_e[:, :], iota_i[:, :]).then_inc(s_const, 1)
            with pool.Fori(0, B) as b:
                def rsqrt(n):
                    pool.wait_ge(S["var"], n)
                    pool.tensor_tensor(rstd[:, 0:QT], ve[:, 0:QT], mhalf[:, 0:QT], ALU.pow).then_inc(S["rstd_ok"], 1)
                rsqrt(1)
                for g in range(NG):
                    pool.wait_ge(S["self_ok"], 2 * g + 2)
                    for a in (0, 2):
                        v = Ps[:, :, a * P:(a + 1) * P]
                        pool.affine_select(out=v, in_=v, compare_op=ALU.is_ge, fill=0.0, base=0,
                                           pattern=[[0, G], [1, P]], channel_multiplier=-1).then_inc(S["masked"], 1)
                rsqrt(2)
                rsqrt(3)
                pool.wait_ge(S["tanh_ok"], FT)
                pool.tensor_scalar(th[:, :, :], th[:, :, :], 1.0, None, ALU.add).then_inc(S["t1_ok"], 1)
                rsqrt(4)
                for g in range(NG):
                    pool.wait_ge(S[f"rinv_in{g % 2}"], 32 * (g // 2 + 1))
                    pool.wait_ge(S["av_sb"], NG + g + 1)
                    u = U[:, 2 * g:2 * g + 2, :]
                    pool.tensor_tensor(u, u, R[:, g % 2, :, :], ALU.mult).then_inc(S["un_ok"], 1)
                pool.drain()
                pool.wait_ge(arrived, 4)
                pool.sem_clear(arrived)
                for s in S.values():
                    pool.sem_clear(s)
                for s in released.values():
                    pool.sem_inc(s, 1)
            pool.wait_ge(TS["t_var"], 1)
            pool.tensor_tensor(rstd[:, :], ve[:, :], mhalf[:, :], ALU.pow).then_inc(TS["t_rstd"], 1)
            pool.memset(Yg[:, :, :], 0.0).then_inc(TS["t_yzero"], 1)
            pool.wait_ge(TS["t_slot"], 1)
            for t in range(TILES):
                pool.indirect_dma_start(x_slots[:, :], bass.IndirectOffsetOnAxis(slot_i[:, t:t + 1], 0),
                                        xm[:, t, :], None, bounds_check=SLOTS - 1, oob_is_err=False
                                        ).then_inc(TS["t_sc"], 16)
            pool.wait_ge(TS["t_yzero"], 1)
            pool.wait_ge(TS["t_yw"], 16 * (E // 4))
            for t in range(TILES):
                pool.indirect_dma_start(Yg[:, t, :], None, y_slots[:, :],
                                        bass.IndirectOffsetOnAxis(slot_i[:, t:t + 1], 0),
                                        bounds_check=SLOTS - 1, oob_is_err=False).then_inc(s_back[t], 16)

        @block.scalar
        def _(act):
            act.wait_ge(s_load, 16 * 30)
            act.activation(tg[:, :], gates[:, :], ACT.Tanh).then_inc(s_tanh, 1)
            for n in range(NG + 2):
                act.wait_ge(s_ab, n + 1)
                dst = Aall[:, G * n:G * n + G, :] if n < NG else Ball[:, G * (n - NG):G * (n - NG) + G, :]
                act.activation(dst.rearrange("p a b -> p (a b)"), PS[:, n, :], ACT.Copy).then_inc(s_dve0, 1)
            act.wait_ge(s_dve0, NG + 2)
            act.wait_ge(s_const, 1)
            act.drain().then_inc(s_abc, 1)
            act.wait_ge(s_zero, 2)
            with act.Fori(0, B) as b:
                def neg_max0(g, heads):
                    act.wait_ge(S["mt_ps"], g + 1)
                    for c in heads:
                        for q, j in ((QS, c), (QC, G + c)):
                            act.activation(q[ONE0:END0, G * g + c, :], PS[0:2 * G, MISC, 0:T], ACT.Copy,
                                           scale=nd[0:2 * G, j:j + 1]).then_inc(S["mt_sb"], 1)

                def neg_max1(g):
                    act.wait_ge(S["mt_ps"], NG + g + 1)
                    for c in range(G):
                        act.activation(QL[ONE1:ONE1 + G, G * g + c, :], PS[0:G, MISC, 0:T], ACT.Copy,
                                       scale=nd[0:G, c:c + 1]).then_inc(S["mt_sb"], 1)

                act.wait_ge(S["ctx_in"], 48)
                act.activation(K1[:, :], cT[:, :], ACT.Copy).then_inc(S["kk_hi"], 1)
                act.activation(K2[0:CC, :], cT[0:CC, :], ACT.Copy).then_inc(S["kk_hi"], 1)
                for n, (bank, off, w, bias) in enumerate(((5, 3 * T, TC, 3), (0, 0, T, 0), (1, T, T, 1), (2, 2 * T, T, 2))):
                    act.wait_ge(S["ctx_ps"] if n == 0 else S["proj_ps"], 1 if n == 0 else n)
                    act.activation(raw[:, off:off + w], PS[:, bank, 0:w], ACT.Identity, bias=b0_sb[:, bias:bias + 1]
                                   ).then_inc(S["achain"], 1)
                    act.activation(hi[:, off:off + w], PS[:, bank, 0:w], ACT.Identity, bias=b0_sb[:, bias:bias + 1]
                                   ).then_inc(S["split_hi"], 1)
                neg_max0(0, range(G))
                for g in range(NG):
                    for u in range(6):
                        n = 6 * g + u
                        act.wait_ge(S["st_ps"], n + 1)
                        bank = STB + 2 * (n % 2)
                        if u in (0, 3):
                            if g >= 1:
                                act.wait_ge(S["av_ps"], g)
                            j = 2 * (u // 3)
                            act.activation(Ps[:, j:j + 2, :], PS[:, bank:bank + 2, 0:3 * P], ACT.Exp, scale=SCALE0
                                           ).then_inc(S["self_ok"], 1)
                        else:
                            c = u - 1 if u < 3 else u - 2
                            if g >= 2:
                                act.wait_ge(S["av_ps"], g - 1)
                            elif g == 0:
                                act.wait_ge(S["c_in"], 96)
                                act.wait_ge(S["q_in"], 48)
                                act.wait_ge(S["k_in"], 48)
                            act.activation(Pc[:, G * (g % 2) + c, :], PS[:, bank:bank + 2, :].rearrange("p a b -> p (a b)"),
                                           ACT.Exp, scale=SCALE0).then_inc(S["exp_ok"], 1)
                    if g + 1 < NG:
                        neg_max0(g + 1, range(G))
                for f in range(FT):
                    act.wait_ge(S["f_ps"], f // 2 + 1)
                    act.activation(th[:, f, :], PS[:, STB + f // 2, (f % 2) * T:(f % 2 + 1) * T], ACT.Tanh,
                                   scale=0.5, bias=fc1bh[:, f:f + 1]).then_inc(S["tanh_ok"], 1)
                for n in range(H // 2):
                    act.wait_ge(S["q1_ps"], n + 1)
                    act.activation(QH[:, 2 * n:2 * n + 2, :], PS[:, STB + n % 4, :].rearrange("p (a b) -> p a b", a=2),
                                   ACT.Copy).then_inc(S["qh_ok"], 1)
                neg_max1(0)
                for g in range(NG):
                    for c in range(G):
                        n = G * g + c
                        act.wait_ge(S["st_ps"], 6 * NG + n + 1)
                        bank = STB + 2 * (n % 2)
                        if g >= 2:
                            act.wait_ge(S["av_ps"], NG + g - 1)
                        act.activation(Pc[:, G * (g % 2) + c, :], PS[:, bank:bank + 2, :].rearrange("p a b -> p (a b)"),
                                       ACT.Exp, scale=SCALE1).then_inc(S["exp_ok"], 1)
                    if g + 1 < NG:
                        neg_max1(g + 1)
                end_of_batch(act, "act")
            act.wait_ge(TS["t_lm"], 1)
            act.activation(ex[:, :, :], eq[:, :, :], ACT.Exp).then_inc(TS["t_ex"], 1)
            for j in range(2):
                act.wait_ge(TS["t_dT"], j + 1)
            for e in range(E):
                act.wait_ge(TS["t_h"], e + 1)
                if e >= 2:
                    act.wait_ge(TS["t_y"], e - 1)
                act.activation(hT[:, e % 2, :, :].rearrange("p f s -> p (f s)"), PS[:, e % 2, 0:FT * CAP],
                               ACT.Gelu_apprx_tanh).then_inc(TS["t_g"], 1)

        @block.tensor
        def _(pe):
            def mm(o, l, r, start=True, stop=True):
                return pe.matmul(o, l, r, start=start, stop=stop)

            pe.wait_ge(s_loadw, 64)
            for n in range(NG):
                for c in range(G):
                    h = G * n + c
                    last = mm(PS[:, n, c * P:(c + 1) * P].rearrange("p (a b) -> p a b", a=2), wqT_sb[:, h, :],
                              wkT_sb[:, h, :].unsqueeze(1).broadcast_to([D1, 2, CC]))
                last.then_inc(s_ab, 1)
            for n in range(2):
                for c in range(2 * G):
                    h = 2 * G * n + c
                    last = mm(PS[D1 * (h % 2):D1 * (h % 2) + D1, NG + n, (c // 2) * P:(c // 2 + 1) * P],
                              wvT_sb[:, h, :], wo_sb[:, h, :])
                last.then_inc(s_ab, 1)
            pe.wait_ge(s_zero, 2)
            pe.wait_ge(s_abc, 1)
            with pe.Fori(0, B) as b:
                def turn(src, n, out_bank=MISC):
                    for t in range(QT):
                        last = pe.transpose(PS[:, out_bank, t * P:(t + 1) * P], src[:, t, :], ident[:, :])
                    last.then_inc(S["xT_ps"], 1)

                pe.wait_ge(S["ctx_in"], 48)
                mm(PS[:, 5, :], w0_sb[:, 4, :], cT[:, :]).then_inc(S["ctx_ps"], 1)
                for k in range(KT):
                    last = mm(PS[:, 4, k * P:(k + 1) * P], cT[:, k * P:(k + 1) * P], w0_sb[:, 5, :])
                last.then_inc(S["ctx_ps"], 1)
                pe.wait_ge(S["xn_ok"], 1)
                turn(xn, 1)
                pe.wait_ge(S["xT_sb"], 1)
                for j in range(3):
                    mm(PS[:, j, 0:T], w0_sb[:, j, :], xnT[:, :]).then_inc(S["proj_ps"], 1)
                for t in range(QT):
                    last = mm(PS[:, 3, t * P:(t + 1) * P], xnT[:, t * P:(t + 1) * P], w0_sb[:, 3, :])
                last.then_inc(S["proj_ps"], 1)

                def mx_slot(n, base):
                    if n >= 2:
                        pe.wait_ge(S["mx_ok"], base + n - 1)
                    return MX + n % 2

                def max_self(g, c):
                    n, h = 3 * G * g + 3 * c, G * g + c
                    bank = mx_slot(n, 0)
                    for t in range(QT):
                        o = PS[:, bank, t * T:(t + 1) * T]
                        mm(o, QS[0:ROWS, h, t * P:(t + 1) * P], KS[0:ROWS, h, :], stop=False)
                        last = mm(o[:, t * P:(t + 1) * P], identb[:, :], causal[:, :], start=False)
                    last.then_inc(S["mx_ps"], 1)

                def max_cross(g, c, t):
                    n, h = 3 * G * g + 3 * c + 1 + t, G * g + c
                    bank = mx_slot(n, 0)
                    mm(PS[:, bank, :], QC[0:ROWS, h, t * P:(t + 1) * P], KC[0:ROWS, h, :]).then_inc(S["mx_ps"], 1)

                def st_slot(n):
                    if n >= 2:
                        done = n - 1
                        if done <= 6 * NG:
                            full, part = divmod(done, 6)
                            pe.wait_ge(S["self_ok"], 2 * full + (0, 1, 1, 1, 2, 2)[part]) if full or part else None
                            if 4 * full + (0, 0, 1, 2, 2, 3)[part]:
                                pe.wait_ge(S["exp_ok"], 4 * full + (0, 0, 1, 2, 2, 3)[part])
                        else:
                            pe.wait_ge(S["exp_ok"], H + done - 6 * NG)
                    return STB + 2 * (n % 2)

                def st_self(g, j):
                    n = 6 * g + 3 * j
                    pe.wait_ge(S["mt_sb"], 2 * (G * g + 2 * j + 2))
                    bank = st_slot(n)
                    for i in range(2):
                        h = G * g + 2 * j + i
                        mm(PS[:, bank + i, P:3 * P], KS[0:END0, h, P:2 * P], QS[0:END0, h, :])
                        last = mm(PS[:, bank + i, 0:T], KS[0:END0, h, 0:P], QS[0:END0, h, :])
                    last.then_inc(S["st_ps"], 1)

                def st_cross(g, c):
                    n, h = 6 * g + (1 + c if c < 2 else 2 + c), G * g + c
                    pe.wait_ge(S["mt_sb"], 2 * (G * g + c + 1))
                    bank = st_slot(n)
                    for k in range(KT):
                        last = mm(PS[:, bank + k // 2, (k % 2) * T:(k % 2 + 1) * T], KC[0:END0, h, k * P:(k + 1) * P], QC[0:END0, h, :])
                    last.then_inc(S["st_ps"], 1)

                def turn_max(n, w):
                    if n >= 1:
                        pe.wait_ge(S["mt_sb"], rows_ok(n))
                    pe.wait_ge(S["mx_ok"], 12 * (n + 1) if n < NG else 12 * NG + 8 * (n - NG + 1))
                    for t in range(QT):
                        last = pe.transpose(PS[0:w, MISC, t * P:(t + 1) * P], rmax[:, n % 2, t, 0:w], ident[:, :])
                    last.then_inc(S["mt_ps"], 1)

                def av0(g):
                    if g >= 1:
                        pe.wait_ge(S["av_sb"], g)
                    pe.wait_ge(S["masked"], 2 * (g + 1))
                    for k in range(QT):
                        for c in range(G):
                            w = T - k * P
                            mm(PS[32 * c:32 * c + DV, AV, k * P:T], Vs[:, k, G * g + c, :],
                               Ps[:, c, 2 * k * P:2 * k * P + w], start=(k == 0), stop=(k == 1))
                    pe.wait_ge(S["exp_ok"], G * (g + 1))
                    for k in range(KT):
                        for c in range(G):
                            last = mm(PS[32 * c:32 * c + DV, AV, T:2 * T], Vc[:, k, G * g + c, :],
                                      Pc[:, G * (g % 2) + c, k * T:(k + 1) * T], start=(k == 0), stop=(k == KT - 1))
                    last.then_inc(S["av_ps"], 1)

                def turn_out(g):
                    pe.wait_ge(S["av_sb"], g + 1)
                    pe.wait_ge(S["mt_sb"], rows_ok(min(g + 2, NG)))
                    for j in range(2 * QT):
                        last = pe.transpose(PS[:, MISC, j * P:(j + 1) * P], OT[:, j * P:(j + 1) * P], ident[:, :])
                    last.then_inc(S["ot_ps"], 1)

                pe.wait_ge(S["q_in"], 48)
                pe.wait_ge(S["k_in"], 48)
                pe.wait_ge(S["ones_in"], 16)
                pe.wait_ge(S["split_hi"], 4)
                pe.wait_ge(S["split_lo"], 4)
                pe.wait_ge(S["v_sb"], 2)
                for c in range(G):
                    max_self(0, c)
                    if c == 0:
                        pe.wait_ge(S["c_in"], 96)
                    max_cross(0, c, 0)
                    max_cross(0, c, 1)
                turn_max(0, 2 * G)
                for g in range(NG):
                    more = g + 1 < NG
                    if more:
                        max_self(g + 1, 0)
                        max_cross(g + 1, 0, 0)
                    st_self(g, 0)
                    if g >= 1:
                        turn_out(g - 1)
                    if more:
                        max_cross(g + 1, 0, 1)
                        max_self(g + 1, 1)
                    st_cross(g, 0)
                    if more:
                        max_cross(g + 1, 1, 0)
                        max_cross(g + 1, 1, 1)
                    st_cross(g, 1)
                    if more:
                        max_self(g + 1, 2)
                        max_cross(g + 1, 2, 0)
                    st_self(g, 1)
                    if more:
                        max_cross(g + 1, 2, 1)
                        max_self(g + 1, 3)
                    st_cross(g, 2)
                    if more:
                        max_cross(g + 1, 3, 0)
                        max_cross(g + 1, 3, 1)
                    st_cross(g, 3)
                    if more:
                        if g >= 1:
                            pe.wait_ge(S["ot_sb"], g)
                        turn_max(g + 1, 2 * G)
                    av0(g)
                turn_out(NG - 1)
                pe.wait_ge(S["y_ok"], NG)
                pe.wait_ge(S["ot_sb"], NG)
                turn(y, 2)
                pe.wait_ge(S["xT_sb"], 2)
                for t in range(QT):
                    last = mm(PS[:, MX, t * P:(t + 1) * P], yT[:, t * P:(t + 1) * P], w0_sb[:, 6, :])
                last.then_inc(S["o_ps"], 1)
                pe.wait_ge(S["xn_ok"], 2)
                turn(xn, 3)
                pe.wait_ge(S["xT_sb"], 3)
                for f in range(FT):
                    last = mm(PS[:, STB + f // 2, (f % 2) * T:(f % 2 + 1) * T], fc1[:, f * P:(f + 1) * P], xnT[:, :])
                    if f % 2:
                        last.then_inc(S["f_ps"], 1)
                for f in range(FT):
                    pe.wait_ge(S["s_ok"], FT) if f == 0 else None
                for t in range(QT):
                    for f in range(FT):
                        last = mm(PS[:, MX, t * P:(t + 1) * P], sT[:, f, t * P:(t + 1) * P], fc2[:, f, :],
                                  start=(f == 0), stop=(f == FT - 1))
                last.then_inc(S["z_ps"], 1)
                pe.wait_ge(S["xn_ok"], 3)
                turn(xn, 4)
                pe.wait_ge(S["xT_sb"], 4)
                for n in range(H // 2):
                    if n >= 4:
                        pe.wait_ge(S["qh_ok"], n - 3)
                        pe.wait_ge(S["ql_ok"], n - 3)
                    for i in range(2):
                        last = mm(PS[:, STB + n % 4, i * T:(i + 1) * T], Aall[:, 2 * n + i, :], xnT[:, :])
                    last.then_inc(S["q1_ps"], 1)

                def max1(g, c, t):
                    n, h = 2 * (G * g + c) + t, G * g + c
                    bank = mx_slot(n, 12 * NG)
                    mm(PS[:, bank, :], QH[:, h, t * P:(t + 1) * P], K1[:, :]).then_inc(S["mx_ps"], 1)

                def st1(g, c):
                    n, h = 6 * NG + G * g + c, G * g + c
                    pe.wait_ge(S["mt_sb"], rows_ok(NG) + h + 1)
                    bank = st_slot(n)
                    for k in range(KT):
                        o = PS[:, bank + k // 2, (k % 2) * T:(k % 2 + 1) * T]
                        mm(o, K1[:, k * P:(k + 1) * P], QH[:, h, :], stop=False)
                        last = mm(o, K2[:, k * P:(k + 1) * P], QL[0:ROWS, h, :], start=False)
                    last.then_inc(S["st_ps"], 1)

                def av1(g):
                    pe.wait_ge(S["exp_ok"], H + G * (g + 1))
                    if g >= 1:
                        pe.wait_ge(S["av_sb"], NG + g)
                    for c in range(0, G, 2):
                        for k in range(KT):
                            for i in range(2):
                                mm(PS[D1 * i:D1 * i + D1, AV, (c // 2) * T:(c // 2 + 1) * T], ctx_sb[:, k, :],
                                   Pc[:, G * (g % 2) + c + i, k * T:(k + 1) * T], start=(k == 0), stop=(k == KT - 1))
                    if g >= 1:
                        pe.wait_ge(S["sum_sb"], g)
                    pe.wait_ge(S["mt_sb"], rows_ok(min(NG + g + 2, 2 * NG)))
                    for k in range(KT):
                        for c in range(G):
                            last = mm(PS[32 * c:32 * c + 32, MISC, T:2 * T], ones32[:, :],
                                      Pc[:, G * (g % 2) + c, k * T:(k + 1) * T], start=(k == 0), stop=(k == KT - 1))
                    last.then_inc(S["av_ps"], 1)

                pe.wait_ge(S["kk_hi"], 2)
                pe.wait_ge(S["kk_lo"], 1)
                pe.wait_ge(S["qh_ok"], H // 2)
                pe.wait_ge(S["ql_ok"], H // 2)
                for c in range(G):
                    max1(0, c, 0)
                    max1(0, c, 1)
                turn_max(NG, G)
                for g in range(NG):
                    for c in range(G):
                        if g + 1 < NG:
                            max1(g + 1, c, 0)
                            max1(g + 1, c, 1)
                        st1(g, c)
                    if g + 1 < NG:
                        if g >= 1:
                            pe.wait_ge(S["sum_sb"], g)
                        turn_max(NG + g + 1, G)
                    av1(g)
                for j in range(H // 2):
                    if j % 2 == 0:
                        pe.wait_ge(S["un_ok"], j // 2 + 1)
                    last = mm(PS[:, MX, 0:T], Ball[:, j, :], U[:, j, :], start=(j == 0), stop=(j == H // 2 - 1))
                last.then_inc(S["o1_ps"], 1)
                pe.wait_ge(S["o1_sb"], 1)
                for t in range(QT):
                    last = pe.transpose(PS[:, MX + 1, t * P:(t + 1) * P], oT[:, t * P:(t + 1) * P], ident[:, :])
                last.then_inc(S["o1T_ps"], 1)
                end_of_batch(pe, "pe")

            pe.wait_ge(TS["t_xm"], 1)
            for t in range(TILES):
                last = pe.transpose(PS[:, t // 4, (t % 4) * P:(t % 4 + 1) * P], xm[:, t, :], ident[:, :])
                if t % 4 == 3:
                    last.then_inc(TS["t_xT"], 1)
            pe.wait_ge(TS["t_xTsb"], 2)
            for t in range(TILES):
                last = mm(PS[:, 2, t * E:(t + 1) * E], xmT[:, t * P:(t + 1) * P], gwT[:, :])
            last.then_inc(TS["t_lg"], 1)
            pe.wait_ge(TS["t_oh"], 1)
            rank = PS[:, 3, 0:TILES * E].rearrange("p (t e) -> p t e", e=E)
            mm(rank, tri[:, :], oh[:, :, :], stop=False)
            for t in range(TILES - 1):
                w = TILES - 1 - t
                last = mm(rank[:, t + 1:TILES, :], onesb[:, :], oh[:, t, :].unsqueeze(1).broadcast_to([P, w, E]),
                          start=False, stop=(t == TILES - 2))
            last.then_inc(TS["t_rk"], 1)
            pe.wait_ge(TS["t_xd"], 16)
            for t in range(ST):
                last = pe.transpose(PS[:, 4 + t // 4, (t % 4) * P:(t % 4 + 1) * P], XD[:, t, :], ident[:, :])
                if t % 4 == 3 or t == ST - 1:
                    last.then_inc(TS["t_dT"], 1)
            pe.wait_ge(TS["t_dTsb"], 3)
            pe.wait_ge(s_w1, 16 * E)
            pe.wait_ge(TS["t_slot"], 1)

            def up(e):
                if e >= 2:
                    pe.wait_ge(TS["t_g"], e - 1)
                for f in range(FT):
                    last = mm(PS[:, e % 2, f * CAP:(f + 1) * CAP], w1_all[:, e, f * P:(f + 1) * P],
                              XT[:, e * CAP:(e + 1) * CAP])
                last.then_inc(TS["t_h"], 1)

            def down(e):
                pe.wait_ge(TS["t_w2"], 16 * (e + 1))
                pe.wait_ge(TS["t_g"], e + 1)
                q = e // 4
                if q >= 2 and e % 4 == 0:
                    pe.wait_ge(TS["t_ysb"], q - 1)
                for f in range(FT):
                    last = mm(PS[0:CAP, 2 + q % 2, (e % 4) * C:(e % 4 + 1) * C], hT[:, e % 2, f, :], w2_all[:, e, f, :],
                              start=(f == 0), stop=(f == FT - 1))
                last.then_inc(TS["t_y"], 1)
            up(0)
            for e in range(E):
                if e + 1 < E:
                    up(e + 1)
                down(e)

        @block.vector
        def _(dve):
            dve.memset(y[:, :, :], 0.0).then_inc(s_zero, 1)
            for t in (KS, QS, QC):
                dve.memset(t[:, :, :].bitcast(F32), 0.0)
            setup = Chain(dve, s_setup)
            setup(dve.memset(K2[:, :].bitcast(F32), 0.0))
            dve.memset(w0_sb[CC:P, 4:6, :], 0.0)
            dve.memset(PS[:, AV, :], 0.0)
            dve.memset(onesb[:, :], 1.0)
            dve.memset(ones32[:, :], 1.0)
            dve.memset(Vs[:, :, :, D0:DV], 1.0)
            dve.memset(Vc[:, :, :, D0:DV], 1.0)
            dve.wait_ge(s_load, 16 * 30)
            dve.wait_ge(s_tanh, 1)
            dve.scalar_tensor_tensor(out=fc1[:, :], in0=fcq[:, 0, :], scalar=-128.0, in1=fcs[:, 0, :], op0=ALU.add, op1=ALU.mult)
            dve.scalar_tensor_tensor(out=fc2[:, :, :].rearrange("p f c -> p (f c)"), in0=fcq[:, 1, :], scalar=-128.0,
                                     in1=fcs[:, 1, :], op0=ALU.add, op1=ALU.mult)
            dve.tensor_scalar(fc1bh[:, :], fc1b[:, :], 0.5, None, ALU.mult)
            dve.tensor_scalar(fc2bh[:, :], fc2bh[:, :], 0.5, None, ALU.mult)
            dve.tensor_tensor(bvsum[:, :], bv_sb[:, 0:1], bv_sb[:, 1:2], ALU.add)
            dve.memset(K2[ONE1:ONE1 + G, :].bitcast(F32), 1.0)
            setup(dve.memset(KS[ONE0:END0, :, :].bitcast(F32), 1.0))
            setup(dve.memset(KC[:, :, :].bitcast(F32), 0.0))
            setup(dve.memset(KC[ONE0:END0, :, T:TC].bitcast(F32), 1.0))
            dve.drain().then_inc(s_zero, 1)
            dve.wait_ge(s_abc, 1)
            dve.wait_ge(s_const, 1)
            dve.wait_ge(s_zslots, 16 * ST)
            with dve.Fori(0, B) as b:
                link = Chain(dve, S["dchain"])
                count = {"var": 0, "rstd_ok": 0, "xn_ok": 0, "xT_sb": 0, "mx": 0}

                def norm(src, dst, last=None):
                    for t in range(QT):
                        i = dve.bn_stats(stats[:, t, :], src[:, t, :])
                    link(i)
                    for t in range(QT):
                        i = dve.bn_aggr(mv[:, t, :], stats[:, t, :])
                    link(i)
                    dve.tensor_scalar(ve[:, 0:QT], mv[:, 0:QT, 1], EPS, None, ALU.add).then_inc(S["var"], 1)
                    count["var"] += 1
                    dve.wait_ge(S["rstd_ok"], count["var"])
                    for t in range(QT):
                        i = dve.tensor_scalar(dst[:, t, :], src[:, t, :], mv[:, t, 0:1], rstd[:, t:t + 1],
                                              ALU.subtract, ALU.mult)
                    if last:
                        i.then_inc(S[last], 1)
                    else:
                        link(i)

                def turned(n, dst):
                    dve.wait_ge(S["xT_ps"], n)
                    return PS[:, MISC, 0:T]

                x_in = x_all[:, bass.ds(b * QT, QT), :]
                link(dve.tensor_copy(x1[:, :, :], x_in))
                norm(x1, xn, "xn_ok")
                dve.wait_ge(S["kk_hi"], 2)
                dve.tensor_tensor(K1[CC:P, :], cT[CC:P, :], K1[CC:P, :], ALU.subtract).then_inc(S["kk_lo"], 1)
                dve.wait_ge(S["xT_ps"], 1)
                dve.tensor_copy(xnT[:, :], PS[:, MISC, 0:T]).then_inc(S["xT_sb"], 1)

                def low(n):
                    off, w = ((3 * T, TC), (0, T), (T, T), (2 * T, T))[n]
                    dve.wait_ge(S["split_hi"], n + 1)
                    dve.tensor_tensor(lo[:, off:off + w], raw[:, off:off + w], hi[:, off:off + w], ALU.subtract
                                      ).then_inc(S["split_lo"], 1)
                low(0)
                dve.wait_ge(S["ctx_ps"], 2)
                dve.tensor_copy(Vc[:, :, :, 0:D0], PS[:, 4, :].rearrange("p (k h d) -> p k h d", k=KT, h=H)
                                ).then_inc(S["v_sb"], 1)
                for n in (1, 2, 3):
                    low(n)
                dve.wait_ge(S["proj_ps"], 4)
                dve.tensor_copy(Vs[:, :, :, 0:D0], PS[:, 3, 0:T].rearrange("p (k h d) -> p k h d", k=QT, h=H)
                                ).then_inc(S["v_sb"], 1)

                def take_max(n, bank_n, g, reduces):
                    dve.wait_ge(S["mx_ps"], n)
                    for (a, e), t, col in reduces:
                        i = dve.tensor_reduce(rmax[:, g % 2, t, col:col + 1], PS[:, MX + bank_n % 2, a:e], X, ALU.max)
                    i.then_inc(S["mx_ok"], 1)

                def max0(g):
                    if g >= 2:
                        dve.wait_ge(S["mt_ps"], g - 1)
                    for c in range(G):
                        n = 12 * g + 3 * c
                        take_max(n + 1, n, g, [((0, P), 0, c), ((T, 2 * T), 1, c)])
                        for t in range(QT):
                            take_max(n + 2 + t, n + 1 + t, g, [((0, TC), t, G + c)])
                        if c == 1 and g >= 2:
                            out0(g - 2)

                def evac0(g):
                    dve.wait_ge(S["av_ps"], g + 1)
                    if g >= 1:
                        dve.wait_ge(S["ot_ps"], g)
                    dve.tensor_copy(OT[:, :], PS[:, AV, :]).then_inc(S["av_sb"], 1)

                def out0(g):
                    dve.wait_ge(S["ot_ps"], g + 1)
                    o = PS[:, MISC, :].rearrange("p (j c d) -> p j c d", j=2 * QT, c=G)
                    link(dve.reciprocal(rc0[:, :, :], o[:, :, :, D0]))
                    i = dve.tensor_tensor(yn[:, :, :, :], o[:, :, :, 0:D0],
                                          rc0[:, :, :].unsqueeze(3).broadcast_to([P, 2 * QT, G, D0]), ALU.mult)
                    i.then_inc(S["ot_sb"], 1)
                    dve.wait_ge(S["ot_sb"], g + 1)
                    dve.tensor_tensor(y[:, :, :].rearrange("p t (h d) -> p t h d", h=H)[:, :, G * g:G * g + G, :],
                                      yn[:, 0:QT, :, :], yn[:, QT:2 * QT, :, :], ALU.add).then_inc(S["y_ok"], 1)
                max0(0)
                for g in range(NG):
                    if g + 1 < NG:
                        max0(g + 1)
                    elif g >= 1:
                        out0(g - 1)
                    evac0(g)
                out0(NG - 1)
                dve.wait_ge(S["xT_ps"], 2)
                dve.tensor_scalar(yT[:, :], PS[:, MISC, 0:T], bvsum[:, :], None, ALU.add).then_inc(S["xT_sb"], 1)
                dve.wait_ge(S["o_ps"], 1)
                o = PS[:, MX, 0:T].rearrange("p (t c) -> p t c", t=QT)
                link(dve.tensor_tensor(tmp[:, :, :], o, bp_sb[:, :].unsqueeze(1).broadcast_to([P, QT, C]), ALU.add))
                link(dve.scalar_tensor_tensor(out=x1[:, :, :], in0=tmp[:, :, :], scalar=tg[:, 0:1], in1=x1[:, :, :],
                                              op0=ALU.mult, op1=ALU.add))
                norm(x1, xn1)
                norm(xn1, xn, "xn_ok")
                dve.wait_ge(S["xT_ps"], 3)
                dve.tensor_scalar(xnT[:, :], PS[:, MISC, 0:T], gb_sb[:, 0:1], gb_sb[:, 1:2], ALU.mult, ALU.add
                                  ).then_inc(S["xT_sb"], 1)
                dve.wait_ge(S["t1_ok"], 1)
                for f in range(FT):
                    dve.scalar_tensor_tensor(out=sT[:, f, :], in0=PS[:, STB + f // 2, (f % 2) * T:(f % 2 + 1) * T],
                                             scalar=fc1b[:, f:f + 1], in1=th[:, f, :], op0=ALU.add, op1=ALU.mult
                                             ).then_inc(S["s_ok"], 1)
                dve.wait_ge(S["z_ps"], 1)
                link(dve.scalar_tensor_tensor(out=tmp[:, :, :], in0=o, scalar=0.25, in1=xn1[:, :, :], op0=ALU.mult, op1=ALU.add))
                link(dve.tensor_tensor(tmp[:, :, :], tmp[:, :, :], fc2bh[:, :].unsqueeze(1).broadcast_to([P, QT, C]), ALU.add))
                link(dve.scalar_tensor_tensor(out=x1[:, :, :], in0=tmp[:, :, :], scalar=tg[:, 2:3], in1=x1[:, :, :],
                                              op0=ALU.mult, op1=ALU.add))
                norm(x1, xn, "xn_ok")
                dve.wait_ge(S["xT_ps"], 4)
                dve.tensor_copy(xnT[:, :], PS[:, MISC, 0:T]).then_inc(S["xT_sb"], 1)
                for n in range(H // 2):
                    dve.wait_ge(S["qh_ok"], n + 1)
                    dve.tensor_tensor(QL[0:CC, 2 * n:2 * n + 2, :],
                                      PS[0:CC, STB + n % 4, :].rearrange("p (a b) -> p a b", a=2),
                                      QH[0:CC, 2 * n:2 * n + 2, :], ALU.subtract
                                      ).then_inc(S["ql_ok"], 1)

                def max1(g):
                    if g >= 2:
                        dve.wait_ge(S["mt_ps"], NG + g - 1)
                    for c in range(G):
                        for t in range(QT):
                            n = 2 * (G * g + c) + t
                            take_max(12 * NG + n + 1, n, g, [((0, TC), t, c)])

                def evac1(g):
                    dve.wait_ge(S["av_ps"], NG + g + 1)
                    dve.tensor_copy(U[:, 2 * g:2 * g + 2, :].rearrange("p a b -> p (a b)"), PS[:, AV, :]
                                    ).then_inc(S["av_sb"], 1)
                    if g >= 1:
                        dve.wait_ge(S["rinv_out"], 16 * g)
                    dve.reciprocal(rsum[:, :], PS[:, MISC, T:2 * T]).then_inc(S["sum_sb"], 1)
                max1(0)
                for g in range(NG):
                    if g + 1 < NG:
                        max1(g + 1)
                    evac1(g)
                dve.wait_ge(S["o1_ps"], 1)
                dve.tensor_scalar(oT[:, :], PS[:, MX, 0:T], bo_sb[:, :], tg[:, 1:2], ALU.add, ALU.mult).then_inc(S["o1_sb"], 1)
                dve.wait_ge(S["o1T_ps"], 1)
                dve.tensor_tensor(x_all[:, bass.ds(b * QT, QT), :],
                                  PS[:, MX + 1, 0:T].rearrange("p (t c) -> p t c", t=QT), x1[:, :, :], ALU.add)
                end_of_batch(dve, "dve")

            link = Chain(dve, TS["t_chain"])
            for t in range(TILES):
                i = dve.bn_stats(stats[:, t, :], x_all[:, t, :])
            link(i)
            for t in range(TILES):
                i = dve.bn_aggr(mv[:, t, :], stats[:, t, :])
            link(i)
            dve.tensor_scalar(ve[:, :], mv[:, :, 1], EPS, None, ALU.add).then_inc(TS["t_var"], 1)
            dve.wait_ge(TS["t_rstd"], 1)
            for t in range(TILES):
                i = dve.tensor_scalar(xm[:, t, :], x_all[:, t, :], mv[:, t, 0:1], rstd[:, t:t + 1], ALU.subtract, ALU.mult)
            i.then_inc(TS["t_xm"], 1)
            for j in range(2):
                dve.wait_ge(TS["t_xT"], j + 1)
                dve.tensor_copy(xmT[:, 512 * j:512 * j + 512], PS[:, j, :]).then_inc(TS["t_xTsb"], 1)
            dve.wait_ge(TS["t_lg"], 1)
            lg = PS[:, 2, 0:TILES * E].rearrange("p (t e) -> p t e", e=E)

            def over_e(a):
                return a[:, :].unsqueeze(2).broadcast_to([P, TILES, E])
            iota3 = iota_e[:, :].unsqueeze(1).broadcast_to([P, TILES, E])
            link(dve.tensor_reduce(lmax[:, :], lg, X, ALU.max))
            dve.tensor_tensor(eq[:, :, :], lg, over_e(lmax), ALU.subtract).then_inc(TS["t_lm"], 1)
            dve.wait_ge(TS["t_lm"], 1)
            link(dve.tensor_scalar(pick[:, :, :], eq[:, :, :], 0.0, None, ALU.is_ge))
            link(dve.tensor_tensor(pick[:, :, :], pick[:, :, :], iota3, ALU.mult))
            link(dve.tensor_reduce(arg[:, :], pick[:, :, :], X, ALU.min))
            dve.tensor_tensor(oh[:, :, :], over_e(arg), iota3, ALU.is_equal).then_inc(TS["t_oh"], 1)
            dve.wait_ge(TS["t_ex"], 1)
            link(dve.reduce_sum(exs[:, :], ex[:, :, :], X))
            link(dve.reciprocal(wgt[:, :], exs[:, :]))
            link(dve.tensor_scalar(wgt[:, :], wgt[:, :], tg[:, 3:4], None, ALU.mult))
            dve.wait_ge(TS["t_oh"], 1)
            dve.wait_ge(TS["t_rk"], 1)
            link(dve.tensor_tensor(ex[:, :, :], PS[:, 3, 0:TILES * E].rearrange("p (t e) -> p t e", e=E), oh[:, :, :], ALU.mult))
            link(dve.reduce_sum(rk[:, :], ex[:, :, :], X))
            link(dve.tensor_scalar(drop[:, :], rk[:, :], float(CAP), FAR, ALU.is_gt, ALU.mult))
            link(dve.scalar_tensor_tensor(out=slot[:, :], in0=arg[:, :], scalar=float(CAP), in1=rk[:, :], op0=ALU.mult, op1=ALU.add))
            link(dve.tensor_scalar(slot[:, :], slot[:, :], float(E * CAP - 1), None, ALU.add))
            dve.tensor_tensor(slot_i[:, :], slot[:, :], drop[:, :], ALU.add).then_inc(TS["t_slot"], 1)
            for j in range(3):
                w = min(512, SLOTS - 512 * j)
                dve.wait_ge(TS["t_dT"], j + 1)
                dve.tensor_copy(XT[:, 512 * j:512 * j + w], PS[:, 4 + j, 0:w]).then_inc(TS["t_dTsb"], 1)
            for q in range(E // 4):
                dve.wait_ge(TS["t_y"], 4 * q + 4)
                dve.tensor_copy(YB[:, 4 * q:4 * q + 4, :].rearrange("p e c -> p (e c)"), PS[0:CAP, 2 + q % 2, :]
                                ).then_inc(TS["t_ysb"], 1)
            dve.wait_ge(TS["t_sc"], 16 * TILES)
            for t in range(TILES):
                dve.wait_ge(s_back[t], 16)
                dve.scalar_tensor_tensor(out=xm[:, t, :], in0=Yg[:, t, :], scalar=wgt[:, t:t + 1], in1=x_all[:, t, :],
                                         op0=ALU.mult, op1=ALU.add).then_inc(TS["t_out"], 1)


_OUT = (B, T, C)


def kernel(**inputs):
    import numpy as np
    import concourse.bacc as bacc
    from concourse.bass_utils import run_bass_kernel_spmd

    a = {k: np.asarray(v) for k, v in inputs.items()}
    pre = "L0_xattn_"
    heads = lambda w: np.ascontiguousarray(w.reshape(w.shape[0], H, D1).transpose(2, 1, 0))
    arrays = {
        "x": a["x"], "ctx": a["ctx_512"], "ctxT": np.ascontiguousarray(a["ctx_512"].transpose(0, 2, 1)),
        "g_xattn": a["g_xattn"], "g_ffn": a["g_ffn"],
        "wqT": heads(a["L1_xattn_Wq"]), "wkT": heads(a["L1_xattn_Wk"]), "wvT": heads(a["L1_xattn_Wv"]),
        "wo": np.ascontiguousarray(a["L1_xattn_Wo"].reshape(H, D1, C).transpose(1, 0, 2)),
        "bo": a["L1_xattn_bo"], "gate_wT": np.ascontiguousarray(a["L1_ffn_gate_w"].T),
        "w1": a["L1_ffn_w1"], "w2": a["L1_ffn_w2"],
        "gamma": a["L0_ffn_ln_gamma"], "beta": a["L0_ffn_ln_beta"],
        "fc1_q": a["L0_ffn_fc1_q"], "fc1_s": a["L0_ffn_fc1_scales"], "fc1_b": np.ascontiguousarray(a["L0_ffn_fc1_bias"].reshape(FT, P).T),
        "fc2_q": a["L0_ffn_fc2_q"], "fc2_s": a["L0_ffn_fc2_scales"], "fc2_b": a["L0_ffn_fc2_bias"],
    }
    for n in ("Wq", "Wk", "Wcq", "Wv", "Wck", "Wcv", "Wp", "bq", "bk", "bcq", "bck", "bv", "bcv", "bp"):
        arrays[n] = a[pre + n]
    nc = bacc.Bacc("TRN2", target_bir_lowering=False, num_devices=1)
    t = {}
    for name, v in arrays.items():
        t[name] = nc.dram_tensor(f"in_{name}", v.shape, mybir.dt.from_np(v.dtype), kind="ExternalInput").ap()
    out = nc.dram_tensor("out_x", _OUT, F32, kind="ExternalOutput").ap()
    build(nc, t["x"], t["ctx"], t["ctxT"], t["g_xattn"], t["g_ffn"],
          [t[n] for n in ("Wq", "Wk", "Wcq", "Wv", "Wck", "Wcv", "Wp")],
          [t[n] for n in ("bq", "bk", "bcq", "bck")], [t["bv"], t["bcv"]], t["bp"], t["gamma"], t["beta"],
          t["fc1_q"], t["fc1_s"], t["fc1_b"], t["fc2_q"], t["fc2_s"], t["fc2_b"],
          t["wqT"], t["wkT"], t["wvT"], t["wo"], t["bo"], t["gate_wT"], t["w1"], t["w2"], out)
    r = run_bass_kernel_spmd(nc, [{f"in_{k}": v for k, v in arrays.items()}], core_ids=[0])
    return r.results[0]["out_x"]
```

```python
from contextlib import ExitStack

import concourse.bass as bass
from concourse import mybir

F32 = mybir.dt.float32
F32R = mybir.dt.float32r
BF16 = mybir.dt.bfloat16
I32 = mybir.dt.int32
U32 = mybir.dt.uint32
ALU = mybir.AluOpType
ACT = mybir.ActivationFunctionType
X = mybir.AxisListType.X

P = 128
B, T, C = 4, 256, 128
TC, CC = 512, 64
QT, KT = T // P, TC // P
H, D0, D1 = 16, 8, 64
G = 4
NG = H // G
FF = 512
FT = FF // P
E = 16
TILES = B * QT
CAP = int(1.25 * B * T / E)
CAP += CAP % 2
SLOTS = E * CAP
ST = SLOTS // P
EPS = 1e-5
NEG = -1e30
FAR = 1e6
SCALE0 = D0 ** -0.5
SCALE1 = D1 ** -0.5
ROWS = 96
ONE0 = ROWS
END0 = ONE0 + 2 * G
ONE1 = 64
DV = D0 + 1


class Chain:

    def __init__(self, eng, sem):
        self.eng, self.sem, self.n = eng, sem, 0

    def __call__(self, ins):
        self.n += 1
        ins.then_inc(self.sem, 1)
        self.eng.wait_ge(self.sem, self.n)


def build(nc, x, ctx, ctxT, w0, columns, rows, fc_q, heads_w, w1, w2, out):
    place = [(nc.sbuf_base + 31) // 32 * 32]

    def sb(name, shape, dt=F32, at=None):
        size = 2 if dt == BF16 else 4
        for n in shape[1:]:
            size *= n
        offset = place[0] if at is None else at
        if at is None:
            place[0] += (size + 31) // 32 * 32
        return nc.alloc_sbuf_tensor_at(name, shape, dt, offset=offset)

    with ExitStack() as stack:
        def sem(name):
            return stack.enter_context(nc.semaphore(name))

        Aall = sb("Aall", [P, H, P])
        Ball = sb("Ball", [P, H // 2, P])
        w0_sb = sb("w0_sb", [P, 7, C])
        cols = sb("cols", [P, 9 + FT + E])
        b0_sb, bv_sb, gb_sb, bo_sb = cols[:, 0:4], cols[:, 4:6], cols[:, 6:8], cols[:, 8:9]
        fc1b, gwT = cols[:, 9:9 + FT], cols[:, 9 + FT:9 + FT + E]
        bcast = sb("bcast", [P, 2 * C + 4])
        bp_sb, fc2bh, gates = bcast[:, 0:C], bcast[:, C:2 * C], bcast[:, 2 * C:2 * C + 4]
        bvsum = sb("bvsum", [P, 1])
        fc1 = sb("fc1", [P, FF])
        fc2 = sb("fc2", [P, FT, C])
        fc1bh = sb("fc1bh", [P, FT])
        tg = sb("tg", [P, 4])
        ident = sb("ident", [P, P])
        identb = sb("identb", [P, P], BF16)
        causal = sb("causal", [P, P], BF16)
        tri = sb("tri", [P, P], BF16)
        pick_sum = sb("pick_sum", [P, 2, P])
        onesb = sb("onesb", [P, P], BF16)
        ones32 = sb("ones32", [P, 32])
        nd = sb("nd", [P, 2 * G])
        mhalf = sb("mhalf", [P, TILES])
        iota_i = sb("iota_i", [P, E], I32)
        iota_e = sb("iota_e", [P, E])
        x_all = sb("x_all", [P, TILES, C])

        KC_at = place[0]
        KC = sb("KC", [P, H, TC], F32R)
        KS_at = place[0]
        KS = sb("KS", [P, H, T], F32R)
        QS_at = place[0]
        assert QS_at - KC_at == 4 * H * (TC + T)
        QS = sb("QS", [P, H, T], F32R)
        QC = sb("QC", [P, H, T], F32R)
        QH_at = place[0]
        QH = sb("QH", [P, H, T], F32R)
        QL = sb("QL", [ROWS, H, T], F32R)
        w2_all = sb("w2_all", [P, E, FT, C], at=QS_at)

        Pc_at = place[0]
        Pc = sb("Pc", [P, 2 * G, KT * T])
        Ps_at = place[0]
        Ps = sb("Ps", [P, G, 3 * P])
        w1_all = sb("w1_all", [P, E, FF], at=Pc_at)
        heads_sb = sb("heads_sb", [D1, H, 2 * C + 2 * CC], at=Pc_at)
        wqT_sb, wo_sb = heads_sb[:, :, 0:C], heads_sb[:, :, C:2 * C]
        wkT_sb, wvT_sb = heads_sb[:, :, 2 * C:2 * C + CC], heads_sb[:, :, 2 * C + CC:2 * C + 2 * CC]
        U = sb("U", [P, H // 2, T], at=Ps_at)
        place[0] = max(place[0], Ps_at + 4 * H // 2 * T)
        sT = sb("sT", [P, FT, T], at=Ps_at)
        th = sb("th", [P, FT, T], at=Pc_at)
        fh = sb("fh", [P, FT, T], at=Pc_at + 4 * FT * T)
        fcq = sb("fcq", [P, 2, FF], I32, at=QH_at)
        fcs = sb("fcs", [P, 2, FF], at=QH_at + 8 * FF)

        ctx_sb = sb("ctx_sb", [P, KT, CC])
        cT = sb("cT", [P, TC])
        K1 = sb("K1", [P, TC], F32R)
        K2 = sb("K2", [ROWS, TC], F32R)
        Vs = sb("Vs", [P, QT, H, DV])
        Vc = sb("Vc", [P, KT, H, DV])
        xn = sb("xn", [P, QT, C])
        xnT = sb("xnT", [P, T])
        y_at = place[0]
        y = sb("y", [P, QT, C])
        xn1 = sb("xn1", [P, QT, C])
        tmp = sb("tmp", [P, QT, C])
        hi = sb("hi", [P, 3 * T], F32R, at=y_at)
        lo = sb("lo", [P, 3 * T], F32R)
        x1 = sb("x1", [P, QT, C])
        rmax = sb("rmax", [P, 2, QT, 2 * G])
        OT_at = place[0]
        OT = sb("OT", [P, 2 * T])
        rc0 = sb("rc0", [P, 2 * QT, G])
        yn = sb("yn", [P, 2 * QT, G, D0])
        yT = sb("yT", [P, T])
        R = sb("R", [P, 2, 2, T], at=OT_at)
        place[0] = max(place[0], OT_at + 16 * T)
        rsum = sb("rsum", [P, T])
        oT = sb("oT", [P, T])
        stats = sb("stats", [P, TILES, 6])
        mv = sb("mv", [P, TILES, 2])
        ve = sb("ve", [P, TILES])
        rstd = sb("rstd", [P, TILES])

        at = [KC_at]

        def late(name, shape, dt=F32):
            t = sb(name, shape, dt, at=at[0])
            n = 4 if dt != BF16 else 2
            for k in shape[1:]:
                n *= k
            at[0] += (n + 31) // 32 * 32
            assert at[0] <= QS_at, at[0] - QS_at
            return t
        xm = late("xm", [P, TILES, C])
        xmT = late("xmT", [P, TILES * P])
        XD = late("XD", [P, ST, C])
        XT = late("XT", [P, SLOTS])
        hT = late("hT", [P, 2, FT, CAP])
        YB = late("YB", [CAP, E, C])
        Yg = late("Yg", [P, TILES, C])
        lmax = late("lmax", [P, TILES])
        eq = late("eq", [P, TILES, E])
        arg = late("arg", [P, TILES])
        pick = late("pick", [P, TILES, E])
        oh = late("oh", [P, TILES, E], BF16)
        ex = late("ex", [P, TILES, E])
        exs = late("exs", [P, TILES])
        wgt = late("wgt", [P, TILES])
        rk = late("rk", [P, TILES])
        drop = late("drop", [P, TILES])
        slot = late("slot", [P, TILES])
        slot_i = late("slot_i", [P, TILES], U32)
        assert place[0] <= nc.sbuf_usable_end, (place[0], nc.sbuf_usable_end)

        zrow = U[:, 0, 0:C]
        PS = stack.enter_context(nc.psum_tensor("PS", [P, 8, 512], F32))
        MX, STB, AV, MISC = 0, 2, 6, 7
        x_slots = nc.dram_tensor("x_slots", (SLOTS, C), F32)
        ctx_parts = nc.dram_tensor("ctx_parts", (2, P, TC), F32)
        x_parts = nc.dram_tensor("x_parts", (2, P, 3 * T), F32)
        r_dram = nc.dram_tensor("r_dram", (2, G, T), F32)
        y_slots = nc.dram_tensor("y_slots", (SLOTS, C), F32)

        s_x = sem("s_x")
        s_w0 = sem("s_w0")
        s_cols = sem("s_cols")
        s_rows = sem("s_rows")
        s_fcq = sem("s_fcq")
        s_heads = sem("s_heads")
        s_w1 = sem("s_w1")
        s_pool0 = sem("s_pool0")
        s_zrow = sem("s_zrow")
        s_zslots = sem("s_zslots")
        s_dve_zero = sem("s_dve_zero")
        s_pool_zero = sem("s_pool_zero")
        s_ones = sem("s_ones")
        s_picks = sem("s_picks")
        s_ab = sem("s_ab")
        s_ab_sb = sem("s_ab_sb")
        s_tanh = sem("s_tanh")
        s_setup = sem("s_setup")
        s_const = sem("s_const")
        arrived = sem("arrived")
        released = {k: sem(f"released_{k}") for k in ("pe", "act", "dve", "sp")}
        early = ("ctx_in cT_in kk_hi kk_lo self_ok masked ot_ps ot_sb y_ok xT_ps xT_sb o_ps var rstd_ok xn_ok "
                 "f_ps tanh_ok h_ok s_ok z_ps q1_ps qh_ok ql_ok p_var p_rstd p_xn p_xT_ps p_xT_sb ctx_ps proj_ps v_sb "
                 "split_hi split_lo cparts_out parts_out").split()
        names = early + ("q_in k_in c_in mx_ps mx_ok mt_ps mt_sb st_ps exp_ok av_ps av_sb "
                         "pmx_ps pmx_ok pmt_ps pmt_sb sum_sb rinv_out rinv_in0 rinv_in1 r_ps un_ok un_last o1_ps o1_sb o1T_ps dchain").split()
        S = {n: sem(n) for n in names}
        t_names = ("t_var t_rstd t_xm t_xT t_xTsb t_lg t_d t_lm t_ex t_oh t_rk t_slot t_sc t_xd t_dT t_dTsb t_h t_g "
                   "t_y t_ysb t_yw t_w2 t_out t_yzero t_chain").split()
        TS = {n: sem(n) for n in t_names}
        s_back = [sem(f"s_back{t}") for t in range(TILES)]

        block = stack.enter_context(nc.Block())

        def end_of_batch(eng, key):
            eng.drain().then_inc(arrived, 1)
            eng.wait_ge(released[key], 1)
            eng.sem_clear(released[key])

        def r_rows(sp, g):
            sp.wait_ge(S["sum_sb"], g + 1)
            if g >= 2:
                sp.wait_ge(S[f"rinv_in{g % 2}"], 32 * (g // 2))
            sp.dma_start(r_dram[g % 2], rsum[0:P:32, :]).then_inc(S["rinv_out"], 16)
            sp.wait_ge(S["rinv_out"], 16 * (g + 1))
            if g >= 2:
                sp.wait_ge(S["un_ok"], g - 1)
            for i in range(2):
                sp.dma_start(R[D1 * i:D1 * i + D1, g % 2, :, :], r_dram[g % 2, i:G:2, :].partition_broadcast(D1)
                             ).then_inc(S[f"rinv_in{g % 2}"], 16)

        def rows_ok(n):
            return 2 * min(n, NG - 1) + G * max(n - (NG - 1), 0)

        AB_BANKS = (0, 1, 3, 7, 0, 1)
        SPLIT = ((4, 0, 0, TC, 3), (4, 0, 0, T, 0), (4, T, T, T, 1), (5, 0, 2 * T, T, 2))

        @block.sync
        def _(sp):
            for half in range(2):
                sp.dma_start(cT[half * CC:half * CC + CC, :], ctxT[0]).then_inc(S["cT_in"], 16)
            sp.dma_start(x_all[:, :, :], x.rearrange("b (t p) c -> p (b t) c", p=P)).then_inc(s_x, 16)
            sp.dma_start(w0_sb[:, :, :], w0).then_inc(s_w0, 16)
            sp.dma_start(cols[:, :], columns).then_inc(s_cols, 16)
            sp.dma_start(bcast[:, :], rows[0:2 * C + 4].partition_broadcast(P)).then_inc(s_rows, 16)
            sp.dma_start(heads_sb[:, :, :], heads_w).then_inc(s_heads, 16)
            sp.dma_start(fcq[:, :, :], fc_q).then_inc(s_fcq, 16)
            sp.dma_start(fcs[:, :, :].rearrange("p a f -> p (a f)"),
                         rows[2 * C + 4:2 * C + 4 + 2 * FF].partition_broadcast(P)).then_inc(s_fcq, 16)
            sp.wait_ge(s_zrow, 1)
            sp.dma_start(x_slots[:, :].rearrange("(t p) c -> p t c", p=P),
                         zrow.unsqueeze(1).broadcast_to([P, ST, C])).then_inc(s_zslots, 16)

            def load_ctxT(b):
                for half in range(2):
                    sp.dma_start(cT[half * CC:half * CC + CC, :], ctxT[bass.ds(b, 1)].rearrange("o c k -> (o c) k")
                                 ).then_inc(S["cT_in"], 16)

            def stack(dst, src, off, w, parts, s):
                for j, part in enumerate(parts):
                    sp.dma_start(dst[D0 * j:D0 * j + D0, :, :].bitcast(F32),
                                 src[part, :, off:off + w].rearrange("(h d) k -> d h k", d=D0)).then_inc(S[s], 16)

            def stack_ctx():
                sp.wait_ge(S["split_hi"], 1)
                sp.dma_start(ctx_parts[0], hi[:, 0:TC].bitcast(F32)).then_inc(S["cparts_out"], 16)
                sp.wait_ge(S["split_lo"], 1)
                sp.dma_start(ctx_parts[1], lo[:, 0:TC].bitcast(F32)).then_inc(S["cparts_out"], 16)
                sp.wait_ge(S["cparts_out"], 32)
                stack(KC, ctx_parts, 0, TC, (0, 1, 0), "c_in")

            def parts_x():
                sp.wait_ge(S["split_hi"], 4)
                sp.dma_start(x_parts[0], hi[:, :].bitcast(F32)).then_inc(S["parts_out"], 16)
                sp.wait_ge(S["split_lo"], 4)
                sp.dma_start(x_parts[1], lo[:, :].bitcast(F32)).then_inc(S["parts_out"], 16)

            def stack_x():
                sp.wait_ge(S["parts_out"], 32)
                stack(QS, x_parts, 0, T, (0, 0, 1), "q_in")
                stack(KS, x_parts, T, T, (0, 1, 0), "k_in")
                stack(QC, x_parts, 2 * T, T, (0, 0, 1), "c_in")

            def stacked():
                sp.wait_ge(S["q_in"], 48)
                sp.wait_ge(S["k_in"], 48)
                sp.wait_ge(S["c_in"], 96)

            sp.wait_ge(s_dve_zero, 1)
            stack_ctx()
            parts_x()
            sp.wait_ge(s_pool_zero, 1)
            stack_x()
            stacked()
            sp.wait_ge(s_zslots, 16)
            end_of_batch(sp, "sp")
            with sp.Fori(0, B) as b:
                sp.dma_start(ctx_sb[:, :, :],
                             ctx[bass.ds(b, 1)].rearrange("o (t p) c -> p (o t) c", p=P)).then_inc(S["ctx_in"], 16)
                sp.wait_ge(S["kk_hi"], 2)
                sp.wait_ge(S["kk_lo"], 1)
                load_ctxT((b + 1) % B)
                stack_ctx()
                r_rows(sp, 0)
                parts_x()
                stack_x()
                r_rows(sp, 1)
                r_rows(sp, 2)
                stacked()
                end_of_batch(sp, "sp")
            for e in range(E):
                sp.dma_start(w1_all[:, e, :], w1[e]).then_inc(s_w1, 16)
                sp.dma_start(w2_all[:, e, :, :], w2[e].rearrange("(f p) c -> p f c", p=P)).then_inc(TS["t_w2"], 16)
            sp.wait_ge(TS["t_sc"], 16 * TILES)
            sp.dma_start(XD[:, :, :], x_slots[:, :].rearrange("(t p) c -> p t c", p=P)).then_inc(TS["t_xd"], 16)
            for q in range(E // 4):
                sp.wait_ge(TS["t_ysb"], q + 1)
                sp.dma_start(y_slots[q * 4 * CAP:(q + 1) * 4 * CAP, :].rearrange("(e s) c -> s e c", s=CAP),
                             YB[:, 4 * q:4 * q + 4, :]).then_inc(TS["t_yw"], 16)
            for t in range(TILES):
                sp.wait_ge(TS["t_out"], t + 1)
                sp.dma_start(out[t // QT, (t % QT) * P:(t % QT + 1) * P, :], xm[:, t, :]).then_inc(TS["t_d"], 16)
            sp.wait_ge(TS["t_d"], 16 * TILES)

        @block.gpsimd
        def _(pool):
            link = Chain(pool, s_pool0)

            def diagonal(t, op, fill, base=0, step=-1, mult=1):
                return pool.affine_select(out=t[:, :], in_=t[:, :], compare_op=op, fill=fill, base=base,
                                          pattern=[[step, P]], channel_multiplier=mult)
            pool.memset(mhalf[:, :], -0.5)
            pool.memset(pick_sum[:, :, :], 0.0)
            link(pool.memset(ident[:, :], 0.0))
            diagonal(ident, ALU.not_equal, 1.0).then_inc(s_ones, 1)
            pool.memset(identb[:, :], 0.0)
            pool.memset(causal[:, :], 0.0)
            pool.memset(nd[:, :], 0.0)
            link(pool.memset(tri[:, :], 1.0))
            diagonal(identb, ALU.not_equal, 1.0)
            diagonal(causal, ALU.is_ge, NEG)
            diagonal(tri, ALU.is_ge, 0.0, step=1, mult=-1)
            pool.affine_select(out=nd[:, :], in_=nd[:, :], compare_op=ALU.not_equal, fill=-1.0, base=0,
                               pattern=[[-1, 2 * G]], channel_multiplier=1)
            link(pool.iota(iota_i[:, :], pattern=[[1, E]], base=-E, channel_multiplier=0))
            pool.tensor_copy(iota_e[:, :], iota_i[:, :])
            for j in range(2):
                for i in range(2):
                    v = pick_sum[:, j, D1 * i:D1 * i + D1]
                    pool.affine_select(out=v, in_=v, compare_op=ALU.not_equal, fill=1.0, base=-32 * (2 * j + i),
                                       pattern=[[0, D1]], channel_multiplier=1)
            for t in (KS, QC):
                pool.memset(t[:, :, :].bitcast(F32), 0.0)
            pool.memset(QL[:, :, :].bitcast(F32), 0.0)
            pool.drain().then_inc(s_pool_zero, 1)

            def rsqrt_next():
                pool.wait_ge(S["p_var"], 1)
                pool.tensor_tensor(rstd[:, 0:QT], ve[:, 0:QT], mhalf[:, 0:QT], ALU.pow).then_inc(S["p_rstd"], 1)

            def clear(sems):
                for s in sems:
                    pool.sem_clear(S[s])

            def end_batch(sems):
                pool.drain()
                pool.wait_ge(arrived, 4)
                pool.sem_clear(arrived)
                clear(sems)
                for s in released.values():
                    pool.sem_inc(s, 1)
            rsqrt_next()
            end_batch(names)
            with pool.Fori(0, B) as b:
                def rsqrt(n):
                    pool.wait_ge(S["var"], n)
                    pool.tensor_tensor(rstd[:, 0:QT], ve[:, 0:QT], mhalf[:, 0:QT], ALU.pow).then_inc(S["rstd_ok"], 1)
                for g in range(NG):
                    pool.wait_ge(S["self_ok"], 2 * g + 2)
                    for a in (0, 2):
                        v = Ps[:, :, a * P:(a + 1) * P]
                        pool.affine_select(out=v, in_=v, compare_op=ALU.is_ge, fill=0.0, base=0,
                                           pattern=[[0, G], [1, P]], channel_multiplier=-1).then_inc(S["masked"], 1)
                rsqrt(1)
                rsqrt(2)
                rsqrt(3)
                rsqrt_next()
                for g in range(NG - 1):
                    pool.wait_ge(S[f"rinv_in{g % 2}"], 32 * (g // 2 + 1))
                    pool.wait_ge(S["av_sb"], NG + g + 1)
                    u = U[:, 2 * g:2 * g + 2, :]
                    pool.tensor_tensor(u, u, R[:, g % 2, :, :], ALU.mult).then_inc(S["un_ok"], 1)
                clear(early)
                end_batch(names[len(early):])
            pool.wait_ge(TS["t_var"], 1)
            pool.tensor_tensor(rstd[:, :], ve[:, :], mhalf[:, :], ALU.pow).then_inc(TS["t_rstd"], 1)
            pool.memset(Yg[:, :, :], 0.0).then_inc(TS["t_yzero"], 1)
            pool.wait_ge(TS["t_slot"], 1)
            for t in range(TILES):
                pool.indirect_dma_start(x_slots[:, :], bass.IndirectOffsetOnAxis(slot_i[:, t:t + 1], 0),
                                        xm[:, t, :], None, bounds_check=SLOTS - 1, oob_is_err=False
                                        ).then_inc(TS["t_sc"], 16)
            pool.wait_ge(TS["t_yzero"], 1)
            pool.wait_ge(TS["t_yw"], 16 * (E // 4))
            for t in range(TILES):
                pool.indirect_dma_start(Yg[:, t, :], None, y_slots[:, :],
                                        bass.IndirectOffsetOnAxis(slot_i[:, t:t + 1], 0),
                                        bounds_check=SLOTS - 1, oob_is_err=False).then_inc(s_back[t], 16)

        @block.scalar
        def _(act):
            act.wait_ge(s_rows, 16)
            act.activation(tg[:, :], gates, ACT.Tanh).then_inc(s_tanh, 1)
            act.wait_ge(s_cols, 16)

            def high(n):
                bank, at, off, w, bias = SPLIT[n]
                act.wait_ge(S["ctx_ps"] if n == 0 else S["proj_ps"], (1, 2, 2, 4)[n])
                if n == 1:
                    act.wait_ge(S["cparts_out"], 32)
                act.activation(hi[:, off:off + w], PS[:, bank, at:at + w], ACT.Identity, bias=b0_sb[:, bias:bias + 1]
                               ).then_inc(S["split_hi"], 1)
            def neg_max0(g, turned, n, done):
                act.wait_ge(S[turned], n)
                for q in (QS, QC):
                    act.activation(q[ONE0:END0, G * g:G * g + G, :],
                                   PS[0:2 * G, MISC, 0:T].unsqueeze(1).broadcast_to([2 * G, G, T]), ACT.Copy, scale=-1.0
                                   ).then_inc(S[done], 1)
            act.wait_ge(s_ones, 1)
            act.wait_ge(s_dve_zero, 1)
            for t, first, w in ((KC, ONE0 + G, TC), (KS, ONE0, T)):
                if t is KS:
                    act.wait_ge(s_pool_zero, 1)
                for g in range(NG):
                    act.activation(t[ONE0:END0, G * g:G * g + G, :],
                                   ident[ONE0:END0, first:first + G].unsqueeze(2).broadcast_to([2 * G, G, w]), ACT.Copy
                                   ).then_inc(s_picks, 1)
            for n in range(4):
                high(n)
            for n in range(NG + 2):
                act.wait_ge(s_ab, n + 1)
                dst = Aall[:, G * n:G * n + G, :] if n < NG else Ball[:, G * (n - NG):G * (n - NG) + G, :]
                act.activation(dst.rearrange("p a b -> p (a b)"), PS[:, AB_BANKS[n], :], ACT.Copy).then_inc(s_ab_sb, 1)
            neg_max0(0, "pmt_ps", 1, "pmt_sb")
            end_of_batch(act, "act")
            with act.Fori(0, B) as b:
                def neg_max1(g):
                    act.wait_ge(S["mt_ps"], NG + g)
                    for c in range(G):
                        act.activation(QL[ONE1:ONE1 + G, G * g + c, :], PS[0:G, MISC, 0:T], ACT.Copy,
                                       scale=nd[0:G, c:c + 1]).then_inc(S["mt_sb"], 1)

                act.activation(K1[:, :], cT[:, :], ACT.Copy).then_inc(S["kk_hi"], 1)
                act.activation(K2[0:CC, :], cT[0:CC, :], ACT.Copy).then_inc(S["kk_hi"], 1)
                for g in range(NG):
                    for u in range(6):
                        n = 6 * g + u
                        act.wait_ge(S["st_ps"], n + 1)
                        bank = STB + 2 * (n % 2)
                        if u in (0, 3):
                            if g >= 1:
                                act.wait_ge(S["av_ps"], g)
                            j = 2 * (u // 3)
                            act.activation(Ps[:, j:j + 2, :], PS[:, bank:bank + 2, 0:3 * P], ACT.Exp, scale=SCALE0
                                           ).then_inc(S["self_ok"], 1)
                        else:
                            c = u - 1 if u < 3 else u - 2
                            if g >= 2:
                                act.wait_ge(S["av_ps"], g - 1)
                            act.activation(Pc[:, G * (g % 2) + c, :], PS[:, bank:bank + 2, :].rearrange("p a b -> p (a b)"),
                                           ACT.Exp, scale=SCALE0).then_inc(S["exp_ok"], 1)
                    if g + 1 < NG:
                        neg_max0(g + 1, "mt_ps", g + 1, "mt_sb")
                for f in range(FT):
                    act.wait_ge(S["f_ps"], f + 1)
                    act.activation(th[:, f, :], PS[:, STB + f, 0:T], ACT.Tanh,
                                   scale=0.5, bias=fc1bh[:, f:f + 1]).then_inc(S["tanh_ok"], 1)
                    act.activation(fh[:, f, :], PS[:, STB + f, 0:T], ACT.Identity, bias=fc1b[:, f:f + 1]
                                   ).then_inc(S["h_ok"], 1)
                for n in range(H // 2):
                    act.wait_ge(S["q1_ps"], n + 1)
                    act.activation(QH[:, 2 * n:2 * n + 2, :], PS[:, STB + n % 6, :].rearrange("p (a b) -> p a b", a=2),
                                   ACT.Copy).then_inc(S["qh_ok"], 1)
                neg_max1(0)
                for g in range(NG):
                    for c in range(G):
                        n = G * g + c
                        act.wait_ge(S["st_ps"], 6 * NG + n + 1)
                        bank = STB + 2 * (n % 2)
                        if g >= 2:
                            act.wait_ge(S["av_ps"], NG + g - 1)
                        act.activation(Pc[:, G * (g % 2) + c, :], PS[:, bank:bank + 2, :].rearrange("p a b -> p (a b)"),
                                       ACT.Exp, scale=SCALE1).then_inc(S["exp_ok"], 1)
                    if g + 1 < NG:
                        neg_max1(g + 1)
                    if g == 0:
                        high(0)
                    elif g == 1:
                        for n in (1, 2, 3):
                            high(n)
                neg_max0(0, "pmt_ps", 1, "pmt_sb")
                end_of_batch(act, "act")
            act.wait_ge(TS["t_lm"], 1)
            act.activation(ex[:, :, :], eq[:, :, :], ACT.Exp).then_inc(TS["t_ex"], 1)
            for j in range(2):
                act.wait_ge(TS["t_dT"], j + 1)
            for e in range(E):
                act.wait_ge(TS["t_h"], e + 1)
                if e >= 2:
                    act.wait_ge(TS["t_y"], e - 1)
                act.activation(hT[:, e % 2, :, :].rearrange("p f s -> p (f s)"), PS[:, e % 2, 0:FT * CAP],
                               ACT.Gelu_apprx_tanh).then_inc(TS["t_g"], 1)

        @block.tensor
        def _(pe):
            def mm(o, l, r, start=True, stop=True):
                return pe.matmul(o, l, r, start=start, stop=stop)

            pe.wait_ge(s_ones, 1)
            pe.wait_ge(s_w0, 16)

            def products_of_weights():
                pe.wait_ge(s_heads, 16)
                for n in range(NG + 2):
                    if n >= 4:
                        pe.wait_ge(s_ab_sb, n - 3)
                    bank = AB_BANKS[n]
                    if n < NG:
                        for c in range(G):
                            h = G * n + c
                            last = mm(PS[:, bank, c * P:(c + 1) * P].rearrange("p (a b) -> p a b", a=2), wqT_sb[:, h, :],
                                      wkT_sb[:, h, :].unsqueeze(1).broadcast_to([D1, 2, CC]))
                    else:
                        for c in range(2 * G):
                            h = 2 * G * (n - NG) + c
                            last = mm(PS[D1 * (h % 2):D1 * (h % 2) + D1, bank, (c // 2) * P:(c // 2 + 1) * P],
                                      wvT_sb[:, h, :], wo_sb[:, h, :])
                    last.then_inc(s_ab, 1)

            def project_ctx():
                pe.wait_ge(S["p_xn"], 1)
                for t in range(QT):
                    last = pe.transpose(PS[:, 2, t * P:(t + 1) * P], xn[:, t, :], ident[:, :])
                last.then_inc(S["p_xT_ps"], 1)
                pe.wait_ge(S["cT_in"], 32)
                mm(PS[:, 4, :], w0_sb[:, 4, :], cT[:, :]).then_inc(S["ctx_ps"], 1)
                for k in range(KT):
                    last = mm(PS[:, 5, k * P:(k + 1) * P], cT[:, k * P:(k + 1) * P], w0_sb[:, 5, :])
                last.then_inc(S["ctx_ps"], 1)

            def project_x():
                pe.wait_ge(S["p_xT_sb"], 1)
                for j in range(3):
                    mm(PS[:, 4 + j // 2, (j % 2) * T:(j % 2 + 1) * T], w0_sb[:, j, :], xnT[:, :]).then_inc(S["proj_ps"], 1)
                for t in range(QT):
                    last = mm(PS[:, 5, T + t * P:T + (t + 1) * P], xnT[:, t * P:(t + 1) * P], w0_sb[:, 3, :])
                last.then_inc(S["proj_ps"], 1)

            def ctx_evacuated():
                pe.wait_ge(S["split_hi"], 1)
                pe.wait_ge(S["split_lo"], 1)
                pe.wait_ge(S["v_sb"], 1)

            def x_evacuated():
                pe.wait_ge(S["split_hi"], 4)
                pe.wait_ge(S["split_lo"], 4)
                pe.wait_ge(S["v_sb"], 2)

            def mx_slot(n, count, base):
                if base + n - 1 > 0:
                    pe.wait_ge(S[count], base + n - 1)
                return MX + n % 2

            def max_self(g, c, name="mx", n0=0):
                n, h = 3 * c, G * g + c
                bank = mx_slot(n0 + n, name + "_ok", 0)
                for t in range(QT):
                    o = PS[:, bank, t * T:(t + 1) * T]
                    mm(o, QS[0:ROWS, h, t * P:(t + 1) * P], KS[0:ROWS, h, :], stop=False)
                    last = mm(o[:, t * P:(t + 1) * P], identb[:, :], causal[:, :], start=False)
                last.then_inc(S[name + "_ps"], 1)

            def max_cross(g, c, t, name="mx", n0=0):
                n, h = 3 * c + 1 + t, G * g + c
                bank = mx_slot(n0 + n, name + "_ok", 0)
                mm(PS[:, bank, :], QC[0:ROWS, h, t * P:(t + 1) * P], KC[0:ROWS, h, :]).then_inc(S[name + "_ps"], 1)

            def stacked():
                pe.wait_ge(S["q_in"], 48)
                pe.wait_ge(S["k_in"], 48)
                pe.wait_ge(S["c_in"], 96)

            def max_next(c):
                max_self(0, c, "pmx")
                max_cross(0, c, 0, "pmx")
                max_cross(0, c, 1, "pmx")

            def turn_next():
                pe.wait_ge(S["pmx_ok"], 3 * G)
                for t in range(QT):
                    last = pe.transpose(PS[0:2 * G, MISC, t * P:(t + 1) * P], rmax[:, 0, t, 0:2 * G], ident[:, :])
                last.then_inc(S["pmt_ps"], 1)

            project_ctx()
            ctx_evacuated()
            project_x()
            products_of_weights()
            stacked()
            pe.wait_ge(s_picks, 2 * NG)
            pe.wait_ge(s_pool_zero, 1)
            pe.wait_ge(s_ab_sb, NG + 2)
            for c in range(G):
                max_next(c)
            turn_next()
            end_of_batch(pe, "pe")
            with pe.Fori(0, B) as b:
                def turn(src, n, out_bank=MISC):
                    for t in range(QT):
                        last = pe.transpose(PS[:, out_bank, t * P:(t + 1) * P], src[:, t, :], ident[:, :])
                    last.then_inc(S["xT_ps"], 1)

                def st_slot(n):
                    if n >= 2:
                        done = n - 1
                        if done <= 6 * NG:
                            full, part = divmod(done, 6)
                            pe.wait_ge(S["self_ok"], 2 * full + (0, 1, 1, 1, 2, 2)[part]) if full or part else None
                            if 4 * full + (0, 0, 1, 2, 2, 3)[part]:
                                pe.wait_ge(S["exp_ok"], 4 * full + (0, 0, 1, 2, 2, 3)[part])
                        else:
                            pe.wait_ge(S["exp_ok"], H + done - 6 * NG)
                    return STB + 2 * (n % 2)

                def st_self(g, j):
                    n = 6 * g + 3 * j
                    if g >= 1:
                        pe.wait_ge(S["mt_sb"], 2 * g - 1)
                    bank = st_slot(n)
                    for i in range(2):
                        h = G * g + 2 * j + i
                        mm(PS[:, bank + i, P:3 * P], KS[0:END0, h, P:2 * P], QS[0:END0, h, :])
                        last = mm(PS[:, bank + i, 0:T], KS[0:END0, h, 0:P], QS[0:END0, h, :])
                    last.then_inc(S["st_ps"], 1)

                def st_cross(g, c):
                    n, h = 6 * g + (1 + c if c < 2 else 2 + c), G * g + c
                    if g >= 1:
                        pe.wait_ge(S["mt_sb"], 2 * g)
                    bank = st_slot(n)
                    for k in range(KT):
                        last = mm(PS[:, bank + k // 2, (k % 2) * T:(k % 2 + 1) * T], KC[0:END0, h, k * P:(k + 1) * P], QC[0:END0, h, :])
                    last.then_inc(S["st_ps"], 1)

                def turn_max(n, w):
                    if n >= 2:
                        pe.wait_ge(S["mt_sb"], rows_ok(n - 1))
                    pe.wait_ge(S["mx_ok"], 12 * n if n < NG else 12 * (NG - 1) + 8 * (n - NG + 1))
                    for t in range(QT):
                        last = pe.transpose(PS[0:w, MISC, t * P:(t + 1) * P], rmax[:, n % 2, t, 0:w], ident[:, :])
                    last.then_inc(S["mt_ps"], 1)

                def av0(g):
                    if g >= 1:
                        pe.wait_ge(S["av_sb"], g)
                    pe.wait_ge(S["masked"], 2 * (g + 1))
                    for k in range(QT):
                        for c in range(G):
                            w = T - k * P
                            mm(PS[32 * c:32 * c + DV, AV, k * P:T], Vs[:, k, G * g + c, :],
                               Ps[:, c, 2 * k * P:2 * k * P + w], start=(k == 0), stop=(k == 1))
                    pe.wait_ge(S["exp_ok"], G * (g + 1))
                    for k in range(KT):
                        for c in range(G):
                            last = mm(PS[32 * c:32 * c + DV, AV, T:2 * T], Vc[:, k, G * g + c, :],
                                      Pc[:, G * (g % 2) + c, k * T:(k + 1) * T], start=(k == 0), stop=(k == KT - 1))
                    last.then_inc(S["av_ps"], 1)

                def turn_out(g):
                    pe.wait_ge(S["av_sb"], g + 1)
                    if min(g + 1, NG - 1):
                        pe.wait_ge(S["mt_sb"], rows_ok(min(g + 1, NG - 1)))
                    for j in range(2 * QT):
                        last = pe.transpose(PS[:, MISC, j * P:(j + 1) * P], OT[:, j * P:(j + 1) * P], ident[:, :])
                    last.then_inc(S["ot_ps"], 1)

                for g in range(NG):
                    more = g + 1 < NG
                    if more:
                        max_self(g + 1, 0, n0=12 * g)
                        max_cross(g + 1, 0, 0, n0=12 * g)
                    st_self(g, 0)
                    if g >= 1:
                        turn_out(g - 1)
                    if more:
                        max_cross(g + 1, 0, 1, n0=12 * g)
                        max_self(g + 1, 1, n0=12 * g)
                    st_cross(g, 0)
                    if more:
                        max_cross(g + 1, 1, 0, n0=12 * g)
                        max_cross(g + 1, 1, 1, n0=12 * g)
                    st_cross(g, 1)
                    if more:
                        max_self(g + 1, 2, n0=12 * g)
                        max_cross(g + 1, 2, 0, n0=12 * g)
                    st_self(g, 1)
                    if more:
                        max_cross(g + 1, 2, 1, n0=12 * g)
                        max_self(g + 1, 3, n0=12 * g)
                    st_cross(g, 2)
                    if more:
                        max_cross(g + 1, 3, 0, n0=12 * g)
                        max_cross(g + 1, 3, 1, n0=12 * g)
                    st_cross(g, 3)
                    if more:
                        if g >= 1:
                            pe.wait_ge(S["ot_sb"], g)
                        turn_max(g + 1, 2 * G)
                    av0(g)
                turn_out(NG - 1)
                pe.wait_ge(S["y_ok"], NG)
                pe.wait_ge(S["ot_sb"], NG)
                turn(y, 1)
                pe.wait_ge(S["xT_sb"], 1)
                for t in range(QT):
                    last = mm(PS[:, MX, t * P:(t + 1) * P], yT[:, t * P:(t + 1) * P], w0_sb[:, 6, :])
                last.then_inc(S["o_ps"], 1)
                pe.wait_ge(S["xn_ok"], 1)
                turn(xn, 2)
                pe.wait_ge(S["xT_sb"], 2)
                for f in range(FT):
                    mm(PS[:, STB + f, 0:T], fc1[:, f * P:(f + 1) * P], xnT[:, :]).then_inc(S["f_ps"], 1)
                for f in range(FT):
                    pe.wait_ge(S["s_ok"], f + 1)
                    for t in range(QT):
                        last = mm(PS[:, MX + t, 0:P], sT[:, f, t * P:(t + 1) * P], fc2[:, f, :],
                                  start=(f == 0), stop=(f == FT - 1))
                last.then_inc(S["z_ps"], 1)
                pe.wait_ge(S["xn_ok"], 2)
                turn(xn, 3)
                pe.wait_ge(S["xT_sb"], 3)
                def project_heads(n):
                    if n >= 6:
                        pe.wait_ge(S["qh_ok"], n - 5)
                        pe.wait_ge(S["ql_ok"], n - 5)
                    for i in range(2):
                        last = mm(PS[:, STB + n % 6, i * T:(i + 1) * T], Aall[:, 2 * n + i, :], xnT[:, :])
                    last.then_inc(S["q1_ps"], 1)

                def max1(g, c, t):
                    n, h = 2 * (G * g + c) + t, G * g + c
                    bank = mx_slot(n, "mx_ok", 12 * (NG - 1))
                    mm(PS[:, bank, :], QH[:, h, t * P:(t + 1) * P], K1[:, :]).then_inc(S["mx_ps"], 1)

                def st1(g, c):
                    n, h = 6 * NG + G * g + c, G * g + c
                    pe.wait_ge(S["mt_sb"], rows_ok(NG - 1) + h + 1)
                    bank = st_slot(n)
                    for k in range(KT):
                        o = PS[:, bank + k // 2, (k % 2) * T:(k % 2 + 1) * T]
                        mm(o, K1[:, k * P:(k + 1) * P], QH[:, h, :], stop=False)
                        last = mm(o, K2[:, k * P:(k + 1) * P], QL[0:ROWS, h, :], start=False)
                    last.then_inc(S["st_ps"], 1)

                def av1(g):
                    pe.wait_ge(S["exp_ok"], H + G * (g + 1))
                    if g >= 1:
                        pe.wait_ge(S["av_sb"], NG + g)
                    for c in range(0, G, 2):
                        for k in range(KT):
                            for i in range(2):
                                mm(PS[D1 * i:D1 * i + D1, AV, (c // 2) * T:(c // 2 + 1) * T], ctx_sb[:, k, :],
                                   Pc[:, G * (g % 2) + c + i, k * T:(k + 1) * T], start=(k == 0), stop=(k == KT - 1))
                    if g >= 1:
                        pe.wait_ge(S["sum_sb"], g)
                    pe.wait_ge(S["mt_sb"], rows_ok(min(NG + g + 1, 2 * NG - 1)))
                    for k in range(KT):
                        for c in range(G):
                            last = mm(PS[32 * c:32 * c + 32, MISC, T:2 * T], ones32[:, :],
                                      Pc[:, G * (g % 2) + c, k * T:(k + 1) * T], start=(k == 0), stop=(k == KT - 1))
                    last.then_inc(S["av_ps"], 1)

                pe.wait_ge(S["ctx_in"], 16)
                pe.wait_ge(S["kk_hi"], 2)
                pe.wait_ge(S["kk_lo"], 1)
                project_heads(0)
                project_heads(1)
                for c in range(G):
                    pe.wait_ge(S["qh_ok"], c // 2 + 1)
                    max1(0, c, 0)
                    max1(0, c, 1)
                    project_heads(2 + c)
                project_heads(6)
                project_heads(7)
                pe.wait_ge(S["ql_ok"], H // 2)
                turn_max(NG, G)
                for g in range(NG):
                    for c in range(G):
                        if g + 1 < NG:
                            max1(g + 1, c, 0)
                            max1(g + 1, c, 1)
                        if g == 1 and c == 0:
                            pe.wait_ge(S["p_xT_sb"], 1)
                        elif g == 1 and c == 1:
                            ctx_evacuated()
                        elif g == 2 and c == 1:
                            x_evacuated()
                        st1(g, c)
                        if g == NG - 1:
                            if c == 0:
                                stacked()
                            max_next(c)
                    if g + 1 < NG:
                        if g >= 1:
                            pe.wait_ge(S["sum_sb"], g)
                        turn_max(NG + g + 1, G)
                    av1(g)
                    if g == 0:
                        project_ctx()
                    elif g == 1:
                        project_x()
                for j in range(H // 2):
                    if j == H // 2 - 2:
                        pe.wait_ge(S["sum_sb"], NG)
                        for i in range(2):
                            last = mm(PS[:, STB, i * T:(i + 1) * T], pick_sum[:, i, :], rsum[:, :])
                        last.then_inc(S["r_ps"], 1)
                        turn_next()
                        pe.wait_ge(S["un_last"], 1)
                    elif j % 2 == 0:
                        pe.wait_ge(S["un_ok"], j // 2 + 1)
                    last = mm(PS[:, STB + 2, 0:T], Ball[:, j, :], U[:, j, :], start=(j == 0), stop=(j == H // 2 - 1))
                last.then_inc(S["o1_ps"], 1)
                pe.wait_ge(S["o1_sb"], 1)
                for t in range(QT):
                    last = pe.transpose(PS[:, STB + 3, t * P:(t + 1) * P], oT[:, t * P:(t + 1) * P], ident[:, :])
                last.then_inc(S["o1T_ps"], 1)
                end_of_batch(pe, "pe")

            pe.wait_ge(TS["t_xm"], 1)
            for t in range(TILES):
                last = pe.transpose(PS[:, t // 4, (t % 4) * P:(t % 4 + 1) * P], xm[:, t, :], ident[:, :])
                if t % 4 == 3:
                    last.then_inc(TS["t_xT"], 1)
            pe.wait_ge(TS["t_xTsb"], 2)
            for t in range(TILES):
                last = mm(PS[:, 2, t * E:(t + 1) * E], xmT[:, t * P:(t + 1) * P], gwT)
            last.then_inc(TS["t_lg"], 1)
            pe.wait_ge(TS["t_oh"], 1)
            rank = PS[:, 3, 0:TILES * E].rearrange("p (t e) -> p t e", e=E)
            mm(rank, tri[:, :], oh[:, :, :], stop=False)
            for t in range(TILES - 1):
                w = TILES - 1 - t
                last = mm(rank[:, t + 1:TILES, :], onesb[:, :], oh[:, t, :].unsqueeze(1).broadcast_to([P, w, E]),
                          start=False, stop=(t == TILES - 2))
            last.then_inc(TS["t_rk"], 1)
            pe.wait_ge(TS["t_xd"], 16)
            for t in range(ST):
                last = pe.transpose(PS[:, 4 + t // 4, (t % 4) * P:(t % 4 + 1) * P], XD[:, t, :], ident[:, :])
                if t % 4 == 3 or t == ST - 1:
                    last.then_inc(TS["t_dT"], 1)
            pe.wait_ge(TS["t_dTsb"], 3)
            pe.wait_ge(TS["t_slot"], 1)

            def up(e):
                if e >= 2:
                    pe.wait_ge(TS["t_g"], e - 1)
                pe.wait_ge(s_w1, 16 * (e + 1))
                for f in range(FT):
                    last = mm(PS[:, e % 2, f * CAP:(f + 1) * CAP], w1_all[:, e, f * P:(f + 1) * P],
                              XT[:, e * CAP:(e + 1) * CAP])
                last.then_inc(TS["t_h"], 1)

            def down(e):
                pe.wait_ge(TS["t_w2"], 16 * (e + 1))
                pe.wait_ge(TS["t_g"], e + 1)
                q = e // 4
                if q >= 2 and e % 4 == 0:
                    pe.wait_ge(TS["t_ysb"], q - 1)
                for f in range(FT):
                    last = mm(PS[0:CAP, 2 + q % 2, (e % 4) * C:(e % 4 + 1) * C], hT[:, e % 2, f, :], w2_all[:, e, f, :],
                              start=(f == 0), stop=(f == FT - 1))
                last.then_inc(TS["t_y"], 1)
            up(0)
            for e in range(E):
                if e + 1 < E:
                    up(e + 1)
                down(e)

        @block.vector
        def _(dve):
            dve.memset(zrow, 0.0).then_inc(s_zrow, 1)
            setup = Chain(dve, s_setup)
            setup(dve.memset(KC[:, :, :].bitcast(F32), 0.0))
            link = Chain(dve, S["dchain"])

            def center(src, link):
                for t in range(QT):
                    i = dve.bn_stats(stats[:, t, :], src(t))
                link(i)
                for t in range(QT):
                    i = dve.bn_aggr(mv[:, t, :], stats[:, t, :])
                link(i)
                return dve.tensor_scalar(ve[:, 0:QT], mv[:, 0:QT, 1], EPS, None, ALU.add)

            def scaled(src, dst):
                for t in range(QT):
                    i = dve.tensor_scalar(dst[:, t, :], src(t), mv[:, t, 0:1], rstd[:, t:t + 1], ALU.subtract, ALU.mult)
                return i

            def center_next(src, link):
                center(src, link).then_inc(S["p_var"], 1)

            def norm_next(src):
                dve.wait_ge(S["p_rstd"], 1)
                scaled(src, xn).then_inc(S["p_xn"], 1)

            def low(n):
                bank, at, off, w, bias = SPLIT[n]
                if n == 1:
                    dve.wait_ge(S["cparts_out"], 32)
                dve.wait_ge(S["split_hi"], (1, 3, 3, 4)[n])
                dve.scalar_tensor_tensor(out=lo[:, off:off + w], in0=PS[:, bank, at:at + w], scalar=b0_sb[:, bias:bias + 1],
                                         in1=hi[:, off:off + w], op0=ALU.add, op1=ALU.subtract).then_inc(S["split_lo"], 1)

            def ctx_next():
                dve.wait_ge(S["p_xT_ps"], 1)
                dve.tensor_copy(xnT[:, :], PS[:, 2, 0:T]).then_inc(S["p_xT_sb"], 1)
                dve.wait_ge(S["ctx_ps"], 2)
                dve.tensor_copy(Vc[:, :, :, 0:D0], PS[:, 5, :].rearrange("p (k h d) -> p k h d", k=KT, h=H)
                                ).then_inc(S["v_sb"], 1)
                low(0)

            def x_next():
                for n in (1, 2, 3):
                    low(n)
                dve.wait_ge(S["proj_ps"], 4)
                dve.tensor_copy(Vs[:, :, :, 0:D0], PS[:, 5, T:2 * T].rearrange("p (k h d) -> p k h d", k=QT, h=H)
                                ).then_inc(S["v_sb"], 1)

            def take_max(n, g, reduces, name="mx"):
                dve.wait_ge(S[name + "_ps"], n + 1)
                for (a, e), t, col in reduces:
                    i = dve.tensor_reduce(rmax[:, g % 2, t, col:col + 1], PS[:, MX + n % 2, a:e], X, ALU.max)
                i.then_inc(S[name + "_ok"], 1)

            def maxima0(g, c, name, n0):
                n = n0 + 3 * c
                take_max(n, g, [((0, P), 0, c), ((T, 2 * T), 1, c)], name)
                for t in range(QT):
                    take_max(n + 1 + t, g, [((0, TC), t, G + c)], name)

            def first(t):
                return x_all[:, t, :]
            dve.wait_ge(s_x, 16)
            center_next(first, link)
            setup(dve.memset(QS[:, :, :].bitcast(F32), 0.0))
            dve.drain().then_inc(s_dve_zero, 1)
            norm_next(first)
            dve.wait_ge(s_cols, 16)
            ctx_next()
            setup(dve.memset(K2[:, :].bitcast(F32), 0.0))
            dve.memset(K2[ONE1:ONE1 + G, :].bitcast(F32), 1.0)
            dve.memset(PS[:, AV, :], 0.0)
            dve.memset(Vs[:, :, :, D0:DV], 1.0)
            dve.memset(Vc[:, :, :, D0:DV], 1.0)
            x_next()
            dve.memset(onesb[:, :], 1.0)
            dve.memset(ones32[:, :], 1.0)
            dve.wait_ge(s_fcq, 32)
            dve.scalar_tensor_tensor(out=fc1[:, :], in0=fcq[:, 0, :], scalar=-128.0, in1=fcs[:, 0, :], op0=ALU.add, op1=ALU.mult)
            dve.scalar_tensor_tensor(out=fc2[:, :, :].rearrange("p f c -> p (f c)"), in0=fcq[:, 1, :], scalar=-128.0,
                                     in1=fcs[:, 1, :], op0=ALU.add, op1=ALU.mult)
            dve.tensor_scalar(fc1bh[:, :], fc1b, 0.5, None, ALU.mult)
            dve.wait_ge(s_tanh, 1)
            dve.tensor_scalar(fc2bh, fc2bh, 0.5, None, ALU.mult)
            dve.tensor_tensor(bvsum[:, :], bv_sb[:, 0:1], bv_sb[:, 1:2], ALU.add)
            for c in range(G):
                maxima0(0, c, "pmx", 0)
            end_of_batch(dve, "dve")
            with dve.Fori(0, B) as b:
                link = Chain(dve, S["dchain"])
                count = {"var": 0}

                def norm(src, dst, last=None):
                    center(lambda t: src[:, t, :], link).then_inc(S["var"], 1)
                    count["var"] += 1
                    dve.wait_ge(S["rstd_ok"], count["var"])
                    i = scaled(lambda t: src[:, t, :], dst)
                    if last:
                        i.then_inc(S[last], 1)
                    else:
                        link(i)

                def x_next_tile(t):
                    return x_all[:, bass.ds((b * QT + QT) % TILES + t, 1), :].rearrange("p o c -> p (o c)")

                dve.wait_ge(S["kk_hi"], 2)
                dve.tensor_tensor(K1[CC:P, :], cT[CC:P, :], K1[CC:P, :], ALU.subtract).then_inc(S["kk_lo"], 1)

                def max0(g):
                    if g >= 3:
                        dve.wait_ge(S["mt_ps"], g - 2)
                    for c in range(G):
                        maxima0(g, c, "mx", 12 * (g - 1))
                        if c == 1 and g >= 2:
                            out0(g - 2)

                def evac0(g):
                    dve.wait_ge(S["av_ps"], g + 1)
                    if g >= 1:
                        dve.wait_ge(S["ot_ps"], g)
                    dve.tensor_copy(OT[:, :], PS[:, AV, :]).then_inc(S["av_sb"], 1)

                def out0(g):
                    dve.wait_ge(S["ot_ps"], g + 1)
                    o = PS[:, MISC, :].rearrange("p (j c d) -> p j c d", j=2 * QT, c=G)
                    link(dve.reciprocal(rc0[:, :, :], o[:, :, :, D0]))
                    i = dve.tensor_tensor(yn[:, :, :, :], o[:, :, :, 0:D0],
                                          rc0[:, :, :].unsqueeze(3).broadcast_to([P, 2 * QT, G, D0]), ALU.mult)
                    i.then_inc(S["ot_sb"], 1)
                    dve.wait_ge(S["ot_sb"], g + 1)
                    dve.tensor_tensor(y[:, :, :].rearrange("p t (h d) -> p t h d", h=H)[:, :, G * g:G * g + G, :],
                                      yn[:, 0:QT, :, :], yn[:, QT:2 * QT, :, :], ALU.add).then_inc(S["y_ok"], 1)
                for g in range(NG):
                    if g + 1 < NG:
                        max0(g + 1)
                    elif g >= 1:
                        out0(g - 1)
                    evac0(g)
                out0(NG - 1)
                dve.wait_ge(S["xT_ps"], 1)
                dve.tensor_scalar(yT[:, :], PS[:, MISC, 0:T], bvsum[:, :], None, ALU.add).then_inc(S["xT_sb"], 1)
                dve.wait_ge(S["o_ps"], 1)
                o = PS[:, MX, 0:T].rearrange("p (t c) -> p t c", t=QT)
                link(dve.tensor_tensor(tmp[:, :, :], o, bp_sb.unsqueeze(1).broadcast_to([P, QT, C]), ALU.add))
                link(dve.scalar_tensor_tensor(out=x1[:, :, :], in0=tmp[:, :, :], scalar=tg[:, 0:1],
                                              in1=x_all[:, bass.ds(b * QT, QT), :],
                                              op0=ALU.mult, op1=ALU.add))
                norm(x1, xn1)
                norm(xn1, xn, "xn_ok")
                dve.wait_ge(S["xT_ps"], 2)
                dve.tensor_scalar(xnT[:, :], PS[:, MISC, 0:T], gb_sb[:, 0:1], gb_sb[:, 1:2], ALU.mult, ALU.add
                                  ).then_inc(S["xT_sb"], 1)
                for f in range(FT):
                    dve.wait_ge(S["h_ok"], f + 1)
                    dve.scalar_tensor_tensor(out=sT[:, f, :], in0=th[:, f, :], scalar=1.0, in1=fh[:, f, :],
                                             op0=ALU.add, op1=ALU.mult).then_inc(S["s_ok"], 1)
                dve.wait_ge(S["z_ps"], 1)
                z = PS[:, MX:MX + QT, 0:C]
                link(dve.scalar_tensor_tensor(out=tmp[:, :, :], in0=z, scalar=0.25, in1=xn1[:, :, :], op0=ALU.mult, op1=ALU.add))
                link(dve.tensor_tensor(tmp[:, :, :], tmp[:, :, :], fc2bh.unsqueeze(1).broadcast_to([P, QT, C]), ALU.add))
                link(dve.scalar_tensor_tensor(out=x1[:, :, :], in0=tmp[:, :, :], scalar=tg[:, 2:3], in1=x1[:, :, :],
                                              op0=ALU.mult, op1=ALU.add))
                norm(x1, xn, "xn_ok")
                dve.wait_ge(S["xT_ps"], 3)
                dve.tensor_copy(xnT[:, :], PS[:, MISC, 0:T]).then_inc(S["xT_sb"], 1)
                def low_heads(n):
                    dve.wait_ge(S["qh_ok"], n + 1)
                    dve.tensor_tensor(QL[0:CC, 2 * n:2 * n + 2, :],
                                      PS[0:CC, STB + n % 6, :].rearrange("p (a b) -> p a b", a=2),
                                      QH[0:CC, 2 * n:2 * n + 2, :], ALU.subtract).then_inc(S["ql_ok"], 1)

                def max1(g):
                    if g >= 2:
                        dve.wait_ge(S["mt_ps"], NG + g - 2)
                    for c in range(G):
                        for t in range(QT):
                            n = 2 * (G * g + c) + t
                            take_max(12 * (NG - 1) + n, g, [((0, TC), t, c)])
                        if g == 0:
                            low_heads(2 + c)
                        elif g == 1 and c == 0:
                            norm_next(x_next_tile)

                def evac1(g):
                    dve.wait_ge(S["av_ps"], NG + g + 1)
                    dve.tensor_copy(U[:, 2 * g:2 * g + 2, :].rearrange("p a b -> p (a b)"), PS[:, AV, :]
                                    ).then_inc(S["av_sb"], 1)
                    if g >= 1:
                        dve.wait_ge(S["rinv_out"], 16 * g)
                    dve.reciprocal(rsum[:, :], PS[:, MISC, T:2 * T]).then_inc(S["sum_sb"], 1)
                low_heads(0)
                low_heads(1)
                max1(0)
                low_heads(6)
                low_heads(7)
                center_next(x_next_tile, link)
                for g in range(NG):
                    if g + 1 < NG:
                        max1(g + 1)
                    else:
                        dve.wait_ge(S["mt_ps"], 2 * NG - 2)
                        for c in range(G):
                            maxima0(0, c, "pmx", 0)
                    evac1(g)
                    if g == 0:
                        ctx_next()
                    elif g == 1:
                        x_next()
                dve.wait_ge(S["r_ps"], 1)
                u = U[:, H // 2 - 2:H // 2, :].rearrange("p a b -> p (a b)")
                dve.tensor_tensor(u, u, PS[:, STB, :], ALU.mult).then_inc(S["un_last"], 1)
                dve.wait_ge(S["o1_ps"], 1)
                dve.tensor_scalar(oT[:, :], PS[:, STB + 2, 0:T], bo_sb, tg[:, 1:2], ALU.add, ALU.mult).then_inc(S["o1_sb"], 1)
                dve.wait_ge(S["o1T_ps"], 1)
                dve.tensor_tensor(x_all[:, bass.ds(b * QT, QT), :],
                                  PS[:, STB + 3, 0:T].rearrange("p (t c) -> p t c", t=QT), x1[:, :, :], ALU.add)
                end_of_batch(dve, "dve")

            link = Chain(dve, TS["t_chain"])
            for t in range(TILES):
                i = dve.bn_stats(stats[:, t, :], x_all[:, t, :])
            link(i)
            for t in range(TILES):
                i = dve.bn_aggr(mv[:, t, :], stats[:, t, :])
            link(i)
            dve.tensor_scalar(ve[:, :], mv[:, :, 1], EPS, None, ALU.add).then_inc(TS["t_var"], 1)
            dve.wait_ge(TS["t_rstd"], 1)
            for t in range(TILES):
                i = dve.tensor_scalar(xm[:, t, :], x_all[:, t, :], mv[:, t, 0:1], rstd[:, t:t + 1], ALU.subtract, ALU.mult)
            i.then_inc(TS["t_xm"], 1)
            for j in range(2):
                dve.wait_ge(TS["t_xT"], j + 1)
                dve.tensor_copy(xmT[:, 512 * j:512 * j + 512], PS[:, j, :]).then_inc(TS["t_xTsb"], 1)
            dve.wait_ge(TS["t_lg"], 1)
            lg = PS[:, 2, 0:TILES * E].rearrange("p (t e) -> p t e", e=E)

            def over_e(a):
                return a[:, :].unsqueeze(2).broadcast_to([P, TILES, E])
            iota3 = iota_e[:, :].unsqueeze(1).broadcast_to([P, TILES, E])
            link(dve.tensor_reduce(lmax[:, :], lg, X, ALU.max))
            dve.tensor_tensor(eq[:, :, :], lg, over_e(lmax), ALU.subtract).then_inc(TS["t_lm"], 1)
            dve.wait_ge(TS["t_lm"], 1)
            link(dve.tensor_scalar(pick[:, :, :], eq[:, :, :], 0.0, None, ALU.is_ge))
            link(dve.tensor_tensor(pick[:, :, :], pick[:, :, :], iota3, ALU.mult))
            link(dve.tensor_reduce(arg[:, :], pick[:, :, :], X, ALU.min))
            dve.tensor_tensor(oh[:, :, :], over_e(arg), iota3, ALU.is_equal).then_inc(TS["t_oh"], 1)
            dve.wait_ge(TS["t_ex"], 1)
            link(dve.reduce_sum(exs[:, :], ex[:, :, :], X))
            link(dve.reciprocal(wgt[:, :], exs[:, :]))
            link(dve.tensor_scalar(wgt[:, :], wgt[:, :], tg[:, 3:4], None, ALU.mult))
            dve.wait_ge(TS["t_oh"], 1)
            dve.wait_ge(TS["t_rk"], 1)
            link(dve.tensor_tensor(ex[:, :, :], PS[:, 3, 0:TILES * E].rearrange("p (t e) -> p t e", e=E), oh[:, :, :], ALU.mult))
            link(dve.reduce_sum(rk[:, :], ex[:, :, :], X))
            link(dve.tensor_scalar(drop[:, :], rk[:, :], float(CAP), FAR, ALU.is_gt, ALU.mult))
            link(dve.scalar_tensor_tensor(out=slot[:, :], in0=arg[:, :], scalar=float(CAP), in1=rk[:, :], op0=ALU.mult, op1=ALU.add))
            link(dve.tensor_scalar(slot[:, :], slot[:, :], float(E * CAP - 1), None, ALU.add))
            dve.tensor_tensor(slot_i[:, :], slot[:, :], drop[:, :], ALU.add).then_inc(TS["t_slot"], 1)
            for j in range(3):
                w = min(512, SLOTS - 512 * j)
                dve.wait_ge(TS["t_dT"], j + 1)
                dve.tensor_copy(XT[:, 512 * j:512 * j + w], PS[:, 4 + j, 0:w]).then_inc(TS["t_dTsb"], 1)
            for q in range(E // 4):
                dve.wait_ge(TS["t_y"], 4 * q + 4)
                dve.tensor_copy(YB[:, 4 * q:4 * q + 4, :].rearrange("p e c -> p (e c)"), PS[0:CAP, 2 + q % 2, :]
                                ).then_inc(TS["t_ysb"], 1)
            dve.wait_ge(TS["t_sc"], 16 * TILES)
            for t in range(TILES):
                dve.wait_ge(s_back[t], 16)
                dve.scalar_tensor_tensor(out=xm[:, t, :], in0=Yg[:, t, :], scalar=wgt[:, t:t + 1], in1=x_all[:, t, :],
                                         op0=ALU.mult, op1=ALU.add).then_inc(TS["t_out"], 1)


_OUT = (B, T, C)


def kernel(**inputs):
    import numpy as np
    import concourse.bacc as bacc
    from concourse.bass_utils import run_bass_kernel_spmd

    a = {k: np.asarray(v) for k, v in inputs.items()}
    pre = "L0_xattn_"
    f32 = np.float32

    def heads(w):
        return w.reshape(w.shape[0], H, D1).transpose(2, 1, 0)

    w0 = np.zeros((P, 7, C), f32)
    for j, n in enumerate(("Wq", "Wk", "Wcq", "Wv", "Wck", "Wcv", "Wp")):
        w = a[pre + n]
        w0[:w.shape[0], j] = w
    columns = [a[pre + n] for n in ("bq", "bk", "bcq", "bck", "bv", "bcv")]
    columns += [a["L0_ffn_ln_gamma"], a["L0_ffn_ln_beta"], a["L1_xattn_bo"]]
    columns += [*a["L0_ffn_fc1_bias"].reshape(FT, P), *a["L1_ffn_gate_w"]]
    rows = [a[pre + "bp"], a["L0_ffn_fc2_bias"], a["g_xattn"], a["g_ffn"],
            a["L0_ffn_fc1_scales"].reshape(-1), a["L0_ffn_fc2_scales"].reshape(-1)]
    arrays = {
        "x": a["x"], "ctx": a["ctx_512"], "ctxT": np.ascontiguousarray(a["ctx_512"].transpose(0, 2, 1)),
        "w0": w0, "columns": np.stack(columns, axis=1), "rows": np.concatenate(rows),
        "fc_q": np.stack([a["L0_ffn_fc1_q"], a["L0_ffn_fc2_q"].reshape(FT, P, C).transpose(1, 0, 2).reshape(P, FF)], axis=1),
        "heads_w": np.concatenate([heads(a["L1_xattn_Wq"]), a["L1_xattn_Wo"].reshape(H, D1, C).transpose(1, 0, 2),
                                   heads(a["L1_xattn_Wk"]), heads(a["L1_xattn_Wv"])], axis=2),
        "w1": a["L1_ffn_w1"], "w2": a["L1_ffn_w2"],
    }
    nc = bacc.Bacc("TRN2", target_bir_lowering=False, num_devices=1)
    t = {}
    for name, v in arrays.items():
        t[name] = nc.dram_tensor(f"in_{name}", v.shape, mybir.dt.from_np(v.dtype), kind="ExternalInput").ap()
    out = nc.dram_tensor("out_x", _OUT, F32, kind="ExternalOutput").ap()
    build(nc, *(t[n] for n in arrays), out)
    r = run_bass_kernel_spmd(nc, [{f"in_{k}": v for k, v in arrays.items()}], core_ids=[0])
    return r.results[0]["out_x"]
```

```python
from contextlib import ExitStack

import concourse.bass as bass
from concourse import mybir

F32 = mybir.dt.float32
F32R = mybir.dt.float32r
BF16 = mybir.dt.bfloat16
I32 = mybir.dt.int32
U32 = mybir.dt.uint32
ALU = mybir.AluOpType
ACT = mybir.ActivationFunctionType
X = mybir.AxisListType.X

P = 128
B, T, C = 4, 256, 128
TC, CC = 512, 64
QT, KT = T // P, TC // P
H, D0, D1 = 16, 8, 64
G = 4
NG = H // G
FF = 512
FT = FF // P
E = 16
TILES = B * QT
CAP = int(1.25 * B * T / E)
CAP += CAP % 2
SLOTS = E * CAP
ST = SLOTS // P
EPS = 1e-5
NEG = -1e30
FAR = 1e6
SCALE0 = D0 ** -0.5
SCALE1 = D1 ** -0.5
ROWS = 96
ONE0 = ROWS
END0 = ONE0 + 2 * G
ONE1 = 64
DV = D0 + 1
KEEP_WARM = 8
KEEP_WARM_TAIL = 36


class Chain:

    def __init__(self, eng, sem):
        self.eng, self.sem, self.n = eng, sem, 0

    def __call__(self, ins):
        self.n += 1
        ins.then_inc(self.sem, 1)
        self.eng.wait_ge(self.sem, self.n)


def build(nc, x, ctx, ctxT, w0, columns, rows, fc_q, heads_w, w1, w2, out):
    place = [(nc.sbuf_base + 31) // 32 * 32]

    def sb(name, shape, dt=F32, at=None):
        size = 2 if dt == BF16 else 4
        for n in shape[1:]:
            size *= n
        offset = place[0] if at is None else at
        if at is None:
            place[0] += (size + 31) // 32 * 32
        return nc.alloc_sbuf_tensor_at(name, shape, dt, offset=offset)

    with ExitStack() as stack:
        def sem(name):
            return stack.enter_context(nc.semaphore(name))

        Aall = sb("Aall", [P, H, P])
        Ball = sb("Ball", [P, H // 2, P])
        w0_sb = sb("w0_sb", [P, 7, C])
        cols = sb("cols", [P, 9 + FT + E])
        b0_sb, bv_sb, gb_sb, bo_sb = cols[:, 0:4], cols[:, 4:6], cols[:, 6:8], cols[:, 8:9]
        fc1b, gwT = cols[:, 9:9 + FT], cols[:, 9 + FT:9 + FT + E]
        bcast = sb("bcast", [P, 2 * C + 4])
        bp_sb, fc2bh, gates = bcast[:, 0:C], bcast[:, C:2 * C], bcast[:, 2 * C:2 * C + 4]
        bvsum = sb("bvsum", [P, 1])
        fc1 = sb("fc1", [P, FF])
        fc2 = sb("fc2", [P, FT, C])
        fc1bh = sb("fc1bh", [P, FT])
        tg = sb("tg", [P, 4])
        ident = sb("ident", [P, P])
        identb = sb("identb", [P, P], BF16)
        causal = sb("causal", [P, P], BF16)
        tri = sb("tri", [P, P], BF16)
        pick_sum = sb("pick_sum", [P, 2, P])
        onesb = sb("onesb", [P, P], BF16)
        ones32 = sb("ones32", [P, 32])
        nd = sb("nd", [P, 2 * G])
        mhalf = sb("mhalf", [P, TILES])
        iota_i = sb("iota_i", [P, E], I32)
        iota_e = sb("iota_e", [P, E])
        x_all = sb("x_all", [P, TILES, C])

        KC_at = place[0]
        KC = sb("KC", [P, H, TC], F32R)
        KS_at = place[0]
        KS = sb("KS", [P, H, T], F32R)
        QS_at = place[0]
        assert QS_at - KC_at == 4 * H * (TC + T)
        QS = sb("QS", [P, H, T], F32R)
        QC = sb("QC", [P, H, T], F32R)
        QH_at = place[0]
        QH = sb("QH", [P, H, T], F32R)
        QL = sb("QL", [ROWS, H, T], F32R)
        w2_all = sb("w2_all", [P, E, FT, C], at=QS_at)

        Pc_at = place[0]
        Pc = sb("Pc", [P, G, KT * T])
        Ps_at = place[0]
        Ps = sb("Ps", [P, G, 3 * P])
        w1_all = sb("w1_all", [P, E, FF], at=KC_at)
        heads_sb = sb("heads_sb", [D1, H, 2 * C + 2 * CC], at=Pc_at)
        wqT_sb, wo_sb = heads_sb[:, :, 0:C], heads_sb[:, :, C:2 * C]
        wkT_sb, wvT_sb = heads_sb[:, :, 2 * C:2 * C + CC], heads_sb[:, :, 2 * C + CC:2 * C + 2 * CC]
        U = sb("U", [P, H // 2, T], at=Ps_at)
        place[0] = max(place[0], Ps_at + 4 * H // 2 * T)
        th = sb("th", [P, FT, T])
        fh = sb("fh", [P, FT, T])
        fcq = sb("fcq", [P, 2, FF], I32, at=QH_at)
        fcs = sb("fcs", [P, 2, FF], at=QH_at + 8 * FF)

        ctx_sb = sb("ctx_sb", [P, KT, CC])
        cT = sb("cT", [P, TC])
        K1 = sb("K1", [P, TC], F32R)
        K2 = sb("K2", [ROWS, TC], F32R)
        Vs = sb("Vs", [P, QT, H, DV])
        Vc = sb("Vc", [P, KT, H, DV])
        xn = sb("xn", [P, QT, C])
        xnT = sb("xnT", [P, T])
        xn_next = sb("xn_next", [P, QT, C])
        xnT_next = sb("xnT_next", [P, T])
        y = sb("y", [P, QT, C])
        xn1 = sb("xn1", [P, QT, C])
        tmp = sb("tmp", [P, QT, C])
        hi = sb("hi", [P, 3 * T], F32R)
        lo = sb("lo", [P, 3 * T], F32R)
        x1 = sb("x1", [P, QT, C])
        rmax = sb("rmax", [P, 2, QT, 2 * G])
        rmax1 = sb("rmax1", [P, 2, QT, G])
        OT_at = place[0]
        OT = sb("OT", [P, 2 * T])
        rc0 = sb("rc0", [P, 2 * QT, G])
        yn = sb("yn", [P, 2 * QT, G, D0])
        yT = sb("yT", [P, T])
        R = sb("R", [P, 2, 2, T], at=OT_at)
        place[0] = max(place[0], OT_at + 16 * T)
        rsum = sb("rsum", [P, T])
        Pz = sb("Pz", [P, G, T])
        Pz2_at = place[0]
        Pz2 = sb("Pz2", [P, 2, T])
        oT = sb("oT", [P, T], at=Pz2_at)
        stats = sb("stats", [P, TILES, 6])
        mv = sb("mv", [P, TILES, 2])
        ve = sb("ve", [P, TILES])
        rstd = sb("rstd", [P, TILES])

        at = {"routing": KS_at, "experts": QH_at}
        ends = {"routing": QS_at, "experts": Pc_at}

        def late(name, shape, dt=F32, area="routing"):
            t = sb(name, shape, dt, at=at[area])
            n = 4 if dt != BF16 else 2
            for k in shape[1:]:
                n *= k
            at[area] += (n + 31) // 32 * 32
            assert at[area] <= ends[area]
            return t
        xm = late("xm", [P, TILES, C])
        xmT = late("xmT", [P, TILES * P])
        XD = late("XD", [P, ST, C], area="experts")
        XT = late("XT", [P, SLOTS], area="experts")
        hT = late("hT", [P, 2, FT, CAP], area="experts")
        YB = late("YB", [CAP, E, C], area="experts")
        Yg = late("Yg", [P, TILES, C], area="experts")
        lmax = late("lmax", [P, TILES])
        eq = late("eq", [P, TILES, E])
        arg = late("arg", [P, TILES])
        pick = late("pick", [P, TILES, E])
        oh = late("oh", [P, TILES, E], BF16)
        ex = late("ex", [P, TILES, E])
        rko = late("rko", [P, TILES, E])
        exs = late("exs", [P, TILES])
        wgt = late("wgt", [P, TILES])
        rk = late("rk", [P, TILES])
        drop = late("drop", [P, TILES])
        slot = late("slot", [P, TILES])
        slot_i = late("slot_i", [P, TILES], U32)
        assert place[0] <= nc.sbuf_usable_end, (place[0], nc.sbuf_usable_end)

        zrow = x1[:, 0, :]
        PS = stack.enter_context(nc.psum_tensor("PS", [P, 8, 512], F32))
        MX, STB, AV, MISC = 0, 2, 6, 7
        x_slots = nc.dram_tensor("x_slots", (SLOTS, C), F32)
        ctx_parts = nc.dram_tensor("ctx_parts", (2, P, TC), F32)
        x_parts = nc.dram_tensor("x_parts", (2, P, 3 * T), F32)
        r_dram = nc.dram_tensor("r_dram", (2, G, T), F32)
        y_slots = nc.dram_tensor("y_slots", (SLOTS, C), F32)

        s_x = sem("s_x")
        s_w0 = sem("s_w0")
        s_cols = sem("s_cols")
        s_rows = sem("s_rows")
        s_fcq = sem("s_fcq")
        s_heads = sem("s_heads")
        s_w1 = sem("s_w1")
        s_pool0 = sem("s_pool0")
        s_zrow = sem("s_zrow")
        s_zslots = sem("s_zslots")
        s_dve_zero = sem("s_dve_zero")
        s_pool_zero = sem("s_pool_zero")
        s_ones = sem("s_ones")
        s_picks = sem("s_picks")
        s_ab = sem("s_ab")
        s_ab_sb = sem("s_ab_sb")
        s_tanh = sem("s_tanh")
        s_setup = sem("s_setup")
        s_const = sem("s_const")
        arrived = sem("arrived")
        released = {k: sem(f"released_{k}") for k in ("pe", "act", "dve", "sp")}
        start = ("cT_in p_var p_rstd p_xn p_xT_ps p_xT_sb ctx_ps proj_ps v_sb split_hi split_lo cparts_out parts_out "
                 "q_in k_in c_in pmx_ps pmx_ok pmt_ps pmt_sb dchain").split()
        early = ("ctx_in cT_in self_ok masked mx_ps mx_ok mt_ps mt_sb st_ps exp_ok av_ps av_sb ot_ps ot_sb y_ok "
                 "xT_ps xT_sb o_ps o_sb var rstd_ok xn_ok f_ps h_ok s_ok z_ps z_sb p_var p_rstd p_xn p_xT_ps p_xT_sb "
                 "ctx_ps proj_ps v_sb split_hi split_lo cparts_out parts_out").split()
        middle = ("pz_half pz_ok cT_back kk_hi kk_lo m1_ps m1_ok t1_ps t1_sb s1_ps e1_ok a1_ps a1_sb pmx_ps pmx_ok sum_sb rinv_out "
                  "rinv_in0 rinv_in1 r_ps un_ok un_last").split()
        final = ("q_in k_in c_in pmt_ps pmt_sb pm1_ps pm1_ok pt1_ps pt1_sb q1_ps qh_ok ql_ok o1_ps o1_sb o1T_ps "
                 "dchain").split()
        names = early + middle + final
        batch0 = [s for s in names if s not in "pz_half pz_ok ctx_in m1_ps m1_ok t1_ps t1_sb s1_ps e1_ok a1_ps a1_sb sum_sb rinv_out "
                  "rinv_in0 rinv_in1 r_ps un_ok un_last o1_ps o1_sb o1T_ps".split()]
        S = {n: sem(n) for n in names}
        t_names = ("t_var t_rstd t_xm t_xT t_xTsb t_lg t_d t_lm t_ex t_oh t_rk t_slot t_sc t_xd t_dT t_dTsb t_h t_g "
                   "t_y t_ysb t_yw t_w2 t_out t_yzero t_chain").split()
        TS = {n: sem(n) for n in t_names}
        s_back = [sem(f"s_back{t}") for t in range(TILES)]

        block = stack.enter_context(nc.Block())

        def keep_warm(pe, n):
            for _ in range(n):
                pe.matmul(PS[:, 4, 0:P], ident[:, :], ident[:, :], start=True, stop=True)

        def end_of_batch(eng, key):
            eng.drain().then_inc(arrived, 1)
            if key == "pe":
                keep_warm(eng, KEEP_WARM)
            eng.wait_ge(released[key], 1)
            eng.sem_clear(released[key])

        def r_rows(sp, g):
            sp.wait_ge(S["sum_sb"], g + 1)
            if g >= 2:
                sp.wait_ge(S[f"rinv_in{g % 2}"], 32 * (g // 2))
            sp.dma_start(r_dram[g % 2], rsum[0:P:32, :]).then_inc(S["rinv_out"], 16)
            sp.wait_ge(S["rinv_out"], 16 * (g + 1))
            if g >= 2:
                sp.wait_ge(S["un_ok"], g - 1)
            for i in range(2):
                sp.dma_start(R[D1 * i:D1 * i + D1, g % 2, :, :], r_dram[g % 2, i:G:2, :].partition_broadcast(D1)
                             ).then_inc(S[f"rinv_in{g % 2}"], 16)

        AB_BANKS = (0, 1, 4, 7, 0, 1)
        SPLIT = ((4, 0, 0, TC, 3), (2, 0, 0, T, 0), (2, T, T, T, 1), (3, 0, 2 * T, T, 2))
        PAIR_BANKS = (2, 3, 6)

        def st1_bank(n, mlp):
            return STB + 2 * ((n + (mlp and n > 5)) % 2)
        MLP_BANK = STB
        ROUTES = ((0, TILES - QT, (0, 1), 0, 1), (TILES - QT, TILES, (0,), 2, 3))
        DIVIDE_AFTER = ((2, 0), (3, 0), (3, 2))
        MAX1_BESIDE = {(0, 0): [0], (0, 1): [1], (0, 2): [2], (0, 3): [3], (1, 1): [2], (1, 3): [3],
                       (2, 1): [2], (2, 3): [3]}

        @block.sync
        def _(sp):
            for half in range(2):
                sp.dma_start(cT[half * CC:half * CC + CC, :], ctxT[0]).then_inc(S["cT_in"], 16)
            sp.dma_start(x_all[:, :, :], x.rearrange("b (t p) c -> p (b t) c", p=P)).then_inc(s_x, 16)
            sp.dma_start(w0_sb[:, :, :], w0).then_inc(s_w0, 16)
            sp.dma_start(cols[:, :], columns).then_inc(s_cols, 16)
            sp.dma_start(bcast[:, :], rows[0:2 * C + 4].partition_broadcast(P)).then_inc(s_rows, 16)
            sp.dma_start(heads_sb[:, :, :], heads_w).then_inc(s_heads, 16)
            sp.dma_start(fcq[:, :, :], fc_q).then_inc(s_fcq, 16)
            sp.dma_start(fcs[:, :, :].rearrange("p a f -> p (a f)"),
                         rows[2 * C + 4:2 * C + 4 + 2 * FF].partition_broadcast(P)).then_inc(s_fcq, 16)
            sp.wait_ge(s_zrow, 1)
            sp.dma_start(x_slots[:, :].rearrange("(t p) c -> p t c", p=P),
                         zrow.unsqueeze(1).broadcast_to([P, ST, C])).then_inc(s_zslots, 16)

            def load_ctxT(b, s):
                for half in range(2):
                    sp.dma_start(cT[half * CC:half * CC + CC, :], ctxT[bass.ds(b, 1)].rearrange("o c k -> (o c) k")
                                 ).then_inc(S[s], 16)

            def load_ctx(b):
                sp.dma_start(ctx_sb[:, :, :],
                             ctx[bass.ds(b, 1)].rearrange("o (t p) c -> p (o t) c", p=P)).then_inc(S["ctx_in"], 16)

            def stack(dst, src, off, w, parts, s):
                for j, part in enumerate(parts):
                    sp.dma_start(dst[D0 * j:D0 * j + D0, :, :].bitcast(F32),
                                 src[part, :, off:off + w].rearrange("(h d) k -> d h k", d=D0)).then_inc(S[s], 16)

            def stack_ctx():
                sp.wait_ge(S["split_hi"], 1)
                sp.dma_start(ctx_parts[0], hi[:, 0:TC].bitcast(F32)).then_inc(S["cparts_out"], 16)
                sp.wait_ge(S["split_lo"], 1)
                sp.dma_start(ctx_parts[1], lo[:, 0:TC].bitcast(F32)).then_inc(S["cparts_out"], 16)
                sp.wait_ge(S["cparts_out"], 32)
                stack(KC, ctx_parts, 0, TC, (0, 1, 0), "c_in")

            def parts_x():
                sp.wait_ge(S["split_hi"], 4)
                sp.dma_start(x_parts[0], hi[:, :].bitcast(F32)).then_inc(S["parts_out"], 16)
                sp.wait_ge(S["split_lo"], 4)
                sp.dma_start(x_parts[1], lo[:, :].bitcast(F32)).then_inc(S["parts_out"], 16)

            def stack_x():
                sp.wait_ge(S["parts_out"], 32)
                stack(QS, x_parts, 0, T, (0, 0, 1), "q_in")
                stack(KS, x_parts, T, T, (0, 1, 0), "k_in")
                stack(QC, x_parts, 2 * T, T, (0, 0, 1), "c_in")

            def stacked():
                sp.wait_ge(S["q_in"], 48)
                sp.wait_ge(S["k_in"], 48)
                sp.wait_ge(S["c_in"], 96)

            sp.wait_ge(s_dve_zero, 1)
            stack_ctx()
            parts_x()
            sp.wait_ge(s_dve_zero, 2)
            sp.wait_ge(s_pool_zero, 2)
            stack_x()
            stacked()
            sp.wait_ge(s_zslots, 16)
            end_of_batch(sp, "sp")
            load_ctxT(1, "cT_in")
            stack_ctx()
            sp.wait_ge(S["ctx_ps"], 2)
            load_ctxT(0, "cT_back")
            parts_x()
            stack_x()
            stacked()
            end_of_batch(sp, "sp")
            with sp.Fori(0, B - 1) as b:
                load_ctx(b)
                load_ctxT((b + 2) % B, "cT_in")
                stack_ctx()
                sp.wait_ge(S["ctx_ps"], 2)
                load_ctxT(b + 1, "cT_back")
                r_rows(sp, 0)
                parts_x()
                stack_x()
                r_rows(sp, 1)
                r_rows(sp, 2)
                stacked()
                end_of_batch(sp, "sp")
            load_ctx(B - 1)
            for g in range(NG - 1):
                r_rows(sp, g)
            sp.wait_ge(TS["t_sc"], 16 * TILES)
            sp.dma_start(XD[:, :, :], x_slots[:, :].rearrange("(t p) c -> p t c", p=P)).then_inc(TS["t_xd"], 16)
            for q in range(E // 4):
                sp.wait_ge(TS["t_ysb"], q + 1)
                sp.dma_start(y_slots[q * 4 * CAP:(q + 1) * 4 * CAP, :].rearrange("(e s) c -> s e c", s=CAP),
                             YB[:, 4 * q:4 * q + 4, :]).then_inc(TS["t_yw"], 16)
            for t in range(TILES):
                sp.wait_ge(TS["t_out"], t + 1)
                sp.dma_start(out[t // QT, (t % QT) * P:(t % QT + 1) * P, :], xm[:, t, :]).then_inc(TS["t_d"], 16)
            sp.wait_ge(TS["t_d"], 16 * TILES)

        @block.gpsimd
        def _(pool):
            link = Chain(pool, s_pool0)

            def diagonal(t, op, fill, base=0, step=-1, mult=1):
                return pool.affine_select(out=t[:, :], in_=t[:, :], compare_op=op, fill=fill, base=base,
                                          pattern=[[step, P]], channel_multiplier=mult)
            pool.memset(mhalf[:, :], -0.5)
            pool.memset(pick_sum[:, :, :], 0.0)
            link(pool.memset(ident[:, :], 0.0))
            diagonal(ident, ALU.not_equal, 1.0).then_inc(s_ones, 1)
            pool.memset(identb[:, :], 0.0)
            pool.memset(causal[:, :], 0.0)
            pool.memset(nd[:, :], 0.0)
            link(pool.memset(tri[:, :], 1.0))
            diagonal(identb, ALU.not_equal, 1.0)
            diagonal(causal, ALU.is_ge, NEG)
            diagonal(tri, ALU.is_ge, 0.0, step=1, mult=-1)
            pool.affine_select(out=nd[:, :], in_=nd[:, :], compare_op=ALU.not_equal, fill=-1.0, base=0,
                               pattern=[[-1, 2 * G]], channel_multiplier=1)
            link(pool.iota(iota_i[:, :], pattern=[[1, E]], base=-E, channel_multiplier=0))
            pool.tensor_copy(iota_e[:, :], iota_i[:, :])
            for j in range(2):
                for i in range(2):
                    v = pick_sum[:, j, D1 * i:D1 * i + D1]
                    pool.affine_select(out=v, in_=v, compare_op=ALU.not_equal, fill=1.0, base=-32 * (2 * j + i),
                                       pattern=[[0, D1]], channel_multiplier=1)
            pool.memset(KS[:, :, :].bitcast(F32), 0.0).then_inc(s_pool_zero, 1)

            def rsqrt_next():
                pool.wait_ge(S["p_var"], 1)
                pool.tensor_tensor(rstd[:, QT:2 * QT], ve[:, QT:2 * QT], mhalf[:, 0:QT], ALU.pow).then_inc(S["p_rstd"], 1)

            def clear(sems):
                for s in sems:
                    pool.sem_clear(S[s])

            def end_batch(sems):
                pool.drain()
                pool.wait_ge(arrived, 4)
                pool.sem_clear(arrived)
                clear(sems)
                for s in released.values():
                    pool.sem_inc(s, 1)
            rsqrt_next()
            pool.memset(QC[:, :, :].bitcast(F32), 0.0)
            pool.memset(QL[:, :, :].bitcast(F32), 0.0)
            pool.drain().then_inc(s_pool_zero, 1)
            end_batch(start)

            def rsqrt(n):
                pool.wait_ge(S["var"], n)
                pool.tensor_tensor(rstd[:, 0:QT], ve[:, 0:QT], mhalf[:, 0:QT], ALU.pow).then_inc(S["rstd_ok"], 1)

            def causal_weights():
                for g in range(NG):
                    pool.wait_ge(S["self_ok"], 2 * g + 2)
                    for a in (0, 2):
                        v = Ps[:, :, a * P:(a + 1) * P]
                        pool.affine_select(out=v, in_=v, compare_op=ALU.is_ge, fill=0.0, base=0,
                                           pattern=[[0, G], [1, P]], channel_multiplier=-1).then_inc(S["masked"], 1)
                    if g == 2:
                        rsqrt_next()

            def divide(g):
                pool.wait_ge(S[f"rinv_in{g % 2}"], 32 * (g // 2 + 1))
                pool.wait_ge(S["a1_sb"], g + 1)
                u = U[:, 2 * g:2 * g + 2, :]
                pool.tensor_tensor(u, u, R[:, g % 2, :, :], ALU.mult).then_inc(S["un_ok"], 1)
            def sum_tiles(g, c):
                n = G * g + c
                if g >= 1 and c == 0:
                    pool.wait_ge(S["a1_ps"], g)
                if n >= 1:
                    pool.wait_ge(S["pz_ok"], n)
                pool.wait_ge(S["e1_ok"], n + 1)
                pool.tensor_tensor(Pz2[:, :, :].rearrange("p a b -> p (a b)"), Pc[:, c, 0:2 * T], Pc[:, c, 2 * T:4 * T], ALU.add
                                   ).then_inc(S["pz_half"], 1)
                pool.wait_ge(S["pz_half"], n + 1)
                pool.tensor_tensor(Pz[:, c, :], Pz2[:, 0, :], Pz2[:, 1, :], ALU.add).then_inc(S["pz_ok"], 1)

            def route_norm(part):
                t0, t1 = ROUTES[part][0:2]
                pool.wait_ge(TS["t_var"], part + 1)
                pool.tensor_tensor(rstd[:, t0:t1], ve[:, t0:t1], mhalf[:, t0:t1], ALU.pow).then_inc(TS["t_rstd"], 1)

            def scatter(part):
                pool.wait_ge(TS["t_slot"], part + 1)
                for t in range(*ROUTES[part][0:2]):
                    pool.indirect_dma_start(x_slots[:, :], bass.IndirectOffsetOnAxis(slot_i[:, t:t + 1], 0),
                                            xm[:, t, :], None, bounds_check=SLOTS - 1, oob_is_err=False
                                            ).then_inc(TS["t_sc"], 16)

            def attention1(beside):
                for g in range(NG):
                    for c in range(G):
                        if not beside and (g, c) == (1, 0):
                            route_norm(0)
                        sum_tiles(g, c)
                        if beside and (g, c) in ((0, 2), (0, 3), (1, 3)):
                            rsqrt({(0, 2): 1, (0, 3): 2, (1, 3): 3}[g, c])
                        elif (g, c) in DIVIDE_AFTER:
                            divide(DIVIDE_AFTER.index((g, c)))
            causal_weights()
            for n in (1, 2, 3):
                rsqrt(n)
            end_batch(batch0)
            with pool.Fori(0, B - 1) as b:
                causal_weights()
                attention1(True)
                clear(early)
                pool.wait_ge(S["o1_sb"], 1)
                clear(middle)
                end_batch(final)
            attention1(False)
            scatter(0)
            route_norm(1)
            pool.memset(Yg[:, :, :], 0.0).then_inc(TS["t_yzero"], 1)
            scatter(1)
            pool.wait_ge(TS["t_yzero"], 1)
            pool.wait_ge(TS["t_yw"], 16 * (E // 4))
            for t in range(TILES):
                pool.indirect_dma_start(Yg[:, t, :], None, y_slots[:, :],
                                        bass.IndirectOffsetOnAxis(slot_i[:, t:t + 1], 0),
                                        bounds_check=SLOTS - 1, oob_is_err=False).then_inc(s_back[t], 16)

        @block.scalar
        def _(act):
            act.wait_ge(s_rows, 16)
            act.activation(tg[:, :], gates, ACT.Tanh).then_inc(s_tanh, 1)
            act.wait_ge(s_cols, 16)

            def high(n):
                bank, at, off, w, bias = SPLIT[n]
                act.wait_ge(S["ctx_ps"] if n == 0 else S["proj_ps"], (1, 2, 2, 4)[n])
                if n == 1:
                    act.wait_ge(S["cparts_out"], 32)
                act.activation(hi[:, off:off + w], PS[:, bank, at:at + w], ACT.Identity, bias=b0_sb[:, bias:bias + 1]
                               ).then_inc(S["split_hi"], 1)

            def neg_max0(g, turned, n, done):
                act.wait_ge(S[turned], n)
                for q in (QS, QC):
                    act.activation(q[ONE0:END0, G * g:G * g + G, :],
                                   PS[0:2 * G, MISC, 0:T].unsqueeze(1).broadcast_to([2 * G, G, T]), ACT.Copy, scale=-1.0
                                   ).then_inc(S[done], 1)
            for n in range(4):
                high(n)
            for n in range(NG + 2):
                act.wait_ge(s_ab, n + 1)
                dst = Aall[:, G * n:G * n + G, :] if n < NG else Ball[:, G * (n - NG):G * (n - NG) + G, :]
                act.activation(dst.rearrange("p a b -> p (a b)"), PS[:, AB_BANKS[n], :], ACT.Copy).then_inc(s_ab_sb, 1)
            act.wait_ge(s_ones, 1)
            act.wait_ge(s_dve_zero, 1)
            act.wait_ge(s_pool_zero, 1)
            for t, first, w in ((KC, ONE0 + G, TC), (KS, ONE0, T)):
                for g in range(NG):
                    act.activation(t[ONE0:END0, G * g:G * g + G, :],
                                   ident[ONE0:END0, first:first + G].unsqueeze(2).broadcast_to([2 * G, G, w]), ACT.Copy
                                   ).then_inc(s_picks, 1)
            neg_max0(0, "pmt_ps", 1, "pmt_sb")
            end_of_batch(act, "act")

            def attention0():
                for g in range(NG):
                    for u in range(6):
                        n = 6 * g + u
                        act.wait_ge(S["st_ps"], n + 1)
                        bank = STB + 2 * (n % 2)
                        if u in (0, 3):
                            j = 2 * (u // 3)
                            act.activation(Ps[:, j:j + 2, :], PS[:, bank:bank + 2, 0:3 * P], ACT.Exp, scale=SCALE0
                                           ).then_inc(S["self_ok"], 1)
                        else:
                            c = u - 1 if u < 3 else u - 2
                            act.activation(Pc[:, c, :], PS[:, bank:bank + 2, :].rearrange("p a b -> p (a b)"),
                                           ACT.Exp, scale=SCALE0).then_inc(S["exp_ok"], 1)
                    if g + 1 < NG:
                        neg_max0(g + 1, "mt_ps", g + 1, "mt_sb")

            def mlp(bank):
                for f in range(FT):
                    act.wait_ge(S["f_ps"], 2 * (f // 2) + 2)
                    h = PS[:, bank + f // 2, (f % 2) * T:(f % 2 + 1) * T]
                    act.activation(th[:, f, :], h, ACT.Tanh, scale=0.5, bias=fc1bh[:, f:f + 1])
                    act.activation(fh[:, f, :], h, ACT.Identity, bias=fc1b[:, f:f + 1]).then_inc(S["h_ok"], 1)

            def neg_max1(g, turned, n, done):
                act.wait_ge(S[turned], n)
                for c in range(G):
                    act.activation(QL[ONE1:ONE1 + G, G * g + c, :], PS[0:G, MISC, 0:T], ACT.Copy,
                                   scale=nd[0:G, c:c + 1]).then_inc(S[done], 1)

            def attention1(beside):
                for g in range(NG):
                    for c in range(G):
                        n = G * g + c
                        act.wait_ge(S["s1_ps"], n + 1)
                        bank = st1_bank(n, beside)
                        act.activation(Pc[:, c, :], PS[:, bank:bank + 2, :].rearrange("p a b -> p (a b)"),
                                       ACT.Exp, scale=SCALE1).then_inc(S["e1_ok"], 1)
                        if not beside:
                            act.dma_start(w1_all[:, n, :], w1[n]).then_inc(s_w1, 16)
                            act.dma_start(w2_all[:, n, :, :], w2[n].rearrange("(f p) c -> p f c", p=P)
                                          ).then_inc(TS["t_w2"], 16)
                        if beside and n == 5:
                            mlp(MLP_BANK)
                    if g + 1 < NG:
                        neg_max1(g + 1, "t1_ps", g + 1, "t1_sb")
                    if beside and g == 0:
                        high(0)
                    elif beside and g == 1:
                        for n in (1, 2, 3):
                            high(n)

            def next_heads():
                act.wait_ge(S["cT_back"], 32)
                act.activation(K1[:, :], cT[:, :], ACT.Copy).then_inc(S["kk_hi"], 1)
                act.activation(K2[0:CC, :], cT[0:CC, :], ACT.Copy).then_inc(S["kk_hi"], 1)
                for n in range(H // 2):
                    act.wait_ge(S["q1_ps"], n + 1)
                    act.activation(QH[:, 2 * n:2 * n + 2, :], PS[:, PAIR_BANKS[n % 3], :].rearrange("p (a b) -> p a b", a=2),
                                   ACT.Copy).then_inc(S["qh_ok"], 1)
                    if n == 1:
                        neg_max0(0, "pmt_ps", 1, "pmt_sb")
                neg_max1(0, "pt1_ps", 1, "pt1_sb")
            attention0()
            for n in range(4):
                high(n)
            mlp(4)
            next_heads()
            end_of_batch(act, "act")
            with act.Fori(0, B - 1) as b:
                attention0()
                attention1(True)
                next_heads()
                end_of_batch(act, "act")
            attention1(False)
            for part, (t0, t1, _, _, _) in enumerate(ROUTES):
                act.wait_ge(TS["t_lm"], part + 1)
                act.activation(ex[:, t0:t1, :], eq[:, t0:t1, :], ACT.Exp).then_inc(TS["t_ex"], 1)
            act.activation(stats[:, 0, 0:1], cols[:, 0:1], ACT.Gelu_apprx_tanh)
            for j in range(2):
                act.wait_ge(TS["t_dT"], j + 1)
            for e in range(E):
                act.wait_ge(TS["t_h"], e + 1)
                if e >= 2:
                    act.wait_ge(TS["t_y"], e - 1)
                act.activation(hT[:, e % 2, :, :].rearrange("p f s -> p (f s)"), PS[:, e % 2, 0:FT * CAP],
                               ACT.Gelu_apprx_tanh).then_inc(TS["t_g"], 1)

        @block.tensor
        def _(pe):
            def mm(o, l, r, start=True, stop=True):
                return pe.matmul(o, l, r, start=start, stop=stop)

            pe.wait_ge(s_ones, 1)
            pe.wait_ge(s_w0, 16)

            def products_of_weights():
                pe.wait_ge(s_heads, 16)
                for n in range(NG + 2):
                    if n >= 4:
                        pe.wait_ge(s_ab_sb, n - 3)
                    bank = AB_BANKS[n]
                    if n < NG:
                        for c in range(G):
                            h = G * n + c
                            last = mm(PS[:, bank, c * P:(c + 1) * P].rearrange("p (a b) -> p a b", a=2), wqT_sb[:, h, :],
                                      wkT_sb[:, h, :].unsqueeze(1).broadcast_to([D1, 2, CC]))
                    else:
                        for c in range(2 * G):
                            h = 2 * G * (n - NG) + c
                            last = mm(PS[D1 * (h % 2):D1 * (h % 2) + D1, bank, (c // 2) * P:(c // 2 + 1) * P],
                                      wvT_sb[:, h, :], wo_sb[:, h, :])
                    last.then_inc(s_ab, 1)

            def project_ctx():
                pe.wait_ge(S["p_xn"], 1)
                for t in range(QT):
                    last = pe.transpose(PS[:, 2, t * P:(t + 1) * P], xn_next[:, t, :], ident[:, :])
                last.then_inc(S["p_xT_ps"], 1)
                pe.wait_ge(S["cT_in"], 32)
                mm(PS[:, 4, :], w0_sb[:, 4, :], cT[:, :]).then_inc(S["ctx_ps"], 1)
                for k in range(KT):
                    last = mm(PS[:, 5, k * P:(k + 1) * P], cT[:, k * P:(k + 1) * P], w0_sb[:, 5, :])
                last.then_inc(S["ctx_ps"], 1)

            def project_x():
                pe.wait_ge(S["p_xT_sb"], 1)
                for j in range(3):
                    mm(PS[:, 2 + j // 2, (j % 2) * T:(j % 2 + 1) * T], w0_sb[:, j, :], xnT_next[:, :]).then_inc(S["proj_ps"], 1)
                for t in range(QT):
                    last = mm(PS[:, 3, T + t * P:T + (t + 1) * P], xnT_next[:, t * P:(t + 1) * P], w0_sb[:, 3, :])
                last.then_inc(S["proj_ps"], 1)

            def ctx_evacuated():
                pe.wait_ge(S["split_hi"], 1)
                pe.wait_ge(S["split_lo"], 1)
                pe.wait_ge(S["v_sb"], 1)

            def x_evacuated():
                pe.wait_ge(S["split_hi"], 4)
                pe.wait_ge(S["split_lo"], 4)
                pe.wait_ge(S["v_sb"], 2)

            def mx_slot(n, count, base):
                if base + n - 1 > 0:
                    pe.wait_ge(S[count], base + n - 1)
                return MX + n % 2

            def max_self(g, c, name="mx", n0=0):
                n, h = 3 * c, G * g + c
                bank = mx_slot(n0 + n, name + "_ok", 0)
                for t in range(QT):
                    o = PS[:, bank, t * T:(t + 1) * T]
                    mm(o, QS[0:ROWS, h, t * P:(t + 1) * P], KS[0:ROWS, h, :], stop=False)
                    last = mm(o[:, t * P:(t + 1) * P], identb[:, :], causal[:, :], start=False)
                last.then_inc(S[name + "_ps"], 1)

            def max_cross(g, c, t, name="mx", n0=0):
                n, h = 3 * c + 1 + t, G * g + c
                bank = mx_slot(n0 + n, name + "_ok", 0)
                mm(PS[:, bank, :], QC[0:ROWS, h, t * P:(t + 1) * P], KC[0:ROWS, h, :]).then_inc(S[name + "_ps"], 1)

            def stacked():
                pe.wait_ge(S["q_in"], 48)
                pe.wait_ge(S["k_in"], 48)

            def max_next(c):
                max_self(0, c, "pmx")
                if c == 0:
                    pe.wait_ge(S["c_in"], 96)
                max_cross(0, c, 0, "pmx")
                max_cross(0, c, 1, "pmx")

            def turn_next():
                pe.wait_ge(S["pmx_ok"], 3 * G)
                for t in range(QT):
                    last = pe.transpose(PS[0:2 * G, MISC, t * P:(t + 1) * P], rmax[:, 0, t, 0:2 * G], ident[:, :])
                last.then_inc(S["pmt_ps"], 1)

            project_ctx()
            ctx_evacuated()
            project_x()
            products_of_weights()
            stacked()
            pe.wait_ge(s_pool_zero, 2)
            pe.wait_ge(s_ab_sb, NG + 2)
            for c in range(G):
                max_next(c)
            turn_next()
            end_of_batch(pe, "pe")
            def st_slot(n):
                if n >= 2:
                    full, part = divmod(n - 1, 6)
                    pe.wait_ge(S["self_ok"], 2 * full + (0, 1, 1, 1, 2, 2)[part])
                    if 4 * full + (0, 0, 1, 2, 2, 3)[part]:
                        pe.wait_ge(S["exp_ok"], 4 * full + (0, 0, 1, 2, 2, 3)[part])
                return STB + 2 * (n % 2)

            def st_self(g, j):
                n = 6 * g + 3 * j
                if g >= 1:
                    pe.wait_ge(S["mt_sb"], 2 * g - 1)
                bank = st_slot(n)
                for i in range(2):
                    h = G * g + 2 * j + i
                    mm(PS[:, bank + i, P:3 * P], KS[0:END0, h, P:2 * P], QS[0:END0, h, :])
                    last = mm(PS[:, bank + i, 0:T], KS[0:END0, h, 0:P], QS[0:END0, h, :])
                last.then_inc(S["st_ps"], 1)

            def st_cross(g, c):
                n, h = 6 * g + (1 + c if c < 2 else 2 + c), G * g + c
                if g >= 1:
                    pe.wait_ge(S["mt_sb"], 2 * g)
                bank = st_slot(n)
                for k in range(KT):
                    last = mm(PS[:, bank + k // 2, (k % 2) * T:(k % 2 + 1) * T], KC[0:END0, h, k * P:(k + 1) * P], QC[0:END0, h, :])
                last.then_inc(S["st_ps"], 1)

            def turn_max0(g):
                if g >= 2:
                    pe.wait_ge(S["mt_sb"], 2 * (g - 1))
                pe.wait_ge(S["mx_ok"], 12 * g)
                for t in range(QT):
                    last = pe.transpose(PS[0:2 * G, MISC, t * P:(t + 1) * P], rmax[:, g % 2, t, 0:2 * G], ident[:, :])
                last.then_inc(S["mt_ps"], 1)

            def av0(g, between):
                between = iter(between)
                if g >= 1:
                    pe.wait_ge(S["av_sb"], g)
                pe.wait_ge(S["masked"], 2 * (g + 1))
                for k in range(QT):
                    for c in range(G):
                        w = T - k * P
                        mm(PS[32 * c:32 * c + DV, AV, k * P:T], Vs[:, k, G * g + c, :],
                           Ps[:, c, 2 * k * P:2 * k * P + w], start=(k == 0), stop=(k == 1))
                next(between, int)()
                pe.wait_ge(S["exp_ok"], G * (g + 1))
                for k in range(KT):
                    for c in range(G):
                        last = mm(PS[32 * c:32 * c + DV, AV, T:2 * T], Vc[:, k, G * g + c, :],
                                  Pc[:, c, k * T:(k + 1) * T], start=(k == 0), stop=(k == KT - 1))
                    if k == KT - 1:
                        last.then_inc(S["av_ps"], 1)
                    elif k > 0:
                        next(between, int)()

            def turn_out(g):
                pe.wait_ge(S["av_sb"], g + 1)
                pe.wait_ge(S["mt_sb"], 2 * min(g + 1, NG - 1))
                for j in range(2 * QT):
                    last = pe.transpose(PS[:, MISC, j * P:(j + 1) * P], OT[:, j * P:(j + 1) * P], ident[:, :])
                last.then_inc(S["ot_ps"], 1)

            def attention0():
                def maxima(g, c, part):
                    if part == 0:
                        max_self(g, c, n0=12 * (g - 1))
                    else:
                        max_cross(g, c, part - 1, n0=12 * (g - 1))
                for g in range(NG):
                    units = [(c, part) for c in range(1 if g else 0, G) for part in range(3)] if g + 1 < NG else []
                    blocks = ((st_self, 0), (st_cross, 0), (st_cross, 1), (st_self, 1), (st_cross, 2), (st_cross, 3))
                    for j, (scores, c) in enumerate(blocks):
                        for unit in units[len(units) * j // 6:len(units) * (j + 1) // 6]:
                            maxima(g + 1, *unit)
                        scores(g, c)
                        if j == 0 and g >= 1:
                            turn_out(g - 1)
                    if units:
                        if g >= 1:
                            pe.wait_ge(S["ot_sb"], g)
                        turn_max0(g + 1)
                    av0(g, [lambda part=part: maxima(g + 2, 0, part) for part in range(3) if g + 2 < NG])

            def turn(src):
                for t in range(QT):
                    last = pe.transpose(PS[:, MX, t * P:(t + 1) * P], src[:, t, :], ident[:, :])
                last.then_inc(S["xT_ps"], 1)

            def out_turn():
                pe.wait_ge(S["y_ok"], NG)
                turn(y)

            def out_project():
                pe.wait_ge(S["xT_sb"], 1)
                for t in range(QT):
                    last = mm(PS[:, MX, t * P:(t + 1) * P], yT[:, t * P:(t + 1) * P], w0_sb[:, 6, :])
                last.then_inc(S["o_ps"], 1)

            def mlp_turn():
                pe.wait_ge(S["xn_ok"], 1)
                turn(xn)

            def mlp_up(bank):
                pe.wait_ge(S["xT_sb"], 2)
                for f in range(FT):
                    mm(PS[:, bank + f // 2, (f % 2) * T:(f % 2 + 1) * T], fc1[:, f * P:(f + 1) * P], xnT[:, :]
                       ).then_inc(S["f_ps"], 1)

            def mlp_down():
                pe.wait_ge(S["s_ok"], FT)
                for t in range(QT):
                    for f in range(FT):
                        last = mm(PS[:, MX, t * P:(t + 1) * P], th[:, f, t * P:(t + 1) * P], fc2[:, f, :],
                                  start=(f == 0), stop=(f == FT - 1))
                last.then_inc(S["z_ps"], 1)

            def heads_turn():
                pe.wait_ge(S["xn_ok"], 2)
                turn(xn)

            def max1(g, c, t, name="m1"):
                n = 2 * (G * (g - 1) + c) + t if g else 2 * c + t
                if n >= 2:
                    pe.wait_ge(S[name + "_ok"], n - 1)
                mm(PS[:, MX + t, :], QH[:, G * g + c, t * P:(t + 1) * P], K1[:, :]).then_inc(S[name + "_ps"], 1)

            def turn_max1(g, beside):
                pe.wait_ge(S["m1_ok"], 8 * g)
                if g == 1:
                    if beside:
                        pe.wait_ge(S["ot_sb"], NG)
                else:
                    pe.wait_ge(S["t1_sb"], G * (g - 1))
                    pe.wait_ge(S["sum_sb"], g - 1)
                for t in range(QT):
                    last = pe.transpose(PS[0:G, MISC, t * P:(t + 1) * P], rmax1[:, g % 2, t, :], ident[:, :])
                last.then_inc(S["t1_ps"], 1)

            def st1(g, c, beside):
                n = G * g + c
                bank = st1_bank(n, beside)
                if g >= 1:
                    pe.wait_ge(S["t1_sb"], n - G + 1)
                if beside and n == 7:
                    pe.wait_ge(S["h_ok"], FT)
                elif n >= 2:
                    pe.wait_ge(S["e1_ok"], n if beside and n == 6 else n - 1)
                for k in range(KT):
                    o = PS[:, bank + k // 2, (k % 2) * T:(k % 2 + 1) * T]
                    mm(o, K1[:, k * P:(k + 1) * P], QH[:, n, :], stop=False)
                    last = mm(o, K2[:, k * P:(k + 1) * P], QL[0:ROWS, n, :], start=False)
                last.then_inc(S["s1_ps"], 1)

            def av1(g, between):
                pe.wait_ge(S["e1_ok"], G * (g + 1))
                if g == 0:
                    pe.wait_ge(S["ctx_in"], 16)
                else:
                    pe.wait_ge(S["a1_sb"], g)
                for c in range(0, G, 2):
                    for k in range(KT):
                        for i in range(2):
                            mm(PS[D1 * i:D1 * i + D1, AV, (c // 2) * T:(c // 2 + 1) * T], ctx_sb[:, k, :],
                               Pc[:, c + i, k * T:(k + 1) * T], start=(k == 0), stop=(k == KT - 1))
                    if between:
                        between.pop(0)()
                if g >= 1:
                    pe.wait_ge(S["sum_sb"], g)
                pe.wait_ge(S["t1_sb"], G * min(g + 1, NG - 1))
                pe.wait_ge(S["pz_ok"], G * (g + 1))
                for c in range(G):
                    last = mm(PS[32 * c:32 * c + 32, MISC, T:2 * T], ones32[:, :], Pz[:, c, :])
                last.then_inc(S["a1_ps"], 1)

            def turn_tokens(part):
                t0, t1, banks, _, _ = ROUTES[part]
                pe.wait_ge(TS["t_xm"], part + 1)
                for t in range(t0, t1):
                    j = t - t0
                    last = pe.transpose(PS[:, banks[j // 4], (j % 4) * P:(j % 4 + 1) * P], xm[:, t, :], ident[:, :])
                last.then_inc(TS["t_xT"], 1)

            def logits(part):
                t0, t1, _, bank, _ = ROUTES[part]
                pe.wait_ge(TS["t_xTsb"], part + 1)
                for t in range(t0, t1):
                    last = mm(PS[:, bank, t * E:(t + 1) * E], xmT[:, t * P:(t + 1) * P], gwT)
                last.then_inc(TS["t_lg"], 1)

            def ranks(part):
                t0, t1, _, _, bank = ROUTES[part]
                pe.wait_ge(TS["t_oh"], part + 1)
                rank = PS[:, bank, 0:TILES * E].rearrange("p (t e) -> p t e", e=E)
                mm(rank[:, t0:t1, :], tri[:, :], oh[:, t0:t1, :], stop=False)
                for t in range(t1 - 1):
                    first = max(t + 1, t0)
                    last = mm(rank[:, first:t1, :], onesb[:, :],
                              oh[:, t, :].unsqueeze(1).broadcast_to([P, t1 - first, E]), start=False, stop=(t == t1 - 2))
                last.then_inc(TS["t_rk"], 1)

            def attention1(beside):
                bank0 = []
                made = [0]

                def maxima(g, c):
                    for s, n in bank0:
                        pe.wait_ge(S[s], n)
                    bank0.clear()
                    for t in range(QT):
                        max1(g, c, t)
                        made[0] += 1

                def take_bank0(step, s, n):
                    pe.wait_ge(S["m1_ok"], made[0] - 1)
                    step()
                    bank0.append((s, n))

                for g in range(NG):
                    for c in range(G):
                        for h in MAX1_BESIDE.get((g, c), ()):
                            maxima(g + 1, h)
                        if beside and (g, c) == (1, 0):
                            pe.wait_ge(S["p_xT_sb"], 1)
                        elif beside and (g, c) == (1, 1):
                            ctx_evacuated()
                        elif beside and (g, c) == (2, 1):
                            x_evacuated()
                        st1(g, c, beside)
                        if beside:
                            if (g, c) == (0, 0):
                                turn_out(NG - 1)
                            elif (g, c) == (0, 1):
                                take_bank0(out_turn, "xT_sb", 1)
                            elif (g, c) == (0, 2):
                                take_bank0(out_project, "o_sb", 1)
                            elif (g, c) == (1, 0):
                                take_bank0(mlp_turn, "xT_sb", 2)
                            elif (g, c) == (1, 1):
                                pe.wait_ge(S["e1_ok"], 5)
                                mlp_up(MLP_BANK)
                            elif (g, c) == (1, 3):
                                take_bank0(mlp_down, "z_sb", 1)
                            elif (g, c) == (2, 2):
                                take_bank0(heads_turn, "xT_sb", 3)
                            elif g == NG - 1:
                                if c == 0:
                                    stacked()
                                max_next(c)
                        elif g == NG - 1 and c != 2:
                            (turn_tokens, logits, None, ranks)[c](0)
                    if g + 1 < NG:
                        turn_max1(g + 1, beside)
                    av1(g, [lambda h=h: maxima(g + 2, h) for h in range(2) if g + 2 < NG])
                    if beside and g == 0:
                        project_ctx()
                    elif beside and g == 1:
                        project_x()

            def divide_last():
                pe.wait_ge(S["sum_sb"], NG)
                for i in range(2):
                    last = mm(PS[:, 5, i * T:(i + 1) * T], pick_sum[:, i, :], rsum[:, :])
                last.then_inc(S["r_ps"], 1)

            def project_out1():
                for j in range(H // 2):
                    if j == H // 2 - 2:
                        pe.wait_ge(S["un_last"], 1)
                    elif j % 2 == 0:
                        pe.wait_ge(S["un_ok"], j // 2 + 1)
                    last = mm(PS[:, 4, 0:T], Ball[:, j, :], U[:, j, :], start=(j == 0), stop=(j == H // 2 - 1))
                last.then_inc(S["o1_ps"], 1)

            def turn_out1():
                pe.wait_ge(S["o1_sb"], 1)
                for t in range(QT):
                    last = pe.transpose(PS[:, 5, t * P:(t + 1) * P], oT[:, t * P:(t + 1) * P], ident[:, :])
                last.then_inc(S["o1T_ps"], 1)

            def project_heads(n):
                if n >= 3:
                    pe.wait_ge(S["qh_ok"], n - 2)
                    pe.wait_ge(S["ql_ok"], n - 2)
                for i in range(2):
                    last = mm(PS[:, PAIR_BANKS[n % 3], i * T:(i + 1) * T], Aall[:, 2 * n + i, :], xnT[:, :])
                last.then_inc(S["q1_ps"], 1)

            def max1_next(c):
                if c == 0:
                    pe.wait_ge(S["kk_hi"], 2)
                    pe.wait_ge(S["kk_lo"], 1)
                if c % 2 == 0:
                    pe.wait_ge(S["qh_ok"], c // 2 + 1)
                for t in range(QT):
                    max1(0, c, t, "pm1")

            def next_heads(beside):
                project_heads(0)
                project_heads(1)
                if beside:
                    divide_last()
                turn_next()
                pe.wait_ge(S["a1_sb" if beside else "av_sb"], NG)
                project_heads(2)
                max1_next(0)
                if beside:
                    project_out1()
                project_heads(3)
                max1_next(1)
                if beside:
                    turn_out1()
                project_heads(4)
                max1_next(2)
                project_heads(5)
                max1_next(3)
                project_heads(6)
                project_heads(7)
                pe.wait_ge(S["pm1_ok"], 2 * G)
                pe.wait_ge(S["pmt_sb"], 2)
                for t in range(QT):
                    last = pe.transpose(PS[0:G, MISC, t * P:(t + 1) * P], rmax1[:, 0, t, :], ident[:, :])
                last.then_inc(S["pt1_ps"], 1)
                pe.wait_ge(S["ql_ok"], H // 2)

            attention0()
            turn_out(NG - 1)
            project_ctx()
            out_turn()
            out_project()
            pe.wait_ge(S["p_xT_sb"], 1)
            project_x()
            mlp_turn()
            ctx_evacuated()
            mlp_up(4)
            mlp_down()
            heads_turn()
            x_evacuated()
            stacked()
            pe.wait_ge(S["xT_sb"], 3)
            for c in range(G):
                max_next(c)
            next_heads(False)
            end_of_batch(pe, "pe")
            with pe.Fori(0, B - 1) as b:
                attention0()
                attention1(True)
                next_heads(True)
                end_of_batch(pe, "pe")
            attention1(False)
            divide_last()
            project_out1()
            turn_out1()

            turn_tokens(1)
            logits(1)
            ranks(1)
            keep_warm(pe, KEEP_WARM_TAIL)
            pe.wait_ge(TS["t_xd"], 16)
            for t in range(ST):
                last = pe.transpose(PS[:, 4 + t // 4, (t % 4) * P:(t % 4 + 1) * P], XD[:, t, :], ident[:, :])
                if t % 4 == 3 or t == ST - 1:
                    last.then_inc(TS["t_dT"], 1)
            pe.wait_ge(TS["t_dTsb"], 3)

            def up(e):
                if e >= 2:
                    pe.wait_ge(TS["t_g"], e - 1)
                for f in range(FT):
                    last = mm(PS[:, e % 2, f * CAP:(f + 1) * CAP], w1_all[:, e, f * P:(f + 1) * P],
                              XT[:, e * CAP:(e + 1) * CAP])
                last.then_inc(TS["t_h"], 1)

            def down(e):
                pe.wait_ge(TS["t_g"], e + 1)
                q = e // 4
                if q >= 2 and e % 4 == 0:
                    pe.wait_ge(TS["t_ysb"], q - 1)
                for f in range(FT):
                    last = mm(PS[0:CAP, 2 + q % 2, (e % 4) * C:(e % 4 + 1) * C], hT[:, e % 2, f, :], w2_all[:, e, f, :],
                              start=(f == 0), stop=(f == FT - 1))
                last.then_inc(TS["t_y"], 1)
            pe.wait_ge(s_w1, 16 * E)
            pe.wait_ge(TS["t_w2"], 16 * E)
            up(0)
            for e in range(E):
                if e + 1 < E:
                    up(e + 1)
                down(e)

        @block.vector
        def _(dve):
            dve.memset(zrow, 0.0).then_inc(s_zrow, 1)
            setup = Chain(dve, s_setup)
            dve.memset(KC[:, 0:H // 2, :].bitcast(F32), 0.0)
            link = Chain(dve, S["dchain"])

            def center(src, link, at=0):
                for t in range(QT):
                    i = dve.bn_stats(stats[:, at + t, :], src(t))
                link(i)
                for t in range(QT):
                    i = dve.bn_aggr(mv[:, at + t, :], stats[:, at + t, :])
                link(i)
                return dve.tensor_scalar(ve[:, at:at + QT], mv[:, at:at + QT, 1], EPS, None, ALU.add)

            def scaled(src, dst, at=0):
                for t in range(QT):
                    i = dve.tensor_scalar(dst[:, t, :], src(t), mv[:, at + t, 0:1], rstd[:, at + t:at + t + 1],
                                          ALU.subtract, ALU.mult)
                return i

            def center_next(src, link):
                center(src, link, QT).then_inc(S["p_var"], 1)

            def norm_next(src):
                dve.wait_ge(S["p_rstd"], 1)
                scaled(src, xn_next, QT).then_inc(S["p_xn"], 1)

            def low(n):
                bank, at, off, w, bias = SPLIT[n]
                if n == 1:
                    dve.wait_ge(S["cparts_out"], 32)
                dve.wait_ge(S["split_hi"], (1, 3, 3, 4)[n])
                dve.scalar_tensor_tensor(out=lo[:, off:off + w], in0=PS[:, bank, at:at + w], scalar=b0_sb[:, bias:bias + 1],
                                         in1=hi[:, off:off + w], op0=ALU.add, op1=ALU.subtract).then_inc(S["split_lo"], 1)

            def tokens_next():
                dve.wait_ge(S["p_xT_ps"], 1)
                dve.tensor_copy(xnT_next[:, :], PS[:, 2, 0:T]).then_inc(S["p_xT_sb"], 1)

            def context_next():
                dve.wait_ge(S["ctx_ps"], 2)
                dve.tensor_copy(Vc[:, :, :, 0:D0], PS[:, 5, :].rearrange("p (k h d) -> p k h d", k=KT, h=H)
                                ).then_inc(S["v_sb"], 1)
                low(0)

            def x_next():
                for n in (1, 2, 3):
                    low(n)
                dve.wait_ge(S["proj_ps"], 4)
                dve.tensor_copy(Vs[:, :, :, 0:D0], PS[:, 3, T:2 * T].rearrange("p (k h d) -> p k h d", k=QT, h=H)
                                ).then_inc(S["v_sb"], 1)

            def take_max(n, g, reduces, name="mx"):
                dve.wait_ge(S[name + "_ps"], n + 1)
                for (a, e), t, col in reduces:
                    i = dve.tensor_reduce(rmax[:, g % 2, t, col:col + 1], PS[:, MX + n % 2, a:e], X, ALU.max)
                i.then_inc(S[name + "_ok"], 1)

            def maxima0(g, c, name, n0):
                n = n0 + 3 * c
                take_max(n, g, [((0, P), 0, c), ((T, 2 * T), 1, c)], name)
                for t in range(QT):
                    take_max(n + 1 + t, g, [((0, TC), t, G + c)], name)

            def first(t):
                return x_all[:, t, :]
            dve.wait_ge(s_x, 16)
            center_next(first, link)
            dve.memset(KC[:, H // 2:H, :].bitcast(F32), 0.0)
            dve.drain().then_inc(s_dve_zero, 1)
            norm_next(first)
            dve.wait_ge(s_cols, 16)
            tokens_next()
            context_next()
            dve.memset(QS[:, :, :].bitcast(F32), 0.0).then_inc(s_dve_zero, 1)
            setup(dve.memset(K2[:, :].bitcast(F32), 0.0))
            dve.memset(K2[ONE1:ONE1 + G, :].bitcast(F32), 1.0)
            dve.memset(PS[:, AV, :], 0.0)
            dve.memset(Vs[:, :, :, D0:DV], 1.0)
            dve.memset(Vc[:, :, :, D0:DV], 1.0)
            x_next()
            dve.memset(onesb[:, :], 1.0)
            dve.memset(ones32[:, :], 1.0)
            dve.wait_ge(s_fcq, 32)
            dve.scalar_tensor_tensor(out=fc1[:, :], in0=fcq[:, 0, :], scalar=-128.0, in1=fcs[:, 0, :], op0=ALU.add, op1=ALU.mult)
            dve.scalar_tensor_tensor(out=fc2[:, :, :].rearrange("p f c -> p (f c)"), in0=fcq[:, 1, :], scalar=-128.0,
                                     in1=fcs[:, 1, :], op0=ALU.add, op1=ALU.mult)
            dve.tensor_scalar(fc1bh[:, :], fc1b, 0.5, None, ALU.mult)
            dve.wait_ge(s_tanh, 1)
            dve.tensor_scalar(fc2bh, fc2bh, 0.5, None, ALU.mult)
            dve.tensor_tensor(bvsum[:, :], bv_sb[:, 0:1], bv_sb[:, 1:2], ALU.add)
            for c in range(G):
                maxima0(0, c, "pmx", 0)
            end_of_batch(dve, "dve")

            def attention0(tile, link):
                def max0(g):
                    for c in range(1 if g >= 2 else 0, G):
                        maxima0(g, c, "mx", 12 * (g - 1))
                        if c == 1 and g >= 2:
                            out0(g - 2, link)

                def evac0(g):
                    dve.wait_ge(S["av_ps"], g + 1)
                    if g >= 1:
                        dve.wait_ge(S["ot_ps"], g)
                    dve.tensor_copy(OT[:, :], PS[:, AV, :]).then_inc(S["av_sb"], 1)
                for g in range(NG):
                    if g + 1 < NG:
                        max0(g + 1)
                    else:
                        out0(g - 1, link)
                    if g == 2:
                        center_next(tile, link)
                    elif g == 3:
                        norm_next(tile)
                    if g + 2 < NG:
                        if g == 1:
                            dve.wait_ge(S["mt_ps"], 1)
                        maxima0(g + 2, 0, "mx", 12 * (g + 1))
                    evac0(g)

            def out0(g, link):
                dve.wait_ge(S["ot_ps"], g + 1)
                o = PS[:, MISC, :].rearrange("p (j c d) -> p j c d", j=2 * QT, c=G)
                link(dve.reciprocal(rc0[:, :, :], o[:, :, :, D0]))
                i = dve.tensor_tensor(yn[:, :, :, :], o[:, :, :, 0:D0],
                                      rc0[:, :, :].unsqueeze(3).broadcast_to([P, 2 * QT, G, D0]), ALU.mult)
                i.then_inc(S["ot_sb"], 1)
                dve.wait_ge(S["ot_sb"], g + 1)
                dve.tensor_tensor(y[:, :, :].rearrange("p t (h d) -> p t h d", h=H)[:, :, G * g:G * g + G, :],
                                  yn[:, 0:QT, :, :], yn[:, QT:2 * QT, :, :], ALU.add).then_inc(S["y_ok"], 1)

            def x1_tile(t):
                return x1[:, t, :]

            def xn1_tile(t):
                return xn1[:, t, :]

            def out_turned():
                dve.wait_ge(S["xT_ps"], 1)
                dve.tensor_scalar(yT[:, :], PS[:, MX, 0:T], bvsum[:, :], None, ALU.add).then_inc(S["xT_sb"], 1)

            def after_attention(x_tiles, link):
                dve.wait_ge(S["o_ps"], 1)
                o = PS[:, MX, 0:T].rearrange("p (t c) -> p t c", t=QT)
                dve.tensor_tensor(tmp[:, :, :], o, bp_sb.unsqueeze(1).broadcast_to([P, QT, C]), ALU.add).then_inc(S["o_sb"], 1)
                dve.wait_ge(S["o_sb"], 1)
                link(dve.scalar_tensor_tensor(out=x1[:, :, :], in0=tmp[:, :, :], scalar=tg[:, 0:1], in1=x_tiles,
                                              op0=ALU.mult, op1=ALU.add))
                center(x1_tile, link).then_inc(S["var"], 1)

            def second_norm(link):
                dve.wait_ge(S["rstd_ok"], 1)
                link(scaled(x1_tile, xn1))
                center(xn1_tile, link).then_inc(S["var"], 1)

            def mlp_in():
                dve.wait_ge(S["rstd_ok"], 2)
                scaled(xn1_tile, xn).then_inc(S["xn_ok"], 1)

            def mlp_turned():
                dve.wait_ge(S["xT_ps"], 2)
                dve.tensor_scalar(xnT[:, :], PS[:, MX, 0:T], gb_sb[:, 0:1], gb_sb[:, 1:2], ALU.mult, ALU.add
                                  ).then_inc(S["xT_sb"], 1)

            def mlp():
                for f in range(FT):
                    dve.wait_ge(S["h_ok"], f + 1)
                    dve.scalar_tensor_tensor(out=th[:, f, :], in0=th[:, f, :], scalar=1.0, in1=fh[:, f, :],
                                             op0=ALU.add, op1=ALU.mult).then_inc(S["s_ok"], 1)

            def after_mlp(x_tiles, link):
                dve.wait_ge(S["z_ps"], 1)
                z = PS[:, MX, 0:T].rearrange("p (t c) -> p t c", t=QT)
                dve.scalar_tensor_tensor(out=tmp[:, :, :], in0=z, scalar=0.25, in1=xn1[:, :, :], op0=ALU.mult, op1=ALU.add
                                         ).then_inc(S["z_sb"], 1)
                dve.wait_ge(S["z_sb"], 1)
                link(dve.tensor_tensor(tmp[:, :, :], tmp[:, :, :], fc2bh.unsqueeze(1).broadcast_to([P, QT, C]), ALU.add))
                link(dve.scalar_tensor_tensor(out=x1[:, :, :], in0=tmp[:, :, :], scalar=tg[:, 2:3], in1=x1[:, :, :],
                                              op0=ALU.mult, op1=ALU.add))
                center(x1_tile, link).then_inc(S["var"], 1)
                dve.tensor_copy(x_tiles, x1[:, :, :])

            def heads_in():
                dve.wait_ge(S["rstd_ok"], 3)
                scaled(x1_tile, xn).then_inc(S["xn_ok"], 1)

            def heads_turned():
                dve.wait_ge(S["xT_ps"], 3)
                dve.tensor_copy(xnT[:, :], PS[:, MX, 0:T]).then_inc(S["xT_sb"], 1)

            def maxima1(g, c, name="m1"):
                for t in range(QT):
                    n = 2 * (G * (g - 1) + c) + t if g else 2 * c + t
                    dve.wait_ge(S[name + "_ps"], n + 1)
                    dve.tensor_reduce(rmax1[:, g % 2, t, c:c + 1], PS[:, MX + t, :], X, ALU.max).then_inc(S[name + "_ok"], 1)

            def evac1(g, first=()):
                dve.wait_ge(S["a1_ps"], g + 1)
                dve.tensor_copy(U[:, 2 * g:2 * g + 2, :].rearrange("p a b -> p (a b)"), PS[:, AV, :]
                                ).then_inc(S["a1_sb"], 1)
                for step in first:
                    step()
                if g >= 1:
                    dve.wait_ge(S["rinv_out"], 16 * g)
                dve.reciprocal(rsum[:, :], PS[:, MISC, T:2 * T]).then_inc(S["sum_sb"], 1)

            route_link = Chain(dve, TS["t_chain"])

            def route_center(part):
                t0, t1 = ROUTES[part][0:2]
                for t in range(t0, t1):
                    i = dve.bn_stats(stats[:, t, :], x_all[:, t, :])
                route_link(i)
                for t in range(t0, t1):
                    i = dve.bn_aggr(mv[:, t, :], stats[:, t, :])
                route_link(i)
                dve.tensor_scalar(ve[:, t0:t1], mv[:, t0:t1, 1], EPS, None, ALU.add).then_inc(TS["t_var"], 1)

            def route_norm(part):
                t0, t1 = ROUTES[part][0:2]
                dve.wait_ge(TS["t_rstd"], part + 1)
                for t in range(t0, t1):
                    i = dve.tensor_scalar(xm[:, t, :], x_all[:, t, :], mv[:, t, 0:1], rstd[:, t:t + 1],
                                          ALU.subtract, ALU.mult)
                i.then_inc(TS["t_xm"], 1)

            def route_turned(part):
                t0, t1, banks, _, _ = ROUTES[part]
                dve.wait_ge(TS["t_xT"], part + 1)
                for j, bank in enumerate(banks):
                    w = min(4, t1 - t0 - 4 * j) * P
                    at = (t0 + 4 * j) * P
                    i = dve.tensor_copy(xmT[:, at:at + w], PS[:, bank, 0:w])
                i.then_inc(TS["t_xTsb"], 1)

            def route_choose(part):
                t0, t1, _, bank, _ = ROUTES[part]
                n = t1 - t0
                dve.wait_ge(TS["t_lg"], part + 1)
                lg = PS[:, bank, t0 * E:t1 * E].rearrange("p (t e) -> p t e", e=E)
                iota3 = iota_e[:, :].unsqueeze(1).broadcast_to([P, n, E])
                route_link(dve.tensor_reduce(lmax[:, t0:t1], lg, X, ALU.max))
                dve.tensor_tensor(eq[:, t0:t1, :], lg, lmax[:, t0:t1].unsqueeze(2).broadcast_to([P, n, E]), ALU.subtract
                                  ).then_inc(TS["t_lm"], 1)
                dve.wait_ge(TS["t_lm"], part + 1)
                route_link(dve.tensor_scalar(pick[:, t0:t1, :], eq[:, t0:t1, :], 0.0, None, ALU.is_ge))
                route_link(dve.tensor_tensor(pick[:, t0:t1, :], pick[:, t0:t1, :], iota3, ALU.mult))
                route_link(dve.tensor_reduce(arg[:, t0:t1], pick[:, t0:t1, :], X, ALU.min))
                dve.tensor_tensor(oh[:, t0:t1, :], arg[:, t0:t1].unsqueeze(2).broadcast_to([P, n, E]), iota3, ALU.is_equal
                                  ).then_inc(TS["t_oh"], 1)

            def route_slots(part):
                t0, t1, _, _, bank = ROUTES[part]
                a = slice(t0, t1)
                dve.wait_ge(TS["t_ex"], part + 1)
                route_link(dve.reduce_sum(exs[:, a], ex[:, a, :], X))
                route_link(dve.reciprocal(wgt[:, a], exs[:, a]))
                dve.tensor_scalar(wgt[:, a], wgt[:, a], tg[:, 3:4], None, ALU.mult)
                dve.wait_ge(TS["t_oh"], part + 1)
                dve.wait_ge(TS["t_rk"], part + 1)
                rank = PS[:, bank, t0 * E:t1 * E].rearrange("p (t e) -> p t e", e=E)
                route_link(dve.tensor_tensor(rko[:, a, :], rank, oh[:, a, :], ALU.mult))
                route_link(dve.reduce_sum(rk[:, a], rko[:, a, :], X))
                dve.tensor_scalar(drop[:, a], rk[:, a], float(CAP), FAR, ALU.is_gt, ALU.mult)
                route_link(dve.scalar_tensor_tensor(out=slot[:, a], in0=arg[:, a], scalar=float(CAP), in1=rk[:, a],
                                                    op0=ALU.mult, op1=ALU.add))
                route_link(dve.tensor_scalar(slot[:, a], slot[:, a], float(E * CAP - 1), None, ALU.add))
                dve.tensor_tensor(slot_i[:, a], slot[:, a], drop[:, a], ALU.add).then_inc(TS["t_slot"], 1)

            def attention1(beside, x_tiles, link):
                for g in range(NG):
                    for c in range(G):
                        for h in MAX1_BESIDE.get((g, c), ()):
                            maxima1(g + 1, h)
                        if beside and g == NG - 1:
                            maxima0(0, c, "pmx", 0)
                        if not beside:
                            step = {(0, 1): route_center, (1, 1): route_norm, (3, 0): route_turned, (3, 1): route_choose,
                                    (3, 3): route_slots}.get((g, c))
                            if step:
                                step(0)
                        if beside:
                            if (g, c) == (0, 0):
                                out0(NG - 1, link)
                            elif (g, c) == (0, 1):
                                out_turned()
                            elif (g, c) == (0, 2):
                                after_attention(x_tiles, link)
                            elif (g, c) == (0, 3):
                                second_norm(link)
                            elif (g, c) == (1, 2):
                                mlp()
                            elif (g, c) == (1, 3):
                                after_mlp(x_tiles, link)
                            elif (g, c) == (2, 2):
                                heads_turned()
                    if g + 2 < NG:
                        if g == 1:
                            dve.wait_ge(S["t1_ps"], 1)
                        for h in range(2):
                            maxima1(g + 2, h)
                    if beside and g == 0:
                        evac1(g, (mlp_in, tokens_next, context_next, mlp_turned))
                    elif beside and g == 1:
                        evac1(g, (x_next,))
                        heads_in()
                    else:
                        evac1(g)

            def low_heads(n):
                dve.wait_ge(S["qh_ok"], n + 1)
                dve.tensor_tensor(QL[0:CC, 2 * n:2 * n + 2, :],
                                  PS[0:CC, PAIR_BANKS[n % 3], :].rearrange("p (a b) -> p a b", a=2),
                                  QH[0:CC, 2 * n:2 * n + 2, :], ALU.subtract).then_inc(S["ql_ok"], 1)

            def divide_last():
                dve.wait_ge(S["r_ps"], 1)
                u = U[:, H // 2 - 2:H // 2, :].rearrange("p a b -> p (a b)")
                dve.tensor_tensor(u, u, PS[:, 5, :], ALU.mult).then_inc(S["un_last"], 1)

            def projected_out1():
                dve.wait_ge(S["o1_ps"], 1)
                dve.tensor_scalar(oT[:, :], PS[:, 4, 0:T], bo_sb, tg[:, 1:2], ALU.add, ALU.mult).then_inc(S["o1_sb"], 1)

            def after_attention1(x_tiles):
                dve.wait_ge(S["o1T_ps"], 1)
                return dve.tensor_tensor(x_tiles, PS[:, 5, 0:T].rearrange("p (t c) -> p t c", t=QT), x_tiles, ALU.add)

            def next_heads(beside, x_tiles):
                dve.wait_ge(S["kk_hi"], 2)
                dve.tensor_tensor(K1[CC:P, :], cT[CC:P, :], K1[CC:P, :], ALU.subtract).then_inc(S["kk_lo"], 1)
                low_heads(0)
                low_heads(1)
                if beside:
                    divide_last()
                    dve.wait_ge(S["t1_ps"], 2)
                low_heads(2)
                maxima1(0, 0, "pm1")
                if beside:
                    projected_out1()
                low_heads(3)
                maxima1(0, 1, "pm1")
                if beside:
                    after_attention1(x_tiles)
                low_heads(4)
                maxima1(0, 2, "pm1")
                low_heads(5)
                maxima1(0, 3, "pm1")
                low_heads(6)
                low_heads(7)

            link = Chain(dve, S["dchain"])
            mine = x_all[:, 0:QT, :]
            attention0(lambda t: x_all[:, QT + t, :], link)
            out0(NG - 1, link)
            tokens_next()
            context_next()
            out_turned()
            after_attention(mine, link)
            x_next()
            second_norm(link)
            mlp_in()
            mlp_turned()
            mlp()
            after_mlp(mine, link)
            heads_in()
            heads_turned()
            for c in range(G):
                maxima0(0, c, "pmx", 0)
            next_heads(False, mine)
            end_of_batch(dve, "dve")
            with dve.Fori(0, B - 1) as b:
                link = Chain(dve, S["dchain"])
                before = x_all[:, bass.ds(b * QT, QT), :]
                mine = x_all[:, bass.ds(b * QT + QT, QT), :]
                attention0(lambda t: x_all[:, bass.ds((b * QT + 2 * QT) % TILES + t, 1), :].rearrange("p o c -> p (o c)"), link)
                attention1(True, mine, link)
                next_heads(True, before)
                end_of_batch(dve, "dve")
            attention1(False, None, None)
            divide_last()
            projected_out1()
            route_link(after_attention1(x_all[:, TILES - QT:TILES, :]))

            route_center(1)
            route_norm(1)
            route_turned(1)
            route_choose(1)
            route_slots(1)
            for j in range(3):
                w = min(512, SLOTS - 512 * j)
                dve.wait_ge(TS["t_dT"], j + 1)
                dve.tensor_copy(XT[:, 512 * j:512 * j + w], PS[:, 4 + j, 0:w]).then_inc(TS["t_dTsb"], 1)
            for q in range(E // 4):
                dve.wait_ge(TS["t_y"], 4 * q + 4)
                dve.tensor_copy(YB[:, 4 * q:4 * q + 4, :].rearrange("p e c -> p (e c)"), PS[0:CAP, 2 + q % 2, :]
                                ).then_inc(TS["t_ysb"], 1)
            dve.wait_ge(TS["t_sc"], 16 * TILES)
            for t in range(TILES):
                dve.wait_ge(s_back[t], 16)
                dve.scalar_tensor_tensor(out=xm[:, t, :], in0=Yg[:, t, :], scalar=wgt[:, t:t + 1], in1=x_all[:, t, :],
                                         op0=ALU.mult, op1=ALU.add).then_inc(TS["t_out"], 1)


_OUT = (B, T, C)


def kernel(**inputs):
    import numpy as np
    import concourse.bacc as bacc
    from concourse.bass_utils import run_bass_kernel_spmd

    a = {k: np.asarray(v) for k, v in inputs.items()}
    pre = "L0_xattn_"
    f32 = np.float32

    def heads(w):
        return w.reshape(w.shape[0], H, D1).transpose(2, 1, 0)

    w0 = np.zeros((P, 7, C), f32)
    for j, n in enumerate(("Wq", "Wk", "Wcq", "Wv", "Wck", "Wcv", "Wp")):
        w = a[pre + n]
        w0[:w.shape[0], j] = w
    columns = [a[pre + n] for n in ("bq", "bk", "bcq", "bck", "bv", "bcv")]
    columns += [a["L0_ffn_ln_gamma"], a["L0_ffn_ln_beta"], a["L1_xattn_bo"]]
    columns += [*a["L0_ffn_fc1_bias"].reshape(FT, P), *a["L1_ffn_gate_w"]]
    rows = [a[pre + "bp"], a["L0_ffn_fc2_bias"], a["g_xattn"], a["g_ffn"],
            a["L0_ffn_fc1_scales"].reshape(-1), a["L0_ffn_fc2_scales"].reshape(-1)]
    arrays = {
        "x": a["x"], "ctx": a["ctx_512"], "ctxT": np.ascontiguousarray(a["ctx_512"].transpose(0, 2, 1)),
        "w0": w0, "columns": np.stack(columns, axis=1), "rows": np.concatenate(rows),
        "fc_q": np.stack([a["L0_ffn_fc1_q"], a["L0_ffn_fc2_q"].reshape(FT, P, C).transpose(1, 0, 2).reshape(P, FF)], axis=1),
        "heads_w": np.concatenate([heads(a["L1_xattn_Wq"]), a["L1_xattn_Wo"].reshape(H, D1, C).transpose(1, 0, 2),
                                   heads(a["L1_xattn_Wk"]), heads(a["L1_xattn_Wv"])], axis=2),
        "w1": a["L1_ffn_w1"], "w2": a["L1_ffn_w2"],
    }
    nc = bacc.Bacc("TRN2", target_bir_lowering=False, num_devices=1)
    t = {}
    for name, v in arrays.items():
        t[name] = nc.dram_tensor(f"in_{name}", v.shape, mybir.dt.from_np(v.dtype), kind="ExternalInput").ap()
    out = nc.dram_tensor("out_x", _OUT, F32, kind="ExternalOutput").ap()
    build(nc, *(t[n] for n in arrays), out)
    r = run_bass_kernel_spmd(nc, [{f"in_{k}": v for k, v in arrays.items()}], core_ids=[0])
    return r.results[0]["out_x"]
```
